# Optimizing a Trainium2 kernel written in Bass

```python
import numpy as np
import jax
import jax.numpy as jnp

def _softmax(x, axis=-1):
    return jax.nn.softmax(x, axis=axis)

def _gelu(x):
    return jax.nn.gelu(x, approximate=True)

def _silu(x):
    return jax.nn.silu(x)

def _sigmoid(x):
    return jax.nn.sigmoid(x)

def _layernorm(x, axis=-1, eps=1e-05):
    m = jnp.mean(x, axis=axis, keepdims=True)
    v = jnp.var(x, axis=axis, keepdims=True)
    return (x - m) / jnp.sqrt(v + eps)

def _scatter_add(tgt, idx, src, axis=0):
    return tgt.at[idx].add(src)

def _segment_sum(src, seg, n):
    return jax.ops.segment_sum(src, seg, n)
kernel_name = 'mk_gnn_resnorm_d4_gnn_r32_a9775a'

def setup_inputs(seed: int=0):
    np.random.seed(seed)
    _w = jnp.asarray

    def _rec_inputs():
        import jax
        import jax.numpy as jnp
        _gk = jax.random.key(seed)
        x = -0.000202 + 1 * jax.random.normal(jax.random.fold_in(_gk, 1), (3125, 64), jnp.float32)
        src = jax.random.randint(jax.random.fold_in(_gk, 2), (100000,), 0, 3125, jnp.int32)
        dst = jax.random.randint(jax.random.fold_in(_gk, 3), (100000,), 0, 3125, jnp.int32)
        _o = jnp.argsort(dst, stable=True)
        src = src[_o]
        dst = dst[_o]
        edge_attr_32 = 0.000189758 + 1.00013 * jax.random.normal(jax.random.fold_in(_gk, 13), (100000, 32), jnp.float32)
        return (x, src, dst, edge_attr_32)
    x, src, dst, edge_attr_32 = _rec_inputs()

    def _L0_gnn_setup():
        import jax, jax.numpy as jnp
        import numpy as np
        N_NODES = 3125
        N_EDGES = 50000
        N_GRAPHS = 64
        NODE_IN = 64
        EDGE_IN = 32
        GLOBAL_IN = 32
        NODE_OUT = 64
        MSG = 32

        def _linear_params(key, fan_in, fan_out):
            kw, kb = jax.random.split(key)
            s = 1.0 / np.sqrt(fan_in)
            W = jax.random.uniform(kw, (fan_in, fan_out), jnp.float32, -s, s)
            b = jax.random.uniform(kb, (fan_out,), jnp.float32, -s, s)
            return (W, b)
        key = jax.random.key(seed)
        ks = jax.random.split(key, 12)
        x = jax.random.normal(ks[0], (N_NODES, NODE_IN), jnp.float32)
        edge_index = jax.random.randint(ks[1], (2, N_EDGES), 0, N_NODES, jnp.int64 if jax.config.jax_enable_x64 else jnp.int32)
        edge_attr = jax.random.normal(ks[2], (N_EDGES, EDGE_IN), jnp.float32)
        u = jax.random.normal(ks[3], (N_GRAPHS, GLOBAL_IN), jnp.float32)
        batch = jnp.sort(jax.random.randint(ks[4], (N_NODES,), 0, N_GRAPHS))
        W1, b1 = _linear_params(ks[5], 2 * NODE_IN + EDGE_IN, MSG)
        W2, b2 = _linear_params(ks[6], MSG, MSG)
        W3, b3 = _linear_params(ks[7], MSG, MSG)
        W4, b4 = _linear_params(ks[8], 2 * MSG + NODE_IN + GLOBAL_IN, MSG)
        W5, b5 = _linear_params(ks[9], MSG, MSG)
        W6, b6 = _linear_params(ks[10], MSG, NODE_OUT)
        return {'x': x, 'edge_index': edge_index, 'edge_attr': edge_attr, 'u': u, 'batch': batch, 'W1': W1, 'b1': b1, 'W2': W2, 'b2': b2, 'W3': W3, 'b3': b3, 'W4': W4, 'b4': b4, 'W5': W5, 'b5': b5, 'W6': W6, 'b6': b6}
    _L0_gnn_all = _L0_gnn_setup()
    _L0_gnn_in = {k: v for k, v in _L0_gnn_all.items() if k in ('u', 'W1', 'b1', 'W2', 'b2', 'W3', 'b3', 'W4', 'b4', 'W5', 'b5', 'W6', 'b6')}
    del _L0_gnn_all

    def _L1_gnn_setup():
        import jax, jax.numpy as jnp
        import numpy as np
        N = 50000
        E = 31250
        D = 64
        L = 3
        LN_EPS = 1e-05

        def layernorm(h, g, b):
            mu = jnp.mean(h, axis=-1, keepdims=True)
            var = jnp.mean(jnp.square(h - mu), axis=-1, keepdims=True)
            return (h - mu) * jax.lax.rsqrt(var + LN_EPS) * g + b

        def transformer_conv(h, src, dst, Wq, bq, Wk, bk, Wv, bv, Ws, bs):
            n = h.shape[0]
            d = Wq.shape[1]
            q = h @ Wq + bq
            k = h @ Wk + bk
            v = h @ Wv + bv
            logits = jnp.sum(q[dst] * k[src], axis=-1) / jnp.sqrt(jnp.asarray(d, h.dtype))
            m = jax.ops.segment_max(logits, dst, num_segments=n)
            e = jnp.exp(logits - m[dst])
            s = jax.ops.segment_sum(e, dst, num_segments=n)
            a = e / s[dst]
            agg = jax.ops.segment_sum(a[:, None] * v[src], dst, num_segments=n)
            return agg + h @ Ws + bs
        key = jax.random.key(seed)
        ks = jax.random.split(key, 24)
        w = lambda k, shape: jax.random.normal(k, shape, jnp.float32) * 0.05
        inp = {'x': jax.random.normal(ks[0], (N, D), jnp.float32), 'edge_index': jax.random.randint(ks[1], (2, E), 0, N, jnp.int32), 'Wq0': w(ks[2], (D, D)), 'bq0': w(ks[3], (D,)), 'Wk0': w(ks[4], (D, D)), 'bk0': w(ks[5], (D,)), 'Wv0': w(ks[6], (D, D)), 'bv0': w(ks[7], (D,)), 'Ws0': w(ks[8], (D, D)), 'bs0': w(ks[9], (D,)), 'ln0_g': jnp.ones((D,), jnp.float32), 'ln0_b': jnp.zeros((D,), jnp.float32), 'Wq': w(ks[10], (L, D, D)), 'bq': w(ks[11], (L, D)), 'Wk': w(ks[12], (L, D, D)), 'bk': w(ks[13], (L, D)), 'Wv': w(ks[14], (L, D, D)), 'bv': w(ks[15], (L, D)), 'Ws': w(ks[16], (L, D, D)), 'bs': w(ks[17], (L, D)), 'ln_g': jnp.ones((L, D), jnp.float32), 'ln_b': jnp.zeros((L, D), jnp.float32)}
        return inp
    _L1_gnn_all = _L1_gnn_setup()
    _L1_gnn_in = {k: v for k, v in _L1_gnn_all.items() if k in ('Wq0', 'bq0', 'Wk0', 'bk0', 'Wv0', 'bv0', 'Ws0', 'bs0', 'ln0_g', 'ln0_b', 'Wq', 'bq', 'Wk', 'bk', 'Wv', 'bv', 'Ws', 'bs', 'ln_g', 'ln_b')}
    del _L1_gnn_all

    def _L2_gnn_setup():
        import jax, jax.numpy as jnp
        import numpy as np
        D = 4
        H = 16
        N = 50000
        E = 25000
        TI, TJ = np.tril_indices(D, -1)

        def _householder(params):
            A = jnp.zeros(params.shape[:-1] + (D, D), params.dtype)
            A = A.at[..., TI, TJ].set(params) + jnp.eye(D, dtype=params.dtype)
            Q, R = jnp.linalg.qr(A)
            s = jnp.sign(jnp.diagonal(R, axis1=-2, axis2=-1))
            s = jnp.where(s == 0, jnp.ones_like(s), s)
            return Q * s[..., None, :]

        def _mlp(z, w1, b1, w2, b2):
            h = jax.nn.relu(z @ w1.T + b1)
            return h @ w2.T + b2

        def _forward(x, edge_index, W1, W2, epsilons, mlp1_w, mlp1_b, mlp2_w, mlp2_b):
            n = x.shape[0]
            xr = x.reshape(n, D, H)
            xt = jnp.einsum('ndf,dk->nkf', xr, W1)
            xt = jnp.einsum('ndf,fg->ndg', xt, W2)
            loops = jnp.arange(n)
            row = jnp.concatenate([edge_index[0], loops])
            col = jnp.concatenate([edge_index[1], loops])
            deg = jax.ops.segment_sum(jnp.ones_like(row, x.dtype), row, num_segments=n)
            dis = jnp.where(deg > 0, deg ** (-0.5), jnp.zeros_like(deg))
            xf = xt.reshape(n, D * H)
            xi = xf[col]
            xj = xf[row]
            cat_ve = jnp.concatenate([xi, xj], axis=-1)
            cat_ue = jnp.concatenate([xj, xi], axis=-1)
            Fve = _householder(_mlp(cat_ve, mlp1_w, mlp1_b, mlp2_w, mlp2_b))
            Fue = _householder(_mlp(cat_ue, mlp1_w, mlp1_b, mlp2_w, mlp2_b))
            xjr = xj.reshape(-1, D, H)
            msg = jnp.einsum('eka,ekb,ebh->eah', Fve, Fue, xjr)
            msg = msg * (dis[col] * dis[row])[:, None, None]
            agg = jax.ops.segment_sum(msg.reshape(-1, D * H), col, num_segments=n)
            lap = jax.nn.elu(agg.reshape(n, D, H))
            coeff = (1.0 + jnp.tanh(epsilons))[None, :, None]
            return (coeff * xr - lap).reshape(n, D * H)
        key = jax.random.key(seed)
        ks = jax.random.split(key, 9)
        dh = D * H
        x = jax.random.normal(ks[0], (N, dh), jnp.float32)
        edge_index = jax.random.randint(ks[1], (2, E), 0, N, dtype=jnp.int64)
        W1 = jax.random.normal(ks[2], (D, D), jnp.float32) / np.sqrt(D)
        W2 = jax.random.normal(ks[3], (H, H), jnp.float32) / np.sqrt(H)
        epsilons = jnp.zeros((D,), jnp.float32)
        mlp1_w = jax.random.normal(ks[4], (H, 2 * dh), jnp.float32) / np.sqrt(2 * dh)
        mlp1_b = jnp.zeros((H,), jnp.float32)
        n_params = D * (D - 1) // 2
        mlp2_w = jax.random.normal(ks[5], (n_params, H), jnp.float32) / np.sqrt(H)
        mlp2_b = jnp.zeros((n_params,), jnp.float32)
        return {'x': x, 'edge_index': edge_index, 'W1': W1, 'W2': W2, 'epsilons': epsilons, 'mlp1_w': mlp1_w, 'mlp1_b': mlp1_b, 'mlp2_w': mlp2_w, 'mlp2_b': mlp2_b}
    _L2_gnn_all = _L2_gnn_setup()
    _L2_gnn_in = {k: v for k, v in _L2_gnn_all.items() if k in ('W1', 'W2', 'epsilons', 'mlp1_w', 'mlp1_b', 'mlp2_w', 'mlp2_b')}
    del _L2_gnn_all

    def _L3_gnn_setup():
        import jax, jax.numpy as jnp
        import numpy as np
        N_NODES = 50000
        N_EDGES = 37500
        IN_FEATS = 64
        OUT_FEATS = 64
        NEG_SLOPE = 0.01
        key = jax.random.key(seed)
        k1, k2, k3, k4, k5, k6 = jax.random.split(key, 6)
        feature = jax.random.normal(k1, (N_NODES, IN_FEATS), dtype=jnp.float32)
        attn_w = jax.random.normal(k2, (2 * IN_FEATS, 1), dtype=jnp.float32) * 0.1
        lin_w = jax.random.normal(k3, (OUT_FEATS, 2 * IN_FEATS), dtype=jnp.float32) * 0.1
        lin_b = jax.random.normal(k4, (OUT_FEATS,), dtype=jnp.float32) * 0.1
        src = jax.random.randint(k5, (N_EDGES,), 0, N_NODES, dtype=jnp.int32)
        dst = jax.random.randint(k6, (N_EDGES,), 0, N_NODES, dtype=jnp.int32)
        return {'feature': feature, 'attn_w': attn_w, 'lin_w': lin_w, 'lin_b': lin_b, 'src': src, 'dst': dst}
    _L3_gnn_all = _L3_gnn_setup()
    _L3_gnn_in = {k: v for k, v in _L3_gnn_all.items() if k in ('attn_w', 'lin_w', 'lin_b')}
    del _L3_gnn_all
    return {'x': x, 'src': src, 'dst': dst, 'edge_attr_32': edge_attr_32, 'L0_gnn_u': _L0_gnn_in['u'], 'L0_gnn_W1': _L0_gnn_in['W1'], 'L0_gnn_b1': _L0_gnn_in['b1'], 'L0_gnn_W2': _L0_gnn_in['W2'], 'L0_gnn_b2': _L0_gnn_in['b2'], 'L0_gnn_W3': _L0_gnn_in['W3'], 'L0_gnn_b3': _L0_gnn_in['b3'], 'L0_gnn_W4': _L0_gnn_in['W4'], 'L0_gnn_b4': _L0_gnn_in['b4'], 'L0_gnn_W5': _L0_gnn_in['W5'], 'L0_gnn_b5': _L0_gnn_in['b5'], 'L0_gnn_W6': _L0_gnn_in['W6'], 'L0_gnn_b6': _L0_gnn_in['b6'], 'L1_gnn_Wq0': _L1_gnn_in['Wq0'], 'L1_gnn_bq0': _L1_gnn_in['bq0'], 'L1_gnn_Wk0': _L1_gnn_in['Wk0'], 'L1_gnn_bk0': _L1_gnn_in['bk0'], 'L1_gnn_Wv0': _L1_gnn_in['Wv0'], 'L1_gnn_bv0': _L1_gnn_in['bv0'], 'L1_gnn_Ws0': _L1_gnn_in['Ws0'], 'L1_gnn_bs0': _L1_gnn_in['bs0'], 'L1_gnn_ln0_g': _L1_gnn_in['ln0_g'], 'L1_gnn_ln0_b': _L1_gnn_in['ln0_b'], 'L1_gnn_Wq': _L1_gnn_in['Wq'], 'L1_gnn_bq': _L1_gnn_in['bq'], 'L1_gnn_Wk': _L1_gnn_in['Wk'], 'L1_gnn_bk': _L1_gnn_in['bk'], 'L1_gnn_Wv': _L1_gnn_in['Wv'], 'L1_gnn_bv': _L1_gnn_in['bv'], 'L1_gnn_Ws': _L1_gnn_in['Ws'], 'L1_gnn_bs': _L1_gnn_in['bs'], 'L1_gnn_ln_g': _L1_gnn_in['ln_g'], 'L1_gnn_ln_b': _L1_gnn_in['ln_b'], 'L2_gnn_W1': _L2_gnn_in['W1'], 'L2_gnn_W2': _L2_gnn_in['W2'], 'L2_gnn_epsilons': _L2_gnn_in['epsilons'], 'L2_gnn_mlp1_w': _L2_gnn_in['mlp1_w'], 'L2_gnn_mlp1_b': _L2_gnn_in['mlp1_b'], 'L2_gnn_mlp2_w': _L2_gnn_in['mlp2_w'], 'L2_gnn_mlp2_b': _L2_gnn_in['mlp2_b'], 'L3_gnn_attn_w': _L3_gnn_in['attn_w'], 'L3_gnn_lin_w': _L3_gnn_in['lin_w'], 'L3_gnn_lin_b': _L3_gnn_in['lin_b']}

def reference(x, src, dst, edge_attr_32, L0_gnn_u, L0_gnn_W1, L0_gnn_b1, L0_gnn_W2, L0_gnn_b2, L0_gnn_W3, L0_gnn_b3, L0_gnn_W4, L0_gnn_b4, L0_gnn_W5, L0_gnn_b5, L0_gnn_W6, L0_gnn_b6, L1_gnn_Wq0, L1_gnn_bq0, L1_gnn_Wk0, L1_gnn_bk0, L1_gnn_Wv0, L1_gnn_bv0, L1_gnn_Ws0, L1_gnn_bs0, L1_gnn_ln0_g, L1_gnn_ln0_b, L1_gnn_Wq, L1_gnn_bq, L1_gnn_Wk, L1_gnn_bk, L1_gnn_Wv, L1_gnn_bv, L1_gnn_Ws, L1_gnn_bs, L1_gnn_ln_g, L1_gnn_ln_b, L2_gnn_W1, L2_gnn_W2, L2_gnn_epsilons, L2_gnn_mlp1_w, L2_gnn_mlp1_b, L2_gnn_mlp2_w, L2_gnn_mlp2_b, L3_gnn_attn_w, L3_gnn_lin_w, L3_gnn_lin_b):
    import jax
    import jax.numpy as jnp

    def _L0_gnn_ref(x, edge_index, edge_attr, u, batch, W1, b1, W2, b2, W3, b3, W4, b4, W5, b5, W6, b6):
        import jax, jax.numpy as jnp
        import numpy as np
        N_NODES = 3125
        N_EDGES = 50000
        N_GRAPHS = 64
        NODE_IN = 64
        EDGE_IN = 32
        GLOBAL_IN = 32
        NODE_OUT = 64
        MSG = 32

        def _linear_params(key, fan_in, fan_out):
            kw, kb = jax.random.split(key)
            s = 1.0 / np.sqrt(fan_in)
            W = jax.random.uniform(kw, (fan_in, fan_out), jnp.float32, -s, s)
            b = jax.random.uniform(kb, (fan_out,), jnp.float32, -s, s)
            return (W, b)
        row, col = (edge_index[0], edge_index[1])
        n = x.shape[0]
        m = jnp.concatenate([x[row], x[col], edge_attr], axis=1)
        h = jnp.maximum(m @ W1 + b1, 0.0)
        h = jnp.maximum(h @ W2 + b2, 0.0)
        h = h @ W3 + b3
        s = jax.ops.segment_sum(h, col, num_segments=n)
        cnt = jax.ops.segment_sum(jnp.ones((h.shape[0], 1), h.dtype), col, num_segments=n)
        agg_mean = s / jnp.maximum(cnt, 1.0)
        agg_max = jax.ops.segment_max(h, col, num_segments=n)
        agg_max = jnp.where(jnp.isfinite(agg_max), agg_max, 0.0)
        o = jnp.concatenate([x, agg_mean, agg_max, u[batch]], axis=1)
        o = jnp.maximum(o @ W4 + b4, 0.0)
        o = jnp.maximum(o @ W5 + b5, 0.0)
        return o @ W6 + b6

    def _L1_gnn_ref(x, edge_index, Wq0, bq0, Wk0, bk0, Wv0, bv0, Ws0, bs0, ln0_g, ln0_b, Wq, bq, Wk, bk, Wv, bv, Ws, bs, ln_g, ln_b):
        import jax, jax.numpy as jnp
        import numpy as np
        N = 50000
        E = 31250
        D = 64
        L = 3
        LN_EPS = 1e-05

        def layernorm(h, g, b):
            mu = jnp.mean(h, axis=-1, keepdims=True)
            var = jnp.mean(jnp.square(h - mu), axis=-1, keepdims=True)
            return (h - mu) * jax.lax.rsqrt(var + LN_EPS) * g + b

        def transformer_conv(h, src, dst, Wq, bq, Wk, bk, Wv, bv, Ws, bs):
            n = h.shape[0]
            d = Wq.shape[1]
            q = h @ Wq + bq
            k = h @ Wk + bk
            v = h @ Wv + bv
            logits = jnp.sum(q[dst] * k[src], axis=-1) / jnp.sqrt(jnp.asarray(d, h.dtype))
            m = jax.ops.segment_max(logits, dst, num_segments=n)
            e = jnp.exp(logits - m[dst])
            s = jax.ops.segment_sum(e, dst, num_segments=n)
            a = e / s[dst]
            agg = jax.ops.segment_sum(a[:, None] * v[src], dst, num_segments=n)
            return agg + h @ Ws + bs
        src, dst = (edge_index[0], edge_index[1])
        h = transformer_conv(x, src, dst, Wq0, bq0, Wk0, bk0, Wv0, bv0, Ws0, bs0)
        h = jax.nn.relu(layernorm(h, ln0_g, ln0_b))
        for i in range(L):
            hi = transformer_conv(h, src, dst, Wq[i], bq[i], Wk[i], bk[i], Wv[i], bv[i], Ws[i], bs[i])
            h = jax.nn.relu(layernorm(hi + h, ln_g[i], ln_b[i]))
        return h

    def _L2_gnn_ref(x, edge_index, W1, W2, epsilons, mlp1_w, mlp1_b, mlp2_w, mlp2_b):
        import jax, jax.numpy as jnp
        import numpy as np
        D = 4
        H = 16
        N = 50000
        E = 25000
        TI, TJ = np.tril_indices(D, -1)

        def _householder(params):
            A = jnp.zeros(params.shape[:-1] + (D, D), params.dtype)
            A = A.at[..., TI, TJ].set(params) + jnp.eye(D, dtype=params.dtype)
            Q, R = jnp.linalg.qr(A)
            s = jnp.sign(jnp.diagonal(R, axis1=-2, axis2=-1))
            s = jnp.where(s == 0, jnp.ones_like(s), s)
            return Q * s[..., None, :]

        def _mlp(z, w1, b1, w2, b2):
            h = jax.nn.relu(z @ w1.T + b1)
            return h @ w2.T + b2

        def _forward(x, edge_index, W1, W2, epsilons, mlp1_w, mlp1_b, mlp2_w, mlp2_b):
            n = x.shape[0]
            xr = x.reshape(n, D, H)
            xt = jnp.einsum('ndf,dk->nkf', xr, W1)
            xt = jnp.einsum('ndf,fg->ndg', xt, W2)
            loops = jnp.arange(n)
            row = jnp.concatenate([edge_index[0], loops])
            col = jnp.concatenate([edge_index[1], loops])
            deg = jax.ops.segment_sum(jnp.ones_like(row, x.dtype), row, num_segments=n)
            dis = jnp.where(deg > 0, deg ** (-0.5), jnp.zeros_like(deg))
            xf = xt.reshape(n, D * H)
            xi = xf[col]
            xj = xf[row]
            cat_ve = jnp.concatenate([xi, xj], axis=-1)
            cat_ue = jnp.concatenate([xj, xi], axis=-1)
            Fve = _householder(_mlp(cat_ve, mlp1_w, mlp1_b, mlp2_w, mlp2_b))
            Fue = _householder(_mlp(cat_ue, mlp1_w, mlp1_b, mlp2_w, mlp2_b))
            xjr = xj.reshape(-1, D, H)
            msg = jnp.einsum('eka,ekb,ebh->eah', Fve, Fue, xjr)
            msg = msg * (dis[col] * dis[row])[:, None, None]
            agg = jax.ops.segment_sum(msg.reshape(-1, D * H), col, num_segments=n)
            lap = jax.nn.elu(agg.reshape(n, D, H))
            coeff = (1.0 + jnp.tanh(epsilons))[None, :, None]
            return (coeff * xr - lap).reshape(n, D * H)
        return _forward(x, edge_index, W1, W2, epsilons, mlp1_w, mlp1_b, mlp2_w, mlp2_b)

    def _L3_gnn_ref(feature, attn_w, lin_w, lin_b, src, dst):
        import jax, jax.numpy as jnp
        import numpy as np
        N_NODES = 50000
        N_EDGES = 37500
        IN_FEATS = 64
        OUT_FEATS = 64
        NEG_SLOPE = 0.01
        N = feature.shape[0]
        a_src, a_dst = (attn_w[:IN_FEATS, 0], attn_w[IN_FEATS:, 0])
        e = jax.nn.leaky_relu(feature[src] @ a_src + feature[dst] @ a_dst, negative_slope=NEG_SLOPE)
        emax = jax.ops.segment_max(e, dst, num_segments=N)
        emax = jnp.where(jnp.isfinite(emax), emax, 0.0)
        ex = jnp.exp(e - emax[dst])
        denom = jax.ops.segment_sum(ex, dst, num_segments=N)
        num = jax.ops.segment_sum(ex[:, None] * feature[src], dst, num_segments=N)
        hm = jnp.where(denom[:, None] > 0, num / denom[:, None], 0.0)
        h = jnp.concatenate([feature, hm], axis=1) @ lin_w.T + lin_b
        return jax.nn.relu(h)
    edge_index = jnp.stack([src, dst])
    batch0 = jnp.zeros((3125,), jnp.int32)
    x = _layernorm(x + _L0_gnn_ref(x, edge_index, edge_attr_32, L0_gnn_u, batch0, L0_gnn_W1, L0_gnn_b1, L0_gnn_W2, L0_gnn_b2, L0_gnn_W3, L0_gnn_b3, L0_gnn_W4, L0_gnn_b4, L0_gnn_W5, L0_gnn_b5, L0_gnn_W6, L0_gnn_b6), axis=-1)
    x = _layernorm(x + _L1_gnn_ref(x, edge_index, L1_gnn_Wq0, L1_gnn_bq0, L1_gnn_Wk0, L1_gnn_bk0, L1_gnn_Wv0, L1_gnn_bv0, L1_gnn_Ws0, L1_gnn_bs0, L1_gnn_ln0_g, L1_gnn_ln0_b, L1_gnn_Wq, L1_gnn_bq, L1_gnn_Wk, L1_gnn_bk, L1_gnn_Wv, L1_gnn_bv, L1_gnn_Ws, L1_gnn_bs, L1_gnn_ln_g, L1_gnn_ln_b), axis=-1)
    x = _layernorm(x + _L2_gnn_ref(x, edge_index, L2_gnn_W1, L2_gnn_W2, L2_gnn_epsilons, L2_gnn_mlp1_w, L2_gnn_mlp1_b, L2_gnn_mlp2_w, L2_gnn_mlp2_b), axis=-1)
    x = _layernorm(x + _L3_gnn_ref(x, L3_gnn_attn_w, L3_gnn_lin_w, L3_gnn_lin_b, src, dst), axis=-1)
    return x

_drawn_inputs = setup_inputs


def setup_inputs(seed=0):
    import zlib

    import numpy as np

    out = dict(_drawn_inputs(seed))
    spreads = {'L1_gnn_ln0_g': (1.0, 0.2),
     'L1_gnn_ln0_b': (0.0, 0.1),
     'L1_gnn_ln_g': (1.0, 0.2),
     'L1_gnn_ln_b': (0.0, 0.1),
     'L2_gnn_epsilons': (0.0, 0.441),
     'L2_gnn_mlp1_b': (0.0, 0.564),
     'L2_gnn_mlp2_b': (0.0, 0.8)}
    factors = {'edge_attr_32': 8.0,
     'L0_gnn_W1': 8.0,
     'L0_gnn_b1': 30.962,
     'L0_gnn_W2': 8.0,
     'L0_gnn_b2': 52.104,
     'L0_gnn_W3': 6.938,
     'L0_gnn_b3': 59.56,
     'L0_gnn_b4': 40.736,
     'L1_gnn_bq0': 64.0,
     'L1_gnn_bk0': 64.0,
     'L1_gnn_Wq': 38.969,
     'L1_gnn_bq': 64.0,
     'L1_gnn_Wk': 25.316,
     'L1_gnn_bk': 64.0,
     'L0_gnn_u': 8.0,
     'L0_gnn_b5': 8.0,
     'L0_gnn_b6': 4.637,
     'L1_gnn_Wq0': 8.0,
     'L1_gnn_Wk0': 8.0,
     'L3_gnn_attn_w': 8.0}
    for name, (base, spread) in spreads.items():
        noise = np.random.default_rng([zlib.crc32(name.encode()), seed]).standard_normal(out[name].shape)
        drawn = base * np.exp(spread * noise) if base else spread * noise
        out[name] = jnp.asarray(drawn.astype(out[name].dtype))
    for name, factor in factors.items():
        out[name] = (out[name] * factor).astype(out[name].dtype)
    return out
```

```python
from contextlib import ExitStack, contextmanager

import numpy as np

import concourse.bass as bass
from concourse import mybir
from concourse.alu_op_type import AluOpType as ALU

F32 = mybir.dt.float32
I32 = mybir.dt.int32
U32 = mybir.dt.uint32
BF16 = mybir.dt.bfloat16
ACT = mybir.ActivationFunctionType
AX = mybir.AxisListType
ds = bass.ds

P = 128
N = 3125
F = 64
M = 32
NC = -(-N // P)
NP = NC * P
FULL = N // P
REST = N - FULL * P
E = 100000
BLK = 512
NB = 50
QE = NB * BLK
EP = 4 * QE
T = EP // P
QT = T // 4
ST = BLK // P
PAD_NODE = N
COUNTS = NP * NP
DB = 448
ND = 7
BIG = 1e38
OFF = 1e30
LN_EPS = 1e-5
assert ND * DB >= N and EP >= E and ND * DB <= NP


class Steps:

    def __init__(self, eng, sem, base=0):
        self.eng, self.sem, self.base, self.n = eng, sem, base, 0

    def mark(self, ins):
        ins.then_inc(self.sem, 1)
        self.n += 1

    def do(self, ins):
        self.mark(ins)
        self.eng.wait_ge(self.sem, self.base + self.n)


class Phase:

    def __init__(self, nc, ctx, name):
        self.nc, self.ctx, self.name = nc, ctx, name
        self.sems = []

    def sb(self, name, shape, dt=F32):
        return self.ctx.enter_context(self.nc.sbuf_tensor(f"{self.name}_{name}", shape, dt))

    def ps(self, name, shape, dt=F32):
        return self.ctx.enter_context(self.nc.psum_tensor(f"{self.name}_{name}", shape, dt))

    def sem(self, name):
        self.sems.append(self.nc.alloc_semaphore(f"{self.name}_{name}"))
        return self.sems[-1]

    def block(self):
        return self.ctx.enter_context(self.nc.Block())


@contextmanager
def phase(nc, name):
    with ExitStack() as ctx:
        ph = Phase(nc, ctx, name)
        yield ph
    nc.clear_and_free_semaphores(ph.sems)
    nc.all_engine_barrier()


def chunked(dram, lo=0, hi=NP):
    return dram[lo:hi, :].rearrange("(c p) f -> p c f", p=P)


def column(vec):
    return vec.rearrange("(p o) -> p o", o=1)


def row(vec):
    return vec.rearrange("(o n) -> o n", o=1)


def setup_phase(nc, io, dram, keep):
    with phase(nc, "su") as ph:
        xT = ph.sb("xT", [F, NP])
        wab = ph.sb("wab", [F, 2 * M])
        proj = ph.sb("proj", [P, NC, 2 * M])
        zeros = ph.sb("zeros", [P, 4000])
        tile_last_i = ph.sb("tile_last_i", [P, T], I32)
        tile_last = ph.sb("tile_last", [P, T])
        hits = ph.sb("hits", [P, T])
        bound_tile = ph.sb("bound_tile", [P, 2, NC])
        bound_idx = ph.sb("bound_idx", [P, 2, NC], I32)
        rows = ph.sb("rows", [P, 2, NC, P], I32)
        below = ph.sb("below", [P, 2, NC, P])
        in_row = ph.sb("in_row", [P, 2, NC])
        nid_i = ph.sb("nid_i", [P, NC], I32)
        dump_i = ph.sb("dump_i", [P, 1], I32)
        pp = ph.ps("pp", [P, 4, 512])
        cleared, loaded, consts, projected = (ph.sem(n) for n in ("cleared", "loaded", "consts", "projected"))
        last_in, zeroed, got_rows, idx_ready, copied = (ph.sem(n) for n in ("last_in", "zeroed", "got_rows", "idx_ready", "copied"))
        stored, dv, po = (ph.sem(n) for n in ("stored", "dv", "po"))
        block = ph.block()

        @block.sync
        def _(sp):
            sp.dma_start(tile_last_i[:, :], row(io["dst_last"]).to_broadcast([P, T])).then_inc(last_in, 16)
            sp.dma_start(wab[:, 0:M], io["L0_gnn_W1"][0:F, :]).then_inc(loaded, 16)
            sp.dma_start(wab[:, M:2 * M], io["L0_gnn_W1"][F:2 * F, :]).then_inc(loaded, 16)
            sp.dma_start(keep["src"][:, :], io["src_pm"]).then_inc(loaded, 16)
            sp.dma_start(keep["dst"][:, :], io["dst_pm"]).then_inc(loaded, 16)
            sp.wait_ge(cleared, 2)
            sp.dma_start(xT[:, 0:N], io["xT"]).then_inc(loaded, 16)
            sp.dma_start(keep["x"][:, 0:FULL, :], chunked(io["x"], 0, FULL * P)).then_inc(loaded, 16)
            sp.dma_start(keep["x"][0:REST, FULL, :], io["x"][FULL * P:N, :]).then_inc(loaded, 16)
            sp.wait_ge(copied, 1)
            sp.dma_start(chunked(dram["table_src"]), proj[:, :, 0:M]).then_inc(stored, 16)
            sp.dma_start(chunked(dram["table_dst"]), proj[:, :, M:2 * M]).then_inc(stored, 16)
            sp.wait_ge(stored, 32)
            sp.wait_ge(loaded, 16 * 7)

        @block.scalar
        def _(act):
            act.wait_ge(cleared, 3)
            counts = dram["counts"][0:COUNTS, :].rearrange("(p n) o -> p (n o)", p=P)
            for k in range(COUNTS // P // 4000):
                act.dma_start(counts[:, 4000 * k:4000 * (k + 1)], zeros[:, :]).then_inc(zeroed, 16)
            act.dma_start(dram["counts"][COUNTS:COUNTS + P, :], zeros[:, 0:1]).then_inc(zeroed, 16)
            act.wait_ge(zeroed, 16 * (COUNTS // P // 4000 + 1))

        @block.gpsimd
        def _(pool):
            s = Steps(pool, po)
            pool.memset(keep["ident"][:, :], 0.0).then_inc(po, 1)
            pool.memset(keep["tri"][:, :], 257.0).then_inc(po, 1)
            s.n = 2
            pool.wait_ge(po, 2)
            s.mark(pool.affine_select(out=keep["ident"][:, :], in_=keep["ident"][:, :], compare_op=ALU.not_equal,
                                      fill=1.0, base=0, pattern=[[-1, P]], channel_multiplier=1))
            s.mark(pool.affine_select(out=keep["tri"][:, :], in_=keep["tri"][:, :], compare_op=ALU.is_gt,
                                      fill=1.0, base=0, pattern=[[-1, P]], channel_multiplier=1))
            s.mark(pool.iota(nid_i[:, :], [[P, NC]], 0, 1))
            s.mark(pool.iota(dump_i[:, :], [[0, 1]], COUNTS, 1))
            pool.wait_ge(idx_ready, 1)
            for k in range(2):
                for c in range(NC):
                    pool.indirect_dma_start(rows[:, k, c, :], None, io["dst_tiles"],
                                            bass.IndirectOffsetOnAxis(bound_idx[:, k, c:c + 1].bitcast(U32), 0)
                                            ).then_inc(got_rows, 16)
            pool.wait_ge(got_rows, 16 * 2 * NC)

        @block.tensor
        def _(pe):
            pe.wait_ge(loaded, 16 * 7)
            for c in range(NC):
                ins = pe.matmul(pp[:, c // 8, F * (c % 8):F * (c % 8 + 1)], xT[:, P * c:P * c + P], wab[:, :],
                                start=True, stop=True)
            ins.then_inc(projected, 1)

        @block.vector
        def _(dve):
            dve.memset(xT[:, :], 0.0).then_inc(cleared, 1)
            dve.memset(keep["x"][:, :, :], 0.0).then_inc(cleared, 1)
            dve.memset(zeros[:, :], 0.0).then_inc(cleared, 1)
            s = Steps(dve, dv)
            dve.wait_ge(last_in, 16)
            dve.wait_ge(po, 6)
            s.mark(dve.tensor_copy(tile_last[:, :], tile_last_i[:, :]))
            s.mark(dve.tensor_copy(keep["dump"][:, :], dump_i[:, :]))
            s.do(dve.tensor_copy(keep["nid"][:, :], nid_i[:, :]))
            for k, op in enumerate((ALU.is_lt, ALU.is_le)):
                for c in range(NC):
                    s.do(dve.tensor_scalar(hits[:, :], tile_last[:, :], keep["nid"][:, c:c + 1], None, op, ALU.add,
                                           accum_out=bound_tile[:, k, c:c + 1]))
            s.do(dve.tensor_scalar(bound_tile[:, :, :], bound_tile[:, :, :], float(T - 1), None, ALU.min))
            dve.tensor_copy(bound_idx[:, :, :], bound_tile[:, :, :]).then_inc(idx_ready, 1)
            dve.wait_ge(loaded, 16 * 7)
            s.mark(dve.scalar_tensor_tensor(keep["key"][:, :], keep["dst"][:, :], float(NP), keep["src"][:, :],
                                            ALU.mult, ALU.add))
            dve.wait_ge(projected, 1)
            for b in range(4):
                w = min(8, NC - 8 * b)
                ins = dve.tensor_copy(proj[:, 8 * b:8 * b + w, :],
                                      pp[:, b, 0:F * w].rearrange("p (c f) -> p c f", f=F))
            ins.then_inc(copied, 1)
            dve.wait_ge(got_rows, 16 * 2 * NC)
            for k, op in enumerate((ALU.is_lt, ALU.is_le)):
                s.mark(dve.tensor_tensor(below[:, k, :, :], rows[:, k, :, :],
                                         keep["nid"][:, :].rearrange("p (c o) -> p c o", o=1).to_broadcast([P, NC, P]), op))
            dve.wait_ge(dv, s.n)
            for k in range(2):
                s.mark(dve.tensor_reduce(in_row[:, k, :], below[:, k, :, :], AX.X, ALU.add))
            dve.wait_ge(dv, s.n)
            for k, out in enumerate((keep["first"], keep["last"])):
                s.mark(dve.scalar_tensor_tensor(out[:, :], bound_tile[:, k, :], float(P), in_row[:, k, :],
                                                ALU.mult, ALU.add))
            dve.wait_ge(dv, s.n)
            s.mark(dve.tensor_tensor(keep["degree"][:, :], keep["last"][:, :], keep["first"][:, :], ALU.subtract))
            s.do(dve.tensor_scalar(keep["last"][:, :], keep["last"][:, :], -1.0, None, ALU.add))
            dve.tensor_scalar(keep["last_idx"][:, :], keep["last"][:, :], 0.0, None, ALU.max)


def message_phase(nc, io, dram, keep):
    with phase(nc, "ms") as ph:
        w1 = ph.sb("w1", [P, P])
        w2 = ph.sb("w2", [P, P])
        w3 = ph.sb("w3", [P, P])
        b1 = ph.sb("b1", [P, 1])
        b2 = ph.sb("b2", [P, 1])
        b3 = ph.sb("b3", [P, 1])
        attr = [ph.sb(f"attr{u}", [P, BLK]) for u in range(2)]
        seq = [ph.sb(f"seq{u}", [P, BLK + 1], I32) for u in range(2)]
        st_src = [ph.sb(f"st_src{u}", [P, ST, 4], I32) for u in range(2)]
        st_dst = [ph.sb(f"st_dst{u}", [P, ST, 4], I32) for u in range(2)]
        st_key = [ph.sb(f"st_key{u}", [P, ST, 4]) for u in range(2)]
        place = [ph.sb(f"place{u}", [P, ST * 4], I32) for u in range(2)]
        mult = [ph.sb(f"mult{u}", [P, ST * 4]) for u in range(2)]
        lead = ph.sb("lead", [P, ST * 4])
        moved = ph.sb("moved", [P, ST * 4])
        same = ph.sb("same", [P, 8, P], BF16)
        got_s = [ph.sb(f"got_s{u}", [P, ST, 4, M]) for u in range(2)]
        got_d = [ph.sb(f"got_d{u}", [P, ST, 4, M]) for u in range(2)]
        h1 = ph.sb("h1", [P, BLK])
        h2 = ph.sb("h2", [P, BLK])
        h3 = ph.sb("h3", [P, BLK])
        cont = ph.sb("cont", [P, BLK])
        gate = ph.sb("gate", [P, BLK])
        run_sum = [ph.sb(f"run_sum{u}", [P, BLK]) for u in range(2)]
        run_max = [ph.sb(f"run_max{u}", [P, BLK]) for u in range(2)]
        out_t = ph.sb("out_t", [P, ST, 4, 2 * M])
        p1, p2, p3, pts, ptm = (ph.ps(n, [P, BLK]) for n in ("p1", "p2", "p3", "pts", "ptm"))
        pkey = [ph.ps(f"pkey{u}", [P, 4, P]) for u in range(2)]
        wz, weights, staged, keyed, keyfree, placed = (ph.sem(n) for n in ("wz", "weights", "staged", "keyed", "keyfree", "placed"))
        multiplied, mm1, mm2, mm3, act1, act2, act3 = (ph.sem(n) for n in ("multiplied", "mm1", "mm2", "mm3", "act1", "act2", "act3"))
        scanned, turned, masked, turned_out, out_st = (ph.sem(n) for n in ("scanned", "turned", "masked", "turned_out", "out_st"))
        counted, dv, ds0 = (ph.sem(n) for n in ("counted", "dv", "ds0"))
        attr_in = [ph.sem(f"attr_in{u}") for u in range(2)]
        seq_in = [ph.sem(f"seq_in{u}") for u in range(2)]
        got = [[ph.sem(f"got{u}_{i}") for i in range(ST)] for u in range(2)]
        block = ph.block()

        attr_d = io["edge_T"]
        seq_d = io["dst_seq"]
        quarter = dram["runs"].rearrange("(q b i p) f -> q b p i f", q=4, b=NB, i=ST)

        def loop(eng, body, count=NB // 2):
            with eng.Fori(0, count - 1) as it:
                body(it, False)
            body(count - 1, True)

        @block.sync
        def _(sp):
            sp.wait_ge(wz, 1)
            k = 0
            for q in range(4):
                lo = M * q
                for w, b, ww, bb in ((w1, b1, io["L0_gnn_W1"][2 * F:2 * F + M, :], "L0_gnn_b1"),
                                     (w2, b2, io["L0_gnn_W2"], "L0_gnn_b2"), (w3, b3, io["L0_gnn_W3"], "L0_gnn_b3")):
                    sp.dma_start(w[lo:lo + M, lo:lo + M], ww).then_inc(weights, 16)
                    sp.dma_start(b[lo:lo + M, :], column(io[bb])).then_inc(weights, 16)
                    k += 2
            assert k == 24

            def load(at, u):
                sp.dma_start(attr[u][:, :], attr_d[:, ds(at, BLK)]).then_inc(attr_in[u], 16)
                for q in range(4):
                    sp.dma_start(seq[u][M * q:M * q + M, :],
                                 seq_d[q:q + 1, ds(at, BLK + 1)].to_broadcast([M, BLK + 1])).then_inc(seq_in[u], 16)

            load(0, 0)
            load(BLK, 1)
            at, done = sp.alloc_register("edges_loaded"), sp.alloc_register("blocks_done")
            sp.reg_mov(at, BLK)
            sp.reg_mov(done, 0)
            with sp.Fori(0, NB // 2 - 1):
                for u in range(2):
                    sp.reg_add(at, at, BLK)
                    sp.reg_add(done, done, 1)
                    blocks = sp.snap(done)
                    sp.wait_ge(wz, 1)
                    sp.wait_ge(multiplied, blocks)
                    sp.wait_ge(masked, blocks)
                    load(sp.snap(at), u)
            sp.wait_ge(weights, 16 * 24)

        @block.gpsimd
        def _(pool):
            turn = pool.alloc_register("block_turn")
            sent = pool.alloc_register("tiles_counted")
            pool.reg_mov(turn, 0)
            pool.reg_mov(sent, 0)

            def body(it, last):
                for u in range(2):
                    pool.reg_add(turn, turn, 1)
                    now = pool.snap(turn)
                    pool.wait_ge(ds0, 1)
                    pool.wait_ge(placed, now)
                    pool.wait_ge(mm1, now)
                    for i in range(ST):
                        for q in range(4):
                            j = 4 * i + q
                            pool.indirect_dma_start(
                                dram["counts"], bass.IndirectOffsetOnAxis(place[u][:, j:j + 1].bitcast(U32), 0),
                                mult[u][:, j:j + 1], None, compute_op=ALU.add).then_inc(counted, 16)
                            pool.indirect_dma_start(
                                got_s[u][:, i, q, :], None, dram["table_src"],
                                bass.IndirectOffsetOnAxis(st_src[u][:, i, q:q + 1].bitcast(U32), 0)).then_inc(got[u][i], 16)
                            pool.indirect_dma_start(
                                got_d[u][:, i, q, :], None, dram["table_dst"],
                                bass.IndirectOffsetOnAxis(st_dst[u][:, i, q:q + 1].bitcast(U32), 0)).then_inc(got[u][i], 16)
                            pool.reg_add(sent, sent, 16)
                            so_far = pool.snap(sent)
                            pool.wait_ge(ds0, 1)
                            pool.wait_ge(counted, so_far)

            with pool.Fori(0, NB // 2) as it:
                body(it, False)

        @block.vector
        def _(dve):
            for w in (w1, w2, w3):
                ins = dve.memset(w[:, :], 0.0)
            ins.then_inc(wz, 1)
            dve.memset(run_sum[1][:, :], 0.0)
            dve.memset(run_max[1][:, :], 0.0).then_inc(ds0, 1)
            dve.wait_ge(ds0, 1)

            def stage(b, u):
                for st, of in ((st_src, "src"), (st_dst, "dst"), (st_key, "key")):
                    ins = dve.tensor_copy(st[u][:, :, :].rearrange("p i q -> p q i"),
                                          keep[of][:, :].rearrange("p (q t) -> p q t", q=4)[:, :, ds(b * ST, ST)])
                ins.then_inc(staged, 1)

            def places(b, u, s):
                dve.wait_ge(staged, b + 1)
                for h in range(4):
                    dve.wait_ge(keyed, 4 * b + h + 1)
                    for j in range(4 * h, 4 * h + 4):
                        ins = dve.scalar_tensor_tensor(same[:, j % 8, :], pkey[h % 2][:, j % 4, :],
                                                       st_key[u][:, j // 4, j % 4:j % 4 + 1], keep["tri"][:, :],
                                                       ALU.is_equal, ALU.mult, accum_out=mult[u][:, j:j + 1])
                    s.do(ins)
                    dve.sem_inc(keyfree, 1)
                s.mark(dve.tensor_scalar(lead[:, :], mult[u][:, :], 256.0, None, ALU.is_lt))
                s.do(dve.tensor_scalar(moved[:, :], st_key[u][:, :, :].rearrange("p i q -> p (i q)"), keep["dump"][:, 0:1],
                                       None, ALU.subtract))
                s.do(dve.tensor_tensor(moved[:, :], moved[:, :], lead[:, :], ALU.mult))
                dve.tensor_scalar(place[u][:, :], moved[:, :], keep["dump"][:, 0:1], None, ALU.add).then_inc(placed, 1)

            def scans(b, u, s, it):
                dve.wait_ge(seq_in[u], it * 64 + 64)
                s.do(dve.tensor_tensor(cont[:, :], seq[u][:, 1:BLK + 1], seq[u][:, 0:BLK], ALU.is_equal))
                s.do(dve.tensor_scalar(gate[:, :], cont[:, :], BIG, -BIG, ALU.mult, ALU.add))
                dve.sem_inc(masked, 1)
                dve.wait_ge(act3, b + 1)
                dve.tensor_tensor_scan(run_sum[u][:, :], cont[:, :], h3[:, :], run_sum[1 - u][:, BLK - 1:BLK],
                                       ALU.mult, ALU.add)
                dve.tensor_tensor_scan(run_max[u][:, :], gate[:, :], h3[:, :], run_max[1 - u][:, BLK - 1:BLK],
                                       ALU.add, ALU.max).then_inc(scanned, 1)
                dve.wait_ge(scanned, b + 1)

            PER = 9
            stage(0, 0)
            s0 = Steps(dve, dv)
            places(0, 0, s0)
            assert s0.n == 7, s0.n

            def body(it, last):
                for u in range(2):
                    b = it * 2 + u
                    ahead = not (last and u == 1)
                    s = Steps(dve, dv, b * PER + 7)
                    if ahead:
                        stage(b + 1, 1 - u)
                        places(b + 1, 1 - u, s)
                    scans(b, u, s, it)
                    assert s.n == (PER if ahead else PER - 7), s.n
                    dve.wait_ge(counted, (b + 1) * 16 * 4 * ST)

            loop(dve, body)

        @block.tensor
        def _(pe):
            pe.sem_inc(mm1, 2)
            pe.wait_ge(weights, 16 * 24)

            def keys(b, u):
                pe.wait_ge(staged, b + 1)
                for h in range(4):
                    pe.wait_ge(keyfree, 4 * b + h - 1 + 2)
                    for j in range(4 * h, 4 * h + 4):
                        ins = pe.matmul(pkey[h % 2][:, j % 4, :], st_key[u][:, j // 4, j % 4:j % 4 + 1].to_broadcast([P, P]),
                                        keep["ident"][:, :], start=True, stop=True)
                    ins.then_inc(keyed, 1)

            pe.sem_inc(keyfree, 2)
            keys(0, 0)

            def body(it, last):
                for u in range(2):
                    b = it * 2 + u
                    if not (last and u == 1):
                        keys(b + 1, 1 - u)
                    pe.wait_ge(attr_in[u], it * 16 + 16)
                    pe.matmul(p1[:, :], w1[:, :], attr[u][:, :], start=True, stop=False).then_inc(multiplied, 1)
                    for i in range(ST):
                        pe.wait_ge(got[u][i], it * 128 + 128)
                        for g in (got_s, got_d):
                            ins = pe.matmul(p1[:, P * i:P * i + P], g[u][:, i, :, :].rearrange("p q m -> p (q m)"),
                                            keep["ident"][:, :], start=False, stop=(i == ST - 1 and g is got_d))
                    ins.then_inc(mm1, 1)
                    pe.wait_ge(act1, b + 1)
                    pe.matmul(p2[:, :], w2[:, :], h1[:, :], start=True, stop=True).then_inc(mm2, 1)
                    pe.wait_ge(act2, b + 1)
                    pe.matmul(p3[:, :], w3[:, :], h2[:, :], start=True, stop=True).then_inc(mm3, 1)
                    pe.wait_ge(scanned, b + 1)
                    for of, to in ((run_sum, pts), (run_max, ptm)):
                        for i in range(ST):
                            ins = pe.transpose(to[:, P * i:P * i + P], of[u][:, P * i:P * i + P], keep["ident"][:, :])
                    ins.then_inc(turned, 1)

            loop(pe, body)

        @block.scalar
        def _(act):
            act.wait_ge(weights, 16 * 24)

            def body(it, last):
                for u in range(2):
                    b = it * 2 + u
                    act.wait_ge(mm1, b + 3)
                    act.activation(h1[:, :], p1[:, :], ACT.Relu, bias=b1[:, 0:1]).then_inc(act1, 1)
                    act.wait_ge(mm2, b + 1)
                    act.activation(h2[:, :], p2[:, :], ACT.Relu, bias=b2[:, 0:1]).then_inc(act2, 1)
                    act.wait_ge(mm3, b + 1)
                    act.activation(h3[:, :], p3[:, :], ACT.Identity, bias=b3[:, 0:1]).then_inc(act3, 1)
                    act.wait_ge(turned, b + 1)
                    for of, lo in ((pts, 0), (ptm, M)):
                        ins = act.activation(out_t[:, :, :, lo:lo + M],
                                             of[:, :].rearrange("p (i q m) -> p i q m", i=ST, q=4), ACT.Copy)
                    ins.then_inc(turned_out, 1)
                    act.wait_ge(turned_out, b + 1)
                    for q in range(4):
                        act.dma_start(quarter[q, b], out_t[:, :, q, :]).then_inc(out_st, 16)
                    act.wait_ge(out_st, b * 64 + 64)

            with act.Fori(0, NB // 2) as it:
                body(it, False)


def spread(col, f=F):
    return col.rearrange("p (c o) -> p c o", o=1).to_broadcast([P, NC, f])


def norm_scratch(ph):
    w = {k: ph.sb(f"ln_{k}", [P, NC]) for k in ("mean", "var", "dev", "rstd")}
    w["mid"], w["square"] = (ph.sb(f"ln_{k}", [P, NC, F]) for k in ("mid", "square"))
    w["has_var"], w["has_dev"] = ph.sem("ln_has_var"), ph.sem("ln_has_dev")
    return w


def norm_vector(dve, s, w, k, x, out):
    s.do(dve.tensor_reduce(w["mean"][:, :], x, AX.X, ALU.add))
    s.do(dve.tensor_scalar(w["mean"][:, :], w["mean"][:, :], 1.0 / F, None, ALU.mult))
    s.do(dve.tensor_tensor(w["mid"][:, :, :], x, spread(w["mean"][:, :]), ALU.subtract))
    s.do(dve.tensor_tensor(w["square"][:, :, :], w["mid"][:, :, :], w["mid"][:, :, :], ALU.mult))
    s.do(dve.tensor_reduce(w["var"][:, :], w["square"][:, :, :], AX.X, ALU.add))
    dve.tensor_scalar(w["var"][:, :], w["var"][:, :], 1.0 / F, LN_EPS, ALU.mult, ALU.add).then_inc(w["has_var"], 1)
    dve.wait_ge(w["has_dev"], k)
    s.do(dve.reciprocal(w["rstd"][:, :], w["dev"][:, :]))
    s.mark(dve.tensor_tensor(out, w["mid"][:, :, :], spread(w["rstd"][:, :]), ALU.mult))


def norm_scalar(act, w, k):
    act.wait_ge(w["has_var"], k)
    act.activation(w["dev"][:, :], w["var"][:, :], ACT.Sqrt).then_inc(w["has_dev"], 1)


def node_phase(nc, io, dram, keep):
    with phase(nc, "nd") as ph:
        runs = ph.sb("runs", [P, NC, 2 * M])
        edge_rows = ph.sb("edge_rows", [P, 3, 2 * M])
        across = ph.sb("across", [P, 3, NC])
        off = ph.sb("off", [P, NC])
        part = ph.sb("part", [P, NC, 2 * M])
        has, inv = ph.sb("has", [P, NC]), ph.sb("inv", [P, NC])
        cat = ph.sb("cat", [P, NC, P])
        catT = ph.sb("catT", [P, NP])
        w4, w4u = ph.sb("w4", [P, M]), ph.sb("w4u", [M, M])
        w5, w6 = ph.sb("w5", [M, M]), ph.sb("w6", [M + 1, F])
        u0, b4, b5 = ph.sb("u0", [M, 1]), ph.sb("b4", [M, 1]), ph.sb("b5", [M, 1])
        b4u = ph.sb("b4u", [M, 1])
        a4, a5 = ph.sb("a4", [M, NP]), ph.sb("a5", [M + 1, NP])
        res = ph.sb("res", [P, NC, F])
        w = norm_scratch(ph)
        pt = ph.ps("pt", [P, 7 * 512])
        pu = ph.ps("pu", [P, 512])
        loaded, got, joined, turned, copied, mm, acted, dv, rows_in = (ph.sem(n) for n in (
            "loaded", "got", "joined", "turned", "copied", "mm", "acted", "dv", "rows_in"))
        block = ph.block()
        ends = [QE * (q + 1) - 1 for q in range(3)]

        @block.sync
        def _(sp):
            for q, e in enumerate(ends):
                sp.dma_start(edge_rows[:, q, :], dram["runs"][e:e + 1, :].to_broadcast([P, 2 * M])).then_inc(rows_in, 16)
            w4_d = io["L0_gnn_W4"]
            sp.dma_start(w4[:, :], w4_d[0:P, :]).then_inc(loaded, 16)
            sp.dma_start(w4u[:, :], w4_d[P:P + M, :]).then_inc(loaded, 16)
            sp.dma_start(w5[:, :], io["L0_gnn_W5"]).then_inc(loaded, 16)
            sp.dma_start(w6[0:M, :], io["L0_gnn_W6"]).then_inc(loaded, 16)
            sp.dma_start(w6[M:M + 1, :], row(io["L0_gnn_b6"])).then_inc(loaded, 16)
            sp.dma_start(u0[:, :], column(io["L0_gnn_u"][0, :])).then_inc(loaded, 16)
            sp.dma_start(b4[:, :], column(io["L0_gnn_b4"])).then_inc(loaded, 16)
            sp.dma_start(b5[:, :], column(io["L0_gnn_b5"])).then_inc(loaded, 16)

        @block.gpsimd
        def _(pool):
            for c in range(NC):
                pool.indirect_dma_start(runs[:, c, :], None, dram["runs"],
                                        bass.IndirectOffsetOnAxis(keep["last_idx"][:, c:c + 1].bitcast(U32), 0)).then_inc(got, 16)

        @block.vector
        def _(dve):
            s = Steps(dve, dv)
            s.mark(dve.memset(a5[M:M + 1, :], 1.0))
            for q, e in enumerate(ends):
                s.do(dve.tensor_scalar(across[:, q, :], keep["first"][:, :], float(e), None, ALU.is_le))
                s.do(dve.scalar_tensor_tensor(across[:, q, :], keep["last"][:, :], float(e), across[:, q, :],
                                              ALU.is_gt, ALU.mult))
            s.do(dve.tensor_scalar(inv[:, :], keep["degree"][:, :], 1.0, None, ALU.max))
            s.do(dve.reciprocal(inv[:, :], inv[:, :]))
            s.do(dve.tensor_scalar(has[:, :], keep["degree"][:, :], 0.0, None, ALU.is_gt))
            s.do(dve.tensor_tensor(inv[:, :], inv[:, :], has[:, :], ALU.mult))
            s.mark(dve.tensor_copy(cat[:, :, 0:F], keep["x"][:, :, :]))
            dve.wait_ge(rows_in, 48)
            dve.wait_ge(got, 16 * NC)
            for q in range(3):
                s.do(dve.tensor_scalar(off[:, :], across[:, q, :], BIG, -BIG, ALU.mult, ALU.add))
                s.do(dve.tensor_tensor(part[:, :, :], edge_rows[:, q:q + 1, :].to_broadcast([P, NC, 2 * M]),
                                       spread(across[:, q, :]), ALU.mult))
                s.do(dve.tensor_tensor(part[:, :, M:2 * M], part[:, :, M:2 * M], spread(off[:, :], M), ALU.add))
                s.do(dve.tensor_tensor(runs[:, :, 0:M], runs[:, :, 0:M], part[:, :, 0:M], ALU.add))
                s.do(dve.tensor_tensor(runs[:, :, M:2 * M], runs[:, :, M:2 * M], part[:, :, M:2 * M], ALU.max))
            s.do(dve.tensor_tensor(cat[:, :, F:F + M], runs[:, :, 0:M], spread(inv[:, :], M), ALU.mult))
            dve.tensor_tensor(cat[:, :, F + M:P], runs[:, :, M:2 * M], spread(has[:, :], M), ALU.mult).then_inc(joined, 1)
            dve.wait_ge(turned, 1)
            dve.tensor_copy(catT[:, :], pt[:, 0:NP]).then_inc(copied, 1)
            dve.wait_ge(loaded, 16 * 8)
            dve.wait_ge(mm, 1)
            dve.tensor_tensor(b4u[:, :], pu[0:M, 0:1], b4[:, :], ALU.add).then_inc(copied, 1)
            dve.wait_ge(mm, 4)
            s.do(dve.tensor_tensor(res[:, :, :].rearrange("p c f -> p (c f)"), pt[:, 0:NC * F],
                                   keep["x"][:, :, :].rearrange("p c f -> p (c f)"), ALU.add))
            norm_vector(dve, s, w, 1, res[:, :, :], keep["x"][:, :, :])

        @block.tensor
        def _(pe):
            pe.wait_ge(joined, 1)
            for c in range(NC):
                ins = pe.transpose(pt[:, P * c:P * c + P], cat[:, c, :], keep["ident"][:, :])
            ins.then_inc(turned, 1)
            pe.wait_ge(loaded, 16 * 8)
            pe.matmul(pu[0:M, 0:1], w4u[:, :], u0[:, :], start=True, stop=True).then_inc(mm, 1)

            def product(weight, of, rows_, m):
                for k in range(0, NP, 512):
                    n = min(512, NP - k)
                    ins = pe.matmul(pt[0:m, k:k + n], weight, of[0:rows_, k:k + n], start=True, stop=True)
                ins.then_inc(mm, 1)

            pe.wait_ge(copied, 2)
            product(w4[:, :], catT, P, M)
            pe.wait_ge(acted, 1)
            product(w5[:, :], a4, M, M)
            pe.wait_ge(acted, 2)
            for c in range(NC):
                ins = pe.matmul(pt[:, F * c:F * c + F], a5[:, P * c:P * c + P], w6[:, :], start=True, stop=True)
            ins.then_inc(mm, 1)

        @block.scalar
        def _(act):
            act.wait_ge(copied, 2)
            act.wait_ge(mm, 2)
            act.activation(a4[:, :], pt[0:M, 0:NP], ACT.Relu, bias=b4u[:, 0:1]).then_inc(acted, 1)
            act.wait_ge(dv, 1)
            act.wait_ge(mm, 3)
            act.activation(a5[0:M, :], pt[0:M, 0:NP], ACT.Relu, bias=b5[:, 0:1]).then_inc(acted, 1)
            norm_scalar(act, w, 1)


def dense_phase(nc, io, dram, keep):
    with phase(nc, "de") as ph:
        cnt = [ph.sb(f"cnt{u}", [P, NP]) for u in range(2)]
        mask = [ph.sb(f"mask{u}", [P, NP], BF16) for u in range(2)]
        logs = [ph.sb(f"logs{u}", [P, NC, P]) for u in range(2)]
        tiny = ph.sb("tiny", [P, 1])
        leave = ph.sb("leave", [P, NC])
        G = -(-NC // 4)
        pt = [ph.ps(f"pt{g}", [P, 4, P]) for g in range(G)]
        loaded = [ph.sem(f"loaded{u}") for u in range(2)]
        masked, turned, logged, evened, stored, freed, dv, ready = (ph.sem(n) for n in (
            "masked", "turned", "logged", "evened", "stored", "freed", "dv", "ready"))
        block = ph.block()
        counts = dram["counts"][0:COUNTS, :].rearrange("(c p s) o -> c p (s o)", p=P, s=NP)
        mask_d = dram["mask"].rearrange("(c p) s -> c p s", p=P)
        logs_d = dram["logs"].rearrange("(c p) d -> p c d", p=P)

        def loop(eng, body):
            with eng.Fori(0, NC // 2) as it:
                for u in range(2):
                    body(it * 2 + u, u, it)
            body(NC - 1, 0, NC // 2)

        @block.sync
        def _(sp):
            sp.dma_start(cnt[0][:, :], counts[0]).then_inc(loaded[0], 16)
            sp.dma_start(cnt[1][:, :], counts[1]).then_inc(loaded[1], 16)
            sp.wait_ge(ready, 1)
            c = sp.alloc_register("groups_evened")
            done, groups, stores = (sp.alloc_register(n) for n in ("chunks_done", "groups_done", "stores_done"))
            for r in (done, groups, stores):
                sp.reg_mov(r, 0)
            sp.reg_mov(c, G)

            def serve(u, more):
                sp.reg_add(done, done, 1)
                sp.reg_add(groups, groups, G)
                sp.reg_add(stores, stores, 32)
                n_done, n_groups, n_stores = sp.snap(done), sp.snap(groups), sp.snap(stores)
                sp.wait_ge(ready, 1)
                sp.wait_ge(masked, n_done)
                sp.wait_ge(turned, n_groups)
                if more:
                    sp.dma_start(cnt[u][:, :], counts[n_done + 1]).then_inc(loaded[u], 16)
                sp.dma_start(mask_d[n_done - 1], mask[u][:, :]).then_inc(stored, 16)
                sp.reg_add(c, c, G)
                logs_done = sp.snap(c)
                sp.wait_ge(ready, 1)
                sp.wait_ge(evened, logs_done)
                sp.dma_start(logs_d[:, :, ds((n_done - 1) * P, P)], logs[u][:, :, :]).then_inc(stored, 16)
                sp.wait_ge(stored, n_stores)
                sp.sem_inc(freed, 1)

            with sp.Fori(0, (NC - 3) // 2):
                serve(0, True)
                serve(1, True)
            serve(0, True)
            serve(1, False)
            serve(0, False)

        @block.vector
        def _(dve):
            dve.memset(tiny[:, :], 1e-18)
            dve.memset(keep["out_deg"][:, :], 1.0).then_inc(ready, 1)
            dve.sem_inc(freed, 2)
            dve.wait_ge(ready, 1)

            def body(c, u, it):
                dve.wait_ge(loaded[u], it * 16 + 16)
                dve.wait_ge(freed, c + 1)
                dve.tensor_scalar(mask[u][:, :], cnt[u][:, :], 0.0, -OFF, ALU.is_equal, ALU.mult).then_inc(masked, 1)
                s = Steps(dve, dv, c * 2)
                for g in range(G):
                    w = min(4, NC - 4 * g)
                    dve.wait_ge(logged, c * G + g + 1)
                    ins = dve.tensor_reduce(leave[:, 4 * g:4 * g + w], pt[g][:, 0:w, :], AX.X, ALU.add)
                    if g == G - 1:
                        s.do(ins)
                    part = logs[u][:, 4 * g:4 * g + w, :].rearrange("p c d -> p (c d)")
                    dve.scalar_tensor_tensor(part, part, OFF, part, ALU.mult, ALU.min).then_inc(evened, 1)
                s.do(dve.tensor_tensor(keep["out_deg"][:, :], keep["out_deg"][:, :], leave[:, :], ALU.add))

            loop(dve, body)

        @block.tensor
        def _(pe):
            def body(c, u, it):
                pe.wait_ge(loaded[u], it * 16 + 16)
                for g in range(G):
                    pe.wait_ge(evened, c * G + g + 1)
                    for k in range(min(4, NC - 4 * g)):
                        j = 4 * g + k
                        ins = pe.transpose(pt[g][:, k, :], cnt[u][:, P * j:P * j + P], keep["ident"][:, :])
                    ins.then_inc(turned, 1)

            pe.sem_inc(evened, G)
            loop(pe, body)

        @block.scalar
        def _(act):
            act.wait_ge(ready, 1)

            def body(c, u, it):
                act.wait_ge(freed, c + 1)
                for g in range(G):
                    w = min(4, NC - 4 * g)
                    act.wait_ge(turned, c * G + g + 1)
                    act.activation(logs[u][:, 4 * g:4 * g + w, :], pt[g][:, 0:w, :], ACT.Ln,
                                   bias=tiny[:, 0:1], scale=float(np.e)).then_inc(logged, 1)

            loop(act, body)


def conv_phase(nc, io, dram, keep, l):
    with phase(nc, f"c{l}") as ph:
        aug = F + 1
        hT = ph.sb("hT", [aug, NP])
        oT = hT
        kT, qT = ph.sb("kT", [aug, NP]), ph.sb("qT", [aug, NP])
        v = ph.sb("v", [P, NC, aug])
        res = ph.sb("res", [P, NC, F])
        agg = ph.sb("agg", [P, NC, F])
        wq, wk, wvs = ph.sb("wq", [aug, F]), ph.sb("wk", [aug, F]), ph.sb("wvs", [aug, 2 * F])
        gain, offset = ph.sb("gain", [P, F]), ph.sb("offset", [P, F])
        mask_in = [ph.sb(f"mask{u}", [P, NP], BF16) for u in range(2)]
        q_st = [ph.sb(f"q_st{u}", [F, P]) for u in range(2)]
        sink = ph.sb("sink", [P, 4, 2 * DB], BF16)
        peaks = ph.sb("peaks", [P, 4])
        peak = ph.sb("peak", [P, NC])
        LG = 5
        R = 5
        LAG = 3
        logs = [ph.sb(f"logs{k}", [P, LG, DB]) for k in range(NC // LG)]
        xs = [ph.sb(f"xs{r}", [P, DB]) for r in range(R)]
        es = [ph.sb(f"es{r}", [P, DB]) for r in range(R)]
        den = ph.sb("den", [P, NC])
        w = norm_scratch(ph)
        pa = ph.ps("pa", [P, 7, 512])
        po = ph.ps("po", [P, 512])
        flat = pa[:, :, :].rearrange("p b n -> p (b n)")
        mask_loaded = [ph.sem(f"mask_loaded{u}") for u in range(2)]
        logs_loaded = [ph.sem(f"logs_loaded{k}") for k in range(NC // LG)]
        (loaded, turned, copied, mm, acted, staged, scored, peaked, dv, rowed, row_in, scored2, added, exped,
         weighted, evac, back) = (ph.sem(n) for n in (
             "loaded", "turned", "copied", "mm", "acted", "staged", "scored", "peaked", "dv", "rowed", "row_in",
             "scored2", "added", "exped", "weighted", "evac", "back"))
        block = ph.block()
        if l == 0:
            W = {k: io[f"L1_gnn_W{k}0"] for k in "qkvs"}
            B = {k: io[f"L1_gnn_b{k}0"] for k in "qkvs"}
            g_d, b_d = io["L1_gnn_ln0_g"], io["L1_gnn_ln0_b"]
        else:
            W = {k: io[f"L1_gnn_W{k}"][l - 1] for k in "qkvs"}
            B = {k: io[f"L1_gnn_b{k}"][l - 1, :] for k in "qkvs"}
            g_d, b_d = io["L1_gnn_ln_g"][l - 1, :], io["L1_gnn_ln_b"][l - 1, :]
        h = keep["x"] if l == 0 else keep["h"]
        mask_d = dram["mask"].rearrange("(c p) s -> c p s", p=P)
        logs_d = dram["logs"].rearrange("(c p) d -> p c d", p=P)
        NG = 4
        PAIRS = [(2 * g, min(2, ND - 2 * g)) for g in range(NG)]

        def loop(eng, body):
            with eng.Fori(0, NC // 2) as it:
                for u in range(2):
                    body(it * 2 + u, u, it)
            body(NC - 1, 0, NC // 2)

        @block.sync
        def _(sp):
            for to, of in ((wq, "q"), (wk, "k")):
                sp.dma_start(to[0:F, :], W[of]).then_inc(loaded, 16)
                sp.dma_start(to[F:aug, :], row(B[of])).then_inc(loaded, 16)
            for lo, of in ((0, "v"), (F, "s")):
                sp.dma_start(wvs[0:F, lo:lo + F], W[of]).then_inc(loaded, 16)
                sp.dma_start(wvs[F:aug, lo:lo + F], row(B[of])).then_inc(loaded, 16)
            sp.dma_start(gain[:, :], row(g_d).to_broadcast([P, F])).then_inc(loaded, 16)
            sp.dma_start(offset[:, :], row(b_d).to_broadcast([P, F])).then_inc(loaded, 16)
            sp.dma_start(mask_in[0][:, :], mask_d[0]).then_inc(mask_loaded[0], 16)
            sp.dma_start(mask_in[1][:, :], mask_d[1]).then_inc(mask_loaded[1], 16)
            for k in range(NC // LG):
                sp.dma_start(logs[k][:, :, :], logs_d[:, LG * k:LG * k + LG, 0:DB]).then_inc(logs_loaded[k], 16)
            used, nxt = sp.alloc_register(f"masks_used{l}"), sp.alloc_register(f"next_mask{l}")
            sp.reg_mov(used, NG)
            sp.reg_mov(nxt, 1)

            def reload(u):
                sp.reg_add(used, used, NG)
                sp.reg_add(nxt, nxt, 1)
                n_used = sp.snap(used)
                sp.wait_ge(loaded, 16 * 10)
                sp.wait_ge(peaked, n_used)
                sp.dma_start(mask_in[u][:, :], mask_d[sp.snap(nxt)]).then_inc(mask_loaded[u], 16)

            with sp.Fori(0, (NC - 3) // 2):
                reload(0)
                reload(1)
            reload(0)
            adds, at = sp.alloc_register(f"logs_used{l}"), sp.alloc_register(f"next_logs{l}")
            sp.reg_mov(adds, R)
            sp.reg_mov(at, 0)
            with sp.Fori(0, ND - 1):
                sp.reg_add(at, at, DB)
                for k in range(NC // LG):
                    sp.reg_add(adds, adds, LG)
                    n_adds = sp.snap(adds)
                    sp.wait_ge(loaded, 16 * 10)
                    sp.wait_ge(added, n_adds)
                    sp.dma_start(logs[k][:, :, :], logs_d[:, LG * k:LG * k + LG, ds(sp.snap(at), DB)]
                                 ).then_inc(logs_loaded[k], 16)

        @block.tensor
        def _(pe):
            for c in range(NC):
                ins = pe.transpose(flat[0:F, P * c:P * c + P], h[:, c, :], keep["ident"][:, :])
            ins.then_inc(turned, 1)
            pe.wait_ge(loaded, 16 * 10)
            for n, weight in enumerate((wq, wk)):
                pe.wait_ge(copied, 1)
                if n:
                    pe.wait_ge(acted, n)
                for k in range(0, NP, 512):
                    m = min(512, NP - k)
                    ins = pe.matmul(flat[0:F, k:k + m], weight[:, :], hT[:, k:k + m], start=True, stop=True)
                ins.then_inc(mm, 1)
            pe.wait_ge(acted, 2)
            for c in range(NC):
                ins = pe.matmul(flat[:, P * c:P * c + P], hT[:, P * c:P * c + P], wvs[:, :], start=True, stop=True)
            ins.then_inc(mm, 1)
            pe.wait_ge(copied, 2)
            pe.sem_inc(peaked, NG)

            def chunk_scores(c, u, it):
                pe.wait_ge(staged, c + 1)
                for g, (b0, nb) in enumerate(PAIRS):
                    pe.wait_ge(peaked, c * NG + g + 1)
                    for b in range(b0, b0 + nb):
                        ins = pe.matmul(pa[:, b, 0:DB], q_st[u][:, :], kT[0:F, DB * b:DB * b + DB], start=True, stop=True)
                    ins.then_inc(scored, 1)

            loop(pe, chunk_scores)
            pe.wait_ge(rowed, 1)
            for c in range(NC):
                ins = pe.matmul(flat[F:F + 1, P * c:P * c + P], peak[:, c:c + 1], keep["ident"][:, :], start=True, stop=True)
            ins.then_inc(mm, 1)
            pe.wait_ge(row_in, 1)
            pe.sem_inc(added, R)
            pe.sem_inc(weighted, R)
            pe.sem_inc(evac, 1)
            with pe.Fori(0, ND) as j:
                def weigh(c):
                    pe.wait_ge(exped, j * NC + c + 1 + R)
                    if c == 0:
                        pe.wait_ge(evac, j + 1)
                    pe.matmul(po[0:aug, 0:DB], v[:, c, :], es[c % R][:, :], start=(c == 0), stop=(c == NC - 1)
                              ).then_inc(weighted, 1)

                for c in range(NC):
                    pe.wait_ge(added, j * NC + c + 1)
                    pe.matmul(pa[:, c % R, 0:DB], kT[:, P * c:P * c + P], qT[:, ds(j * DB, DB)], start=True, stop=True
                              ).then_inc(scored2, 1)
                    if c >= LAG:
                        weigh(c - LAG)
                for c in range(NC - LAG, NC):
                    weigh(c)
            pe.wait_ge(evac, ND + 1)
            for c in range(NC):
                ins = pe.transpose(pa[:, c // 7, aug * (c % 7):aug * (c % 7 + 1)], oT[:, P * c:P * c + P],
                                   keep["ident"][0:aug, 0:aug])
            ins.then_inc(back, 1)

        @block.vector
        def _(dve):
            dve.sem_inc(exped, R)
            s = Steps(dve, dv)
            s.mark(dve.memset(hT[F:aug, :], 1.0))
            s.mark(dve.memset(kT[F:aug, :], 1.0))
            s.mark(dve.memset(v[:, :, F:aug], 1.0))
            dve.wait_ge(turned, 1)
            dve.tensor_copy(hT[0:F, :], flat[0:F, 0:NP]).then_inc(copied, 1)
            dve.wait_ge(mm, 3)
            vs = flat[:, 0:NC * P].rearrange("p (c f) -> p c f", f=P)
            dve.tensor_copy(v[:, :, 0:F], vs[:, :, 0:F])
            dve.tensor_copy(res[:, :, :], vs[:, :, F:P]).then_inc(copied, 1)

            group = dve.alloc_register(f"group{l}")
            dve.reg_mov(group, 0)

            def chunk_peak(c, u, it):
                dve.wait_ge(mask_loaded[u], it * 16 + 16)
                for g, (b0, nb) in enumerate(PAIRS):
                    dve.reg_add(group, group, 1)
                    now = dve.snap(group)
                    dve.wait_ge(copied, 2)
                    dve.wait_ge(scored, now)
                    dve.tensor_tensor_reduce(
                        sink[:, g, 0:nb * DB].rearrange("p (b n) -> p b n", n=DB), pa[:, b0:b0 + nb, 0:DB],
                        mask_in[u][:, b0 * DB:(b0 + nb) * DB].rearrange("p (b n) -> p b n", n=DB),
                        1.0, -3e38, ALU.add, ALU.max, peaks[:, g:g + 1]).then_inc(peaked, 1)
                dve.wait_ge(peaked, c * NG + 2 * NG)
                dve.tensor_reduce(peak[:, ds(c, 1)], peaks[:, :], AX.X, ALU.max).then_inc(dv, 1)
                dve.wait_ge(dv, c + 4)

            loop(dve, chunk_peak)
            s.n += NC
            dve.tensor_scalar(peak[:, :], peak[:, :], -1e29, -1.0, ALU.max, ALU.mult).then_inc(rowed, 1)
            dve.memset(oT[:, ND * DB:NP], 0.0).then_inc(rowed, 1)
            dve.wait_ge(rowed, 2)
            with dve.Fori(0, ND) as j:
                for c in range(NC):
                    if c % LG == 0:
                        dve.wait_ge(logs_loaded[c // LG], j * 16 + 16)
                    dve.wait_ge(scored2, j * NC + c + 1)
                    dve.wait_ge(exped, j * NC + c + 1)
                    dve.tensor_tensor(xs[c % R][:, :], pa[:, c % R, 0:DB], logs[c // LG][:, c % LG, :], ALU.add
                                      ).then_inc(added, 1)
            dve.wait_ge(back, 1)
            for b in range(4):
                n = min(7, NC - 7 * b)
                s.mark(dve.tensor_scalar(den[:, 7 * b:7 * b + n],
                                         pa[:, b, 0:aug * n].rearrange("p (c f) -> p c f", f=aug)[:, :, F], 1e-30, None, ALU.max))
            dve.wait_ge(dv, s.n)
            s.do(dve.reciprocal(den[:, :], den[:, :]))
            for b in range(4):
                n = min(7, NC - 7 * b)
                s.mark(dve.tensor_tensor(agg[:, 7 * b:7 * b + n, :],
                                         pa[:, b, 0:aug * n].rearrange("p (c f) -> p c f", f=aug)[:, :, 0:F],
                                         den[:, 7 * b:7 * b + n].rearrange("p (c o) -> p c o", o=1).to_broadcast([P, n, F]),
                                         ALU.mult))
            dve.wait_ge(dv, s.n)
            s.do(dve.tensor_tensor(res[:, :, :], res[:, :, :], agg[:, :, :], ALU.add))
            if l:
                s.do(dve.tensor_tensor(res[:, :, :], res[:, :, :], h[:, :, :], ALU.add))
            norm_vector(dve, s, w, 1, res[:, :, :], agg[:, :, :])
            dve.wait_ge(dv, s.n)

            def per_feature(vec):
                return vec[:, :].rearrange("p (o f) -> p o f", o=1).to_broadcast([P, NC, F])

            dve.wait_ge(loaded, 16 * 10)
            s.do(dve.tensor_tensor(agg[:, :, :], agg[:, :, :], per_feature(gain), ALU.mult))
            s.do(dve.tensor_tensor(agg[:, :, :], agg[:, :, :], per_feature(offset), ALU.add))
            s.do(dve.tensor_scalar(keep["h"][:, :, :], agg[:, :, :], 0.0, None, ALU.max))
            if l == 3:
                s.do(dve.tensor_tensor(res[:, :, :], keep["x"][:, :, :], keep["h"][:, :, :], ALU.add))
                norm_vector(dve, s, w, 2, res[:, :, :], keep["x"][:, :, :])

        @block.scalar
        def _(act):
            act.wait_ge(mm, 1)
            act.activation(qT[0:F, :], flat[0:F, 0:NP], ACT.Copy, scale=float(F) ** -0.5).then_inc(acted, 1)
            act.wait_ge(mm, 2)
            act.activation(kT[0:F, :], flat[0:F, 0:NP], ACT.Copy).then_inc(acted, 1)
            act.wait_ge(acted, 1)

            def stage(c, u):
                act.activation(q_st[u][:, :], qT[0:F, ds(c * P, P)], ACT.Copy).then_inc(staged, 1)

            stage(0, 0)
            stage(1, 1)
            with act.Fori(0, (NC - 3) // 2) as it:
                for u in range(2):
                    act.wait_ge(scored, (it * 2 + u + 1) * NG)
                    stage(it * 2 + u + 2, u)
            act.wait_ge(scored, (NC - 2) * NG)
            stage(NC - 1, 0)
            act.wait_ge(mm, 4)
            act.activation(qT[F:aug, :], flat[F:F + 1, 0:NP], ACT.Copy).then_inc(row_in, 1)
            act.wait_ge(row_in, 1)
            with act.Fori(0, ND) as j:
                for c in range(NC):
                    act.wait_ge(added, j * NC + c + 1 + R)
                    act.wait_ge(weighted, j * NC + c + 1)
                    act.activation(es[c % R][:, :], xs[c % R][:, :], ACT.Exp).then_inc(exped, 1)
                act.wait_ge(weighted, j * NC + NC + R)
                act.activation(oT[:, ds(j * DB, DB)], po[0:aug, 0:DB], ACT.Copy).then_inc(evac, 1)
            norm_scalar(act, w, 1)
            if l == 3:
                norm_scalar(act, w, 2)


D4 = 4
H16 = F // D4
WS = 2 * H16 + F + 4
WD = 2 * H16 + 4
PAIRS_B = 16
TB = 2 * PAIRS_B
HB = EP // 2 // (PAIRS_B * P)
HE = EP // 2


def sheaf_tables_phase(nc, io, dram, keep):
    with phase(nc, "st") as ph:
        xT, yT, zT = (ph.sb(n, [F, NP]) for n in ("xT", "yT", "zT"))
        w1c = ph.sb("w1c", [F, D4])
        same = ph.sb("same", [F, H16])
        w1x, w2x = ph.sb("w1x", [F, D4, H16]), ph.sb("w2x", [F, F])
        mix = ph.sb("mix", [F, 2 * H16 + F])
        root = ph.sb("root", [P, NC])
        pt = ph.ps("pt", [P, 7 * 512])
        zero, loaded, turned, copied, mm, rooted, dv, stored = (ph.sem(n) for n in (
            "zero", "loaded", "turned", "copied", "mm", "rooted", "dv", "stored"))
        block = ph.block()
        src_tab, dst_tab = keep["src_tab"], keep["dst_tab"]

        @block.sync
        def _(sp):
            for d in range(D4):
                sp.dma_start(w1c[H16 * d:H16 * d + H16, :], io["L2_gnn_W1"][d:d + 1, :].to_broadcast([H16, D4])).then_inc(loaded, 16)
            sp.dma_start(mix[:, 0:H16], io["mlp1_T"][0:F, :]).then_inc(loaded, 16)
            sp.dma_start(mix[:, H16:2 * H16], io["mlp1_T"][F:2 * F, :]).then_inc(loaded, 16)
            sp.wait_ge(zero, 1)
            for d in range(D4):
                lo = H16 * d
                sp.dma_start(w2x[lo:lo + H16, lo:lo + H16], io["L2_gnn_W2"]).then_inc(loaded, 16)
            sp.wait_ge(copied, 4)
            sp.dma_start(chunked(dram["sheaf_src"]), src_tab[:, :, :]).then_inc(stored, 16)
            sp.dma_start(chunked(dram["sheaf_dst"]), dst_tab[:, :, :]).then_inc(stored, 16)
            sp.wait_ge(stored, 32)

        @block.tensor
        def _(pe):
            for c in range(NC):
                ins = pe.transpose(pt[0:F, P * c:P * c + P], keep["x"][:, c, :], keep["ident"][:, :])
            ins.then_inc(turned, 1)
            pe.wait_ge(loaded, 16 * 10)
            pe.wait_ge(dv, 2)
            for n, (weight, of) in enumerate(((w1x[:, :, :].rearrange("p k f -> p (k f)"), xT), (w2x[:, :], yT))):
                pe.wait_ge(copied, n + 1)
                for k in range(0, NP, 512):
                    m = min(512, NP - k)
                    ins = pe.matmul(pt[0:F, k:k + m], weight, of[:, k:k + m], start=True, stop=True)
                ins.then_inc(mm, 1)
            pe.wait_ge(copied, 3)
            for c in range(NC):
                ins = pe.matmul(pt[:, P * c:P * c + 2 * H16 + F], zT[:, P * c:P * c + P], mix[:, :], start=True, stop=True)
            ins.then_inc(mm, 1)

        @block.scalar
        def _(act):
            act.activation(root[:, :], keep["out_deg"][:, :], ACT.Sqrt).then_inc(rooted, 1)

        @block.vector
        def _(dve):
            dve.memset(w2x[:, :], 0.0).then_inc(zero, 1)
            dve.memset(src_tab[:, :, :], 0.0)
            dve.memset(dst_tab[:, :, :], 0.0)
            s = Steps(dve, dv)
            dve.tensor_copy(mix[:, 2 * H16:2 * H16 + F], keep["ident"][0:F, 0:F])
            s.do(dve.tensor_reduce(same[:, :], keep["ident"][0:F, 0:F].rearrange("p (d f) -> p f d", d=D4), AX.X, ALU.add))
            dve.wait_ge(loaded, 16 * 10)
            s.do(dve.tensor_tensor(w1x[:, :, :], w1c[:, :].rearrange("p (k o) -> p k o", o=1).to_broadcast([F, D4, H16]),
                                   same[:, :].rearrange("p (o f) -> p o f", o=1).to_broadcast([F, D4, H16]), ALU.mult))
            dve.wait_ge(turned, 1)
            dve.tensor_copy(xT[:, :], pt[0:F, 0:NP]).then_inc(copied, 1)
            for n, to in enumerate((yT, zT)):
                dve.wait_ge(mm, n + 1)
                dve.tensor_copy(to[:, :], pt[0:F, 0:NP]).then_inc(copied, 1)
            dve.wait_ge(rooted, 1)
            for tab, at in ((src_tab, 2 * H16 + F), (dst_tab, 2 * H16)):
                s.mark(dve.reciprocal(tab[:, :, at], root[:, :]))
            dve.wait_ge(mm, 3)
            out = pt[:, 0:NC * P].rearrange("p (c f) -> p c f", f=P)
            dve.tensor_copy(src_tab[:, :, 0:2 * H16 + F], out[:, :, 0:2 * H16 + F])
            dve.tensor_copy(dst_tab[:, :, 0:H16], out[:, :, H16:2 * H16])
            dve.tensor_copy(dst_tab[:, :, H16:2 * H16], out[:, :, 0:H16]).then_inc(copied, 1)


def sheaf_phase(nc, io, dram, keep):
    with phase(nc, "sh") as ph:
        got_s = [ph.sb(f"got_s{u}", [P, TB, WS]) for u in range(2)]
        got_d = [ph.sb(f"got_d{u}", [P, TB, WD]) for u in range(2)]
        st_src = [ph.sb(f"st_src{u}", [P, PAIRS_B, 2], I32) for u in range(2)]
        st_dst = [ph.sb(f"st_dst{u}", [P, PAIRS_B, 2], I32) for u in range(2)]
        NSEQ = PAIRS_B * P
        seq = [ph.sb(f"seq{u}", [P, NSEQ + 1], I32) for u in range(2)]
        cont = ph.sb("cont", [P, NSEQ])
        bias1 = ph.sb("bias1", [P, 1])
        bias2 = ph.sb("bias2", [P, 6])
        w2 = ph.sb("w2", [P, 48])
        zin = ph.sb("zin", [P, TB, 2 * H16])
        hz = ph.sb("hz", [P, TB // 4, P])
        MT = 2 * TB
        tri = ph.sb("tri", [P, MT, 4, 4])
        q = ph.sb("q", [P, MT, 4, 4])
        prod = ph.sb("prod", [P, MT, 3, 4])
        dot = ph.sb("dot", [P, MT, 3])
        norm2, norm1, inv = (ph.sb(n, [P, MT]) for n in ("norm2", "norm1", "inv"))
        scale = ph.sb("scale", [P, TB])
        gprod = ph.sb("gprod", [P, TB, 4, 16])
        g = ph.sb("g", [P, TB, 16])
        msg = ph.sb("msg", [P, TB, F])
        term = ph.sb("term", [P, TB, F])
        run = [ph.sb(f"run{k}", [P, 512]) for k in range(2)]
        out_t = ph.sb("out_t", [P, PAIRS_B, 2, F])
        pz = ph.ps("pz", [P, TB // 4, P])
        pp = ph.ps("pp", [P, TB // 4, 8, 6])
        pin = [ph.ps(f"pin{k}", [P, 512]) for k in range(2)]
        pout = [ph.ps(f"pout{k}", [P, 512]) for k in range(2)]
        (zero, loaded, ready, staged, messaged, zed, hidden, parred, sized, rooted, turned, scanned, backed, copied,
         stored, masked, added, dv) = (ph.sem(n) for n in (
             "zero", "loaded", "ready", "staged", "messaged", "zed",  "hidden", "parred", "sized", "rooted", "turned",
             "scanned", "backed", "copied", "stored", "masked", "added", "dv"))
        got = [ph.sem(f"got{u}") for u in range(2)]
        seq_in = [ph.sem(f"seq_in{u}") for u in range(2)]
        block = ph.block()
        sums_d = dram["sums"].rearrange("(h b i p) f -> h b p i f", h=2, b=HB, i=PAIRS_B)
        NB4 = PAIRS_B // 4
        assert HB % 2 == 1

        def loop(eng, body):
            body(1, 1, 0)
            with eng.Fori(0, HB // 2) as it:
                body(it * 2 + 2, 0, it)
                body(it * 2 + 3, 1, it + 1)

        @block.sync
        def _(sp):
            for k in range(8):
                sp.dma_start(bias1[H16 * k:H16 * k + H16, :], column(io["L2_gnn_mlp1_b"])).then_inc(loaded, 16)
            sp.dma_start(bias2[:, :], row(io["mlp2_b"]).to_broadcast([P, 6])).then_inc(loaded, 16)
            sp.wait_ge(zero, 1)
            for k in range(8):
                sp.dma_start(w2[H16 * k:H16 * k + H16, 6 * k:6 * k + 6], io["mlp2_T"]).then_inc(loaded, 16)

            def load(at, u):
                for h in range(2):
                    sp.dma_start(seq[u][F * h:F * h + F, :],
                                 io["dst_half"][h:h + 1, ds(at, NSEQ + 1)].to_broadcast([F, NSEQ + 1])).then_inc(seq_in[u], 16)

            load(0, 1)
            load(NSEQ, 0)
            at, masks = sp.alloc_register("edges_at"), sp.alloc_register("masks_done")
            sp.reg_mov(at, NSEQ)
            sp.reg_mov(masks, 0)

            def again(u):
                sp.reg_add(at, at, NSEQ)
                sp.reg_add(masks, masks, 1)
                n_masks = sp.snap(masks)
                sp.wait_ge(zero, 1)
                sp.wait_ge(masked, n_masks)
                load(sp.snap(at), u)

            with sp.Fori(0, (HB - 3) // 2):
                again(1)
                again(0)
            again(1)

        @block.gpsimd
        def _(pool):
            turn = pool.alloc_register("sheaf_turn")
            pool.reg_mov(turn, 0)

            def body(n, u, it):
                pool.reg_add(turn, turn, 1)
                now = pool.snap(turn)
                pool.wait_ge(ready, 1)
                pool.wait_ge(staged, now)
                pool.wait_ge(messaged, now)
                for i in range(PAIRS_B):
                    for h in range(2):
                        for to, st, tab in ((got_s, st_src, "sheaf_src"), (got_d, st_dst, "sheaf_dst")):
                            pool.indirect_dma_start(
                                to[u][:, 2 * i + h, :], None, dram[tab],
                                bass.IndirectOffsetOnAxis(st[u][:, i, h:h + 1].bitcast(U32), 0)).then_inc(got[u], 16)

            loop(pool, body)

        @block.vector
        def _(dve):
            dve.memset(w2[:, :], 0.0).then_inc(zero, 1)
            dve.memset(got_s[0][:, :, :], 0.0)
            dve.memset(got_d[0][:, :, :], 0.0)
            dve.memset(tri[:, :, :, :], 0.0)
            dve.memset(run[1][:, :], 0.0).then_inc(ready, 1)
            dve.sem_inc(messaged, 1)
            dve.wait_ge(ready, 1)
            s = Steps(dve, dv)
            for k in range(4):
                s.mark(dve.memset(tri[:, :, k, k], 1.0))
            s.mark(dve.tensor_copy(got_s[0][:, 0:NC, :], keep["src_tab"][:, :, :]))
            s.mark(dve.tensor_copy(got_d[0][:, 0:NC, :], keep["dst_tab"][:, :, :]))
            dve.wait_ge(dv, 6)
            dve.sem_inc(ready, 1)

            def stage(b, u):
                for st, of in ((st_src, "src"), (st_dst, "dst")):
                    ins = dve.tensor_copy(st[u][:, :, :].rearrange("p i h -> p h i"),
                                          keep[of][:, :].rearrange("p (h t) -> p h t", h=2)[:, :, ds(b * PAIRS_B, PAIRS_B)])
                ins.then_inc(staged, 1)

            def messages(n, u, it, s):
                if it is not None:
                    dve.wait_ge(got[u], it * 1024 + 1024)
                dve.tensor_tensor(zin[:, :, :], got_s[u][:, :, 0:2 * H16], got_d[u][:, :, 0:2 * H16], ALU.add).then_inc(added, 1)
                dve.wait_ge(parred, n + 1)
                for col, lo, hi in ((0, 0, 3), (1, 3, 5), (2, 5, 6)):
                    w = hi - lo
                    ins = dve.tensor_tensor(
                        tri[:, :, col, 4 - w:4], pp[:, :, :, lo:hi].rearrange("p a b k -> p (a b) k"),
                        bias2[:, lo:hi].rearrange("p (o k) -> p o k", o=1).to_broadcast([P, MT, w]), ALU.add)
                    s.mark(ins)
                s.do(dve.tensor_tensor(scale[:, :], got_s[u][:, :, 2 * H16 + F], got_d[u][:, :, 2 * H16], ALU.mult))
                left = tri
                for k in range(4):
                    a = left[:, :, k, :]
                    s.do(dve.tensor_tensor(prod[:, :, 0, :], a, a, ALU.mult))
                    dve.tensor_reduce(norm2[:, :], prod[:, :, 0, :], AX.X, ALU.add).then_inc(sized, 1)
                    dve.wait_ge(rooted, 4 * n + k + 1)
                    s.do(dve.reciprocal(inv[:, :], norm1[:, :]))
                    s.do(dve.tensor_tensor(q[:, :, k, :], a, inv[:, :].rearrange("p (m o) -> p m o", o=1).to_broadcast([P, MT, 4]),
                                           ALU.mult))
                    if k < 3:
                        m = 3 - k
                        qk = q[:, :, k:k + 1, :].to_broadcast([P, MT, m, 4])
                        s.do(dve.tensor_tensor(prod[:, :, 0:m, :], left[:, :, k + 1:4, :], qk, ALU.mult))
                        s.do(dve.tensor_reduce(dot[:, :, 0:m], prod[:, :, 0:m, :], AX.X, ALU.add))
                        s.do(dve.tensor_tensor(prod[:, :, 0:m, :], qk, dot[:, :, 0:m].rearrange("p m (j o) -> p m j o", o=1)
                                               .to_broadcast([P, MT, m, 4]), ALU.mult))
                        s.do(dve.tensor_tensor(q[:, :, k + 1:4, :], left[:, :, k + 1:4, :], prod[:, :, 0:m, :], ALU.subtract))
                    left = q
                both = q[:, :, :, :].rearrange("p (t v) c r -> p t v (c r)", v=2)
                ue, ve = both[:, :, 0, :], both[:, :, 1, :]
                s.do(dve.tensor_tensor(ve, ve, scale[:, :].rearrange("p (t o) -> p t o", o=1).to_broadcast([P, TB, 16]), ALU.mult))
                for a in range(4):
                    s.mark(dve.tensor_tensor(
                        gprod[:, :, a, :].rearrange("p t (b k) -> p t b k", k=4), ue.rearrange("p t (b k) -> p t b k", k=4),
                        ve[:, :, 4 * a:4 * a + 4].rearrange("p t (o k) -> p t o k", o=1).to_broadcast([P, TB, 4, 4]), ALU.mult))
                dve.wait_ge(dv, s.base + s.n)
                s.do(dve.tensor_reduce(g[:, :, :], gprod[:, :, :, :].rearrange("p t a (b k) -> p t (a b) k", k=4), AX.X, ALU.add))
                ga = g[:, :, :].rearrange("p t (a b) -> p t a b", b=4)
                stalks = [got_s[u][:, :, 2 * H16 + H16 * b:2 * H16 + H16 * (b + 1)].rearrange("p t (o h) -> p t o h", o=1)
                          .to_broadcast([P, TB, 4, H16]) for b in range(4)]
                m4 = msg[:, :, :].rearrange("p t (a h) -> p t a h", a=4)
                t4 = term[:, :, :].rearrange("p t (a h) -> p t a h", a=4)
                for b in range(4):
                    s.do(dve.tensor_tensor(t4 if b else m4, stalks[b], ga[:, :, :, b:b + 1].to_broadcast([P, TB, 4, H16]), ALU.mult))
                    if b:
                        s.do(dve.tensor_tensor(msg[:, :, :], msg[:, :, :], term[:, :, :], ALU.add))
                dve.sem_inc(messaged, 1)

            PER = 4 + 4 * 3 + 3 * 4 + 1 + 4 + 1 + 7
            stage(0, 1)
            s = Steps(dve, dv, 6)
            messages(0, 0, None, s)
            assert s.n == PER, (s.n, PER)
            s.do(dve.tensor_copy(keep["loops"][:, :, :], msg[:, 0:NC, :]))

            def body(n, u, it, ahead=True):
                s = Steps(dve, dv, n * PER + 7)
                messages(n, u, it, s)
                assert s.n == PER
                if ahead:
                    stage(n, 1 - u)
                dve.wait_ge(seq_in[u], it * 32 + 32)
                dve.tensor_tensor(cont[:, :], seq[u][:, 1:NSEQ + 1], seq[u][:, 0:NSEQ], ALU.is_equal).then_inc(masked, 1)
                dve.wait_ge(masked, n)
                for k in range(NB4):
                    dve.wait_ge(turned, (n - 1) * NB4 + k + 1)
                    dve.tensor_tensor_scan(run[k % 2][:, :], cont[:, 512 * k:512 * k + 512], pin[k % 2][:, :],
                                           run[1 - k % 2][:, 511:512], ALU.mult, ALU.add).then_inc(scanned, 1)
                    dve.wait_ge(scanned, (n - 1) * NB4 + k + 1)

            body(1, 1, 0)
            with dve.Fori(0, HB // 2 - 1) as it:
                body(it * 2 + 2, 0, it)
                body(it * 2 + 3, 1, it + 1)
            it = HB // 2 - 1
            body(it * 2 + 2, 0, it)
            body(it * 2 + 3, 1, it + 1, ahead=False)

        @block.tensor
        def _(pe):
            pe.wait_ge(loaded, 16 * 17)
            pe.wait_ge(ready, 2)

            def hidden_and_entries(n):
                pe.wait_ge(added, n + 1)
                for k in range(TB // 4):
                    ins = pe.transpose(pz[:, k, :], zin[:, 4 * k:4 * k + 4, :].rearrange("p t f -> p (t f)"), keep["ident"][:, :])
                ins.then_inc(zed, 1)
                pe.wait_ge(hidden, n + 1)
                for k in range(TB // 4):
                    ins = pe.matmul(pp[:, k, :, :].rearrange("p a b -> p (a b)"), hz[:, k, :], w2[:, :], start=True, stop=True)
                ins.then_inc(parred, 1)

            hidden_and_entries(0)
            pe.sem_inc(copied, 2)

            def body(n, u, it):
                pe.wait_ge(messaged, n + 1)
                hidden_and_entries(n)
                pe.wait_ge(messaged, n + 2)
                for k in range(NB4 + 1):
                    if k < NB4:
                        for j in range(4):
                            i = 4 * k + j
                            ins = pe.transpose(pin[k % 2][:, P * j:P * j + P],
                                               msg[:, 2 * i:2 * i + 2, :].rearrange("p t f -> p (t f)"), keep["ident"][:, :])
                        ins.then_inc(turned, 1)
                    if k:
                        m = k - 1
                        pe.wait_ge(scanned, (n - 1) * NB4 + m + 1)
                        pe.wait_ge(copied, (n - 1) * NB4 + m + 1)
                        for j in range(4):
                            ins = pe.transpose(pout[m % 2][:, P * j:P * j + P], run[m % 2][:, P * j:P * j + P], keep["ident"][:, :])
                        ins.then_inc(backed, 1)

            loop(pe, body)

        @block.scalar
        def _(act):
            act.wait_ge(loaded, 16 * 17)

            def roots(n):
                act.wait_ge(zed, n + 1)
                act.activation(hz[:, :, :], pz[:, :, :], ACT.Relu, bias=bias1[:, 0:1]).then_inc(hidden, 1)
                for k in range(4):
                    act.wait_ge(sized, 4 * n + k + 1)
                    act.activation(norm1[:, :], norm2[:, :], ACT.Sqrt).then_inc(rooted, 1)

            roots(0)

            def body(n, u, it):
                roots(n)
                for k in range(NB4):
                    act.wait_ge(backed, (n - 1) * NB4 + k + 1)
                    act.activation(out_t[:, 4 * k:4 * k + 4, :, :], pout[k % 2][:, :].rearrange("p (i h f) -> p i h f", i=4, h=2),
                                   ACT.Copy).then_inc(copied, 1)
                act.wait_ge(copied, n * NB4 + 2)
                for h in range(2):
                    act.dma_start(sums_d[h, n - 1], out_t[:, :, h, :]).then_inc(stored, 16)
                act.wait_ge(stored, n * 32)

            loop(act, body)


def sheaf_node_phase(nc, io, dram, keep):
    with phase(nc, "sn") as ph:
        agg = ph.sb("agg", [P, NC, F])
        edge_row = ph.sb("edge_row", [P, 1, F])
        across, has = ph.sb("across", [P, NC]), ph.sb("has", [P, NC])
        part, low, grown = (ph.sb(n, [P, NC, F]) for n in ("part", "low", "grown"))
        coeff = ph.sb("coeff", [P, D4])
        w = norm_scratch(ph)
        loaded, got, dv, lowered, grew, tanhed = (ph.sem(n) for n in ("loaded", "got", "dv", "lowered", "grew", "tanhed"))
        block = ph.block()

        @block.sync
        def _(sp):
            sp.dma_start(edge_row[:, 0, :], dram["sums"][HE - 1:HE, :].to_broadcast([P, F])).then_inc(loaded, 16)
            sp.dma_start(coeff[:, :], row(io["L2_gnn_epsilons"]).to_broadcast([P, D4])).then_inc(loaded, 16)

        @block.gpsimd
        def _(pool):
            for c in range(NC):
                pool.indirect_dma_start(agg[:, c, :], None, dram["sums"],
                                        bass.IndirectOffsetOnAxis(keep["last_idx"][:, c:c + 1].bitcast(U32), 0)).then_inc(got, 16)

        @block.vector
        def _(dve):
            s = Steps(dve, dv)
            s.do(dve.tensor_scalar(across[:, :], keep["first"][:, :], float(HE - 1), None, ALU.is_le))
            s.do(dve.scalar_tensor_tensor(across[:, :], keep["last"][:, :], float(HE - 1), across[:, :], ALU.is_gt, ALU.mult))
            s.do(dve.tensor_scalar(has[:, :], keep["degree"][:, :], 0.0, None, ALU.is_gt))
            dve.wait_ge(loaded, 32)
            s.do(dve.tensor_tensor(part[:, :, :], edge_row[:, :, :].to_broadcast([P, NC, F]), spread(across[:, :]), ALU.mult))
            dve.wait_ge(got, 16 * NC)
            s.do(dve.tensor_tensor(agg[:, :, :], agg[:, :, :], part[:, :, :], ALU.add))
            s.do(dve.tensor_tensor(agg[:, :, :], agg[:, :, :], spread(has[:, :]), ALU.mult))
            s.do(dve.tensor_tensor(agg[:, :, :], agg[:, :, :], keep["loops"][:, :, :], ALU.add))
            dve.tensor_scalar(low[:, :, :], agg[:, :, :], 0.0, None, ALU.min).then_inc(lowered, 1)
            s.do(dve.tensor_scalar(agg[:, :, :], agg[:, :, :], 0.0, None, ALU.max))
            dve.wait_ge(tanhed, 1)
            s.do(dve.tensor_scalar(coeff[:, :], coeff[:, :], 2.0, None, ALU.add))
            for d in range(D4):
                s.mark(dve.tensor_scalar(part[:, :, H16 * d:H16 * d + H16], keep["x"][:, :, H16 * d:H16 * d + H16],
                                         coeff[:, d:d + 1], 1.0, ALU.mult, ALU.add))
            dve.wait_ge(dv, s.n)
            s.do(dve.tensor_tensor(part[:, :, :], part[:, :, :], agg[:, :, :], ALU.subtract))
            dve.wait_ge(grew, 1)
            s.do(dve.tensor_tensor(part[:, :, :], part[:, :, :], grown[:, :, :], ALU.subtract))
            norm_vector(dve, s, w, 1, part[:, :, :], keep["x"][:, :, :])

        @block.scalar
        def _(act):
            act.wait_ge(loaded, 32)
            act.activation(coeff[:, :], coeff[:, :], ACT.Tanh).then_inc(tanhed, 1)
            act.wait_ge(lowered, 1)
            act.activation(grown[:, :, :], low[:, :, :], ACT.Exp).then_inc(grew, 1)
            norm_scalar(act, w, 1)


def attention_phase(nc, io, dram, keep, out):
    with phase(nc, "at") as ph:
        aug = F + 1
        SLOPE = 0.01
        fT = ph.sb("fT", [aug, NP])
        oT = ph.sb("oT", [aug, NP])
        v = ph.sb("v", [P, NC, aug])
        wa = ph.sb("wa", [F, 2])
        wk, wq = ph.sb("wk", [aug, 2]), ph.sb("wq", [aug, 2])
        lin_w, lin_b = ph.sb("lin_w", [P, F]), ph.sb("lin_b", [P, F])
        dst_all = ph.sb("dst_all", [P, NP])
        col = ph.sb("col", [P, NC, 2])
        kT, qT = ph.sb("kT", [2, NP]), ph.sb("qT", [2, NP])
        peaks, peak, low = ph.sb("peaks", [P, 4]), ph.sb("peak", [P, NC]), ph.sb("low", [P, NC])
        neg = ph.sb("neg", [P, NC, 2])
        mask_in = [ph.sb(f"mask{u}", [P, NP], BF16) for u in range(2)]
        sink = ph.sb("sink", [P, 4, 2 * DB], BF16)
        LG, R, LAG = 5, 5, 3
        logs = [ph.sb(f"logs{k}", [P, LG, DB]) for k in range(NC // LG)]
        rs, xs, es = ([ph.sb(f"{n}{r}", [P, DB]) for r in range(R)] for n in ("rs", "xs", "es"))
        den = ph.sb("den", [P, NC])
        cat = ph.sb("cat", [P, NC, P])
        res = ph.sb("res", [P, NC, F])
        w = norm_scratch(ph)
        pa = ph.ps("pa", [P, 7, 512])
        po = ph.ps("po", [P, 512])
        flat = pa[:, :, :].rearrange("p b n -> p (b n)")
        mask_loaded = [ph.sem(f"mask_loaded{u}") for u in range(2)]
        logs_loaded = [ph.sem(f"logs_loaded{k}") for k in range(NC // LG)]
        (loaded, turned, copied, mm, peaked, dv, lifted, scored, relued, halfway, added, exped, weighted, evac, back, done) = (
            ph.sem(n) for n in ("loaded", "turned", "copied", "mm", "peaked", "dv", "lifted", "scored", "relued", "halfway",
                                "added", "exped", "weighted", "evac", "back", "done"))
        block = ph.block()
        mask_d = dram["mask"].rearrange("(c p) s -> c p s", p=P)
        logs_d = dram["logs"].rearrange("(c p) d -> p c d", p=P)
        NG = 4
        PAIRS = [(2 * g, min(2, ND - 2 * g)) for g in range(NG)]

        @block.sync
        def _(sp):
            sp.dma_start(wa[:, 0:1], io["L3_gnn_attn_w"][0:F, :]).then_inc(loaded, 16)
            sp.dma_start(wa[:, 1:2], io["L3_gnn_attn_w"][F:2 * F, :]).then_inc(loaded, 16)
            sp.dma_start(lin_w[:, :], io["lin_T"]).then_inc(loaded, 16)
            sp.dma_start(lin_b[:, :], row(io["L3_gnn_lin_b"]).to_broadcast([P, F])).then_inc(loaded, 16)
            sp.dma_start(mask_in[0][:, :], mask_d[0]).then_inc(mask_loaded[0], 16)
            sp.dma_start(mask_in[1][:, :], mask_d[1]).then_inc(mask_loaded[1], 16)
            for k in range(NC // LG):
                sp.dma_start(logs[k][:, :, :], logs_d[:, LG * k:LG * k + LG, 0:DB]).then_inc(logs_loaded[k], 16)
            used, nxt = sp.alloc_register("masks_used_a"), sp.alloc_register("next_mask_a")
            sp.reg_mov(used, 0)
            sp.reg_mov(nxt, 1)

            def reload(u):
                sp.reg_add(used, used, NG)
                sp.reg_add(nxt, nxt, 1)
                n_used = sp.snap(used)
                sp.wait_ge(loaded, 64)
                sp.wait_ge(peaked, n_used)
                sp.dma_start(mask_in[u][:, :], mask_d[sp.snap(nxt)]).then_inc(mask_loaded[u], 16)

            with sp.Fori(0, (NC - 3) // 2):
                reload(0)
                reload(1)
            reload(0)
            adds, at = sp.alloc_register("logs_used_a"), sp.alloc_register("next_logs_a")
            sp.reg_mov(adds, R)
            sp.reg_mov(at, 0)
            with sp.Fori(0, ND - 1):
                sp.reg_add(at, at, DB)
                for k in range(NC // LG):
                    sp.reg_add(adds, adds, LG)
                    n_adds = sp.snap(adds)
                    sp.wait_ge(loaded, 64)
                    sp.wait_ge(added, n_adds)
                    sp.dma_start(logs[k][:, :, :], logs_d[:, LG * k:LG * k + LG, ds(sp.snap(at), DB)]
                                 ).then_inc(logs_loaded[k], 16)
            sp.wait_ge(lifted, 3)
            sp.dma_start(chunked(out, 0, FULL * P), keep["x"][:, 0:FULL, :]).then_inc(done, 16)
            sp.dma_start(out[FULL * P:N, :], keep["x"][0:REST, FULL, :]).then_inc(done, 16)
            sp.wait_ge(done, 32)

        @block.tensor
        def _(pe):
            for c in range(NC):
                ins = pe.transpose(flat[0:F, P * c:P * c + P], keep["x"][:, c, :], keep["ident"][:, :])
            ins.then_inc(turned, 1)
            pe.wait_ge(loaded, 64)
            pe.wait_ge(copied, 1)
            for c in range(NC):
                ins = pe.matmul(flat[:, 2 * c:2 * c + 2], fT[0:F, P * c:P * c + P], wa[:, :], start=True, stop=True)
            ins.then_inc(mm, 1)
            pe.wait_ge(copied, 2)
            for at in (1, 0):
                for b in range(ND):
                    ins = pe.matmul(pa[:, b, 0:DB], wa[:, at:at + 1].to_broadcast([F, P]), fT[0:F, DB * b:DB * b + DB],
                                    start=True, stop=True)
                ins.then_inc(mm, 1)
                if at:
                    pe.wait_ge(copied, 3)
            pe.wait_ge(lifted, 1)
            for k in range(0, NP, 512):
                m = min(512, NP - k)
                ins = pe.matmul(flat[0:2, k:k + m], wk[:, :], fT[:, k:k + m], start=True, stop=True)
            ins.then_inc(mm, 1)
            pe.wait_ge(copied, 4)
            for k in range(0, NP, 512):
                m = min(512, NP - k)
                pe.matmul(flat[0:2, k:k + m], wq[:, :], fT[:, k:k + m], start=True, stop=False)
                for c in range(k // P, (k + m) // P):
                    ins = pe.matmul(flat[0:2, P * c:P * c + P], neg[:, c, :], keep["ident"][:, :], start=False,
                                    stop=(c == (k + m) // P - 1))
            ins.then_inc(mm, 1)
            pe.wait_ge(copied, 5)
            pe.sem_inc(added, R)
            pe.sem_inc(weighted, R)
            pe.sem_inc(evac, 1)
            scores = pe.alloc_register("scores")
            pe.reg_mov(scores, 0)
            with pe.Fori(0, ND) as j:
                def weigh(c):
                    pe.wait_ge(exped, j * NC + c + 1 + R)
                    if c == 0:
                        pe.wait_ge(evac, j + 1)
                    pe.matmul(po[0:aug, 0:DB], v[:, c, :], es[c % R][:, :], start=(c == 0), stop=(c == NC - 1)
                              ).then_inc(weighted, 1)

                for c in range(NC):
                    pe.reg_add(scores, scores, 1)
                    n = pe.snap(scores)
                    pe.wait_ge(copied, 5)
                    pe.wait_ge(added, n)
                    pe.matmul(pa[:, c % R, 0:DB], kT[:, P * c:P * c + P], qT[:, ds(j * DB, DB)], start=True, stop=True
                              ).then_inc(scored, 1)
                    if c >= LAG:
                        weigh(c - LAG)
                for c in range(NC - LAG, NC):
                    weigh(c)
            pe.wait_ge(evac, ND + 1)
            for c in range(NC):
                ins = pe.transpose(pa[:, c // 7, aug * (c % 7):aug * (c % 7 + 1)], oT[:, P * c:P * c + P],
                                   keep["ident"][0:aug, 0:aug])
            ins.then_inc(back, 1)
            pe.wait_ge(lifted, 2)
            for c in range(NC):
                ins = pe.transpose(flat[:, P * c:P * c + P], cat[:, c, :], keep["ident"][:, :])
            ins.then_inc(back, 1)
            pe.wait_ge(copied, 6)
            for c in range(NC):
                ins = pe.matmul(flat[:, F * c:F * c + F], dst_all[:, P * c:P * c + P], lin_w[:, :], start=True, stop=True)
            ins.then_inc(back, 1)

        @block.vector
        def _(dve):
            dve.sem_inc(exped, R)
            s = Steps(dve, dv)
            s.mark(dve.memset(fT[F:aug, :], 1.0))
            s.mark(dve.memset(v[:, :, F:aug], 1.0))
            s.mark(dve.memset(wk[:, :], 0.0))
            s.mark(dve.memset(wq[:, :], 0.0))
            s.mark(dve.memset(neg[:, :, :], 0.0))
            s.mark(dve.memset(oT[:, ND * DB:NP], 0.0))
            dve.wait_ge(dv, 6)
            s.mark(dve.memset(wk[F:aug, 1:2], 1.0))
            s.mark(dve.memset(wq[F:aug, 0:1], 1.0))
            s.mark(dve.tensor_copy(v[:, :, 0:F], keep["x"][:, :, :]))
            dve.wait_ge(loaded, 64)
            s.mark(dve.tensor_scalar(wk[0:F, 0:1], wa[:, 0:1], SLOPE, None, ALU.mult))
            s.mark(dve.tensor_scalar(wq[0:F, 1:2], wa[:, 1:2], SLOPE, None, ALU.mult))
            dve.wait_ge(turned, 1)
            dve.tensor_copy(fT[0:F, :], flat[0:F, 0:NP]).then_inc(copied, 1)
            dve.wait_ge(mm, 1)
            dve.tensor_copy(col[:, :, :], flat[:, 0:2 * NC].rearrange("p (c k) -> p c k", k=2)).then_inc(copied, 1)
            dve.wait_ge(mm, 2)
            dve.tensor_copy(dst_all[:, 0:ND * DB].rearrange("p (b n) -> p b n", n=DB), pa[:, :, 0:DB]).then_inc(copied, 1)
            dve.wait_ge(mm, 3)
            base = s.n
            turns = [dve.alloc_register(f"mask_turns{u}") for u in range(2)]
            for r in turns:
                dve.reg_mov(r, 0)

            def chunk_peak(c, u):
                dve.reg_add(turns[u], turns[u], 16)
                now = dve.snap(turns[u])
                dve.wait_ge(copied, 3)
                dve.wait_ge(mask_loaded[u], now)
                for gi, (b0, nb) in enumerate(PAIRS):
                    dve.tensor_tensor_reduce(
                        sink[:, gi, 0:nb * DB].rearrange("p (b n) -> p b n", n=DB), pa[:, b0:b0 + nb, 0:DB],
                        mask_in[u][:, b0 * DB:(b0 + nb) * DB].rearrange("p (b n) -> p b n", n=DB),
                        1.0, -3e38, ALU.add, ALU.max, peaks[:, gi:gi + 1]).then_inc(peaked, 1)
                dve.wait_ge(peaked, c * NG + NG)
                dve.tensor_reduce(peak[:, ds(c, 1)], peaks[:, :], AX.X, ALU.max).then_inc(dv, 1)
                dve.wait_ge(dv, c + base + 1)

            with dve.Fori(0, NC // 2) as it:
                for u in range(2):
                    chunk_peak(it * 2 + u, u)
            chunk_peak(NC - 1, 0)
            s.n += NC
            s.do(dve.tensor_scalar(peak[:, :], peak[:, :], -1e29, None, ALU.max))
            s.do(dve.tensor_tensor(peak[:, :], peak[:, :], col[:, :, 1], ALU.add))
            s.do(dve.tensor_scalar(low[:, :], peak[:, :], SLOPE, None, ALU.mult))
            s.do(dve.tensor_tensor(peak[:, :], peak[:, :], low[:, :], ALU.max))
            dve.tensor_scalar(neg[:, :, 1], peak[:, :], -1.0, None, ALU.mult).then_inc(lifted, 1)
            dve.wait_ge(mm, 4)
            dve.tensor_copy(kT[:, :], flat[0:2, 0:NP]).then_inc(copied, 1)
            dve.wait_ge(mm, 5)
            dve.tensor_copy(qT[:, :], flat[0:2, 0:NP]).then_inc(copied, 1)
            with dve.Fori(0, ND) as j:
                for c in range(NC):
                    if c % LG == 0:
                        dve.wait_ge(logs_loaded[c // LG], j * 16 + 16)
                    dve.wait_ge(exped, j * NC + c + 1)
                    dve.wait_ge(relued, j * NC + c + 1)
                    dve.wait_ge(scored, j * NC + c + 1)
                    dve.scalar_tensor_tensor(xs[c % R][:, :], rs[c % R][:, :], 1.0 - SLOPE, pa[:, c % R, 0:DB],
                                             ALU.mult, ALU.add).then_inc(halfway, 1)
                    dve.wait_ge(halfway, j * NC + c + 1)
                    dve.tensor_tensor(xs[c % R][:, :], xs[c % R][:, :], logs[c // LG][:, c % LG, :], ALU.add
                                      ).then_inc(added, 1)
            dve.wait_ge(back, 1)
            s.mark(dve.tensor_copy(cat[:, :, 0:F], keep["x"][:, :, :]))
            for b in range(4):
                n = min(7, NC - 7 * b)
                s.mark(dve.tensor_scalar(den[:, 7 * b:7 * b + n],
                                         pa[:, b, 0:aug * n].rearrange("p (c f) -> p c f", f=aug)[:, :, F], 1e-30, None, ALU.max))
            dve.wait_ge(dv, s.n)
            s.do(dve.reciprocal(den[:, :], den[:, :]))
            for b in range(4):
                n = min(7, NC - 7 * b)
                ins = dve.tensor_tensor(cat[:, 7 * b:7 * b + n, F:P],
                                        pa[:, b, 0:aug * n].rearrange("p (c f) -> p c f", f=aug)[:, :, 0:F],
                                        den[:, 7 * b:7 * b + n].rearrange("p (c o) -> p c o", o=1).to_broadcast([P, n, F]),
                                        ALU.mult)
            ins.then_inc(lifted, 1)
            dve.wait_ge(back, 2)
            dve.tensor_copy(dst_all[:, :], flat[:, 0:NP]).then_inc(copied, 1)
            dve.wait_ge(back, 3)
            s.do(dve.tensor_tensor(res[:, :, :], flat[:, 0:NC * F].rearrange("p (c f) -> p c f", f=F),
                                   lin_b[:, :].rearrange("p (o f) -> p o f", o=1).to_broadcast([P, NC, F]), ALU.add))
            s.do(dve.tensor_scalar(res[:, :, :], res[:, :, :], 0.0, None, ALU.max))
            s.do(dve.tensor_tensor(res[:, :, :], res[:, :, :], keep["x"][:, :, :], ALU.add))
            norm_vector(dve, s, w, 1, res[:, :, :], keep["x"][:, :, :])
            dve.wait_ge(dv, s.n)
            dve.sem_inc(lifted, 1)

        @block.scalar
        def _(act):
            act.wait_ge(copied, 5)
            act.wait_ge(lifted, 1)
            relus = act.alloc_register("relus")
            act.reg_mov(relus, 0)
            with act.Fori(0, ND) as j:
                def relu(c):
                    act.reg_add(relus, relus, 1)
                    n = act.snap(relus)
                    act.wait_ge(lifted, 1)
                    act.wait_ge(added, n)
                    act.activation(rs[c % R][:, :], dst_all[:, ds(j * DB, DB)], ACT.Relu, bias=col[:, c, 0:1]
                                   ).then_inc(relued, 1)

                relu(0)
                relu(1)
                for c in range(NC):
                    if c + 2 < NC:
                        relu(c + 2)
                    act.wait_ge(added, j * NC + c + 1 + R)
                    act.wait_ge(weighted, j * NC + c + 1)
                    act.activation(es[c % R][:, :], xs[c % R][:, :], ACT.Exp).then_inc(exped, 1)
                act.wait_ge(weighted, j * NC + NC + R)
                act.activation(oT[:, ds(j * DB, DB)], po[0:aug, 0:DB], ACT.Copy).then_inc(evac, 1)
            norm_scalar(act, w, 1)


def program(nc, io, out):
    def scratch(name, shape, dt=F32):
        return nc.dram_tensor(name, shape, dt, kind="Internal").ap()

    dram = {
        "table_src": scratch("table_src", (NP, M)), "table_dst": scratch("table_dst", (NP, M)),
        "counts": scratch("counts", (COUNTS + P, 1)), "runs": scratch("runs", (EP, 2 * M)),
        "mask": scratch("mask", (NP, NP), BF16), "logs": scratch("logs", (NP, NP)),
        "sheaf_src": scratch("sheaf_src", (NP, WS)), "sheaf_dst": scratch("sheaf_dst", (NP, WD)),
        "sums": scratch("sums", (EP, F)),
    }
    with ExitStack() as ctx:
        def sb(name, shape, dt=F32):
            return ctx.enter_context(nc.sbuf_tensor(name, shape, dt))

        keep = {n: sb(n, [P, NC]) for n in ("nid", "first", "last", "degree", "out_deg")}
        keep.update({n: sb(n, [P, T], I32) for n in ("src", "dst")})
        keep["last_idx"] = sb("last_idx", [P, NC], I32)
        keep["ident"] = sb("ident", [P, P])
        keep["x"] = sb("x", [P, NC, F])
        with ExitStack() as ctx:
            keep["key"], keep["dump"], keep["tri"] = sb("key", [P, T]), sb("dump", [P, 1]), sb("tri", [P, P])
            setup_phase(nc, io, dram, keep)
            message_phase(nc, io, dram, keep)
        node_phase(nc, io, dram, keep)
        dense_phase(nc, io, dram, keep)
        with ExitStack() as ctx:
            keep["h"] = sb("h", [P, NC, F])
            for l in range(4):
                conv_phase(nc, io, dram, keep, l)
        with ExitStack() as ctx:
            keep["src_tab"], keep["dst_tab"] = sb("src_tab", [P, NC, WS]), sb("dst_tab", [P, NC, WD])
            keep["loops"] = sb("loops", [P, NC, F])
            sheaf_tables_phase(nc, io, dram, keep)
            sheaf_phase(nc, io, dram, keep)
            sheaf_node_phase(nc, io, dram, keep)
        attention_phase(nc, io, dram, keep, out)


SHAPE = (N, F)


def kernel(**inputs):
    import concourse.bacc as _bacc
    from concourse.bass_utils import run_bass_kernel_spmd as _run

    nc = _bacc.Bacc("TRN2", target_bir_lowering=False, num_devices=1)
    a = {k: np.ascontiguousarray(v) for k, v in inputs.items()}
    x, src, dst, attr = (a[k] for k in ("x", "src", "dst", "edge_attr_32"))
    node = np.full(EP, PAD_NODE, dst.dtype)
    node[:E] = dst
    of = np.full(EP, PAD_NODE, src.dtype)
    of[:E] = src
    feats = np.zeros((EP, M), attr.dtype)
    feats[:E] = attr
    arrays = {k: v for k, v in a.items() if k[0] == "L"}
    arrays["x"] = x
    arrays["xT"] = x.T
    arrays["src_pm"] = of.reshape(T, P).T
    arrays["dst_pm"] = node.reshape(T, P).T
    arrays["dst_tiles"] = node.reshape(T, P)
    arrays["dst_last"] = node.reshape(T, P)[:, P - 1]
    seq = np.full((4, QE + 1), -1, dst.dtype)
    seq[:, 1:] = node.reshape(4, QE)
    arrays["dst_seq"] = seq
    half = np.full((2, 2 * QE + 1), -1, dst.dtype)
    half[:, 1:] = node.reshape(2, 2 * QE)
    arrays["dst_half"] = half
    arrays["edge_T"] = feats.reshape(4, QE, M).transpose(0, 2, 1).reshape(4 * M, QE)
    arrays["mlp1_T"] = a["L2_gnn_mlp1_w"].T
    order = [0, 1, 3, 2, 4, 5]
    arrays["mlp2_T"] = a["L2_gnn_mlp2_w"][order].T
    arrays["mlp2_b"] = a["L2_gnn_mlp2_b"][order]
    arrays["lin_T"] = a["L3_gnn_lin_w"].T
    arrays = {k: np.ascontiguousarray(v) for k, v in arrays.items()}
    io = {k: nc.dram_tensor(f"in_{k}", v.shape, mybir.dt.from_np(v.dtype), kind="ExternalInput").ap()
          for k, v in arrays.items()}
    out = nc.dram_tensor("out", SHAPE, F32, kind="ExternalOutput").ap()
    program(nc, io, out)
    r = _run(nc, [{f"in_{k}": v for k, v in arrays.items()}], core_ids=[0])
    return r.results[0]["out"]
```

```python
from contextlib import ExitStack, contextmanager

import numpy as np

import concourse.bass as bass
from concourse import mybir
from concourse.alu_op_type import AluOpType as ALU

F32 = mybir.dt.float32
I32 = mybir.dt.int32
U32 = mybir.dt.uint32
BF16 = mybir.dt.bfloat16
ACT = mybir.ActivationFunctionType
AX = mybir.AxisListType
ds = bass.ds

P = 128
N = 3125
F = 64
M = 32
NC = -(-N // P)
NP = NC * P
FULL = N // P
REST = N - FULL * P
E = 100000
BLK = 512
NB = 50
QE = NB * BLK
EP = 4 * QE
T = EP // P
QT = T // 4
ST = BLK // P
PAD_NODE = N
COUNTS = NP * NP
DB = 448
ND = 7
BIG = 1e38
OFTEN = 4.0 * P * 2
OFF = 1e30
LN_EPS = 1e-5
assert ND * DB >= N and EP >= E and ND * DB <= NP


class Steps:

    def __init__(self, eng, sem, base=0):
        self.eng, self.sem, self.base, self.n = eng, sem, base, 0

    def mark(self, ins):
        ins.then_inc(self.sem, 1)
        self.n += 1

    def do(self, ins):
        self.mark(ins)
        self.eng.wait_ge(self.sem, self.base + self.n)


class Phase:

    def __init__(self, nc, ctx, name):
        self.nc, self.ctx, self.name = nc, ctx, name
        self.sems = []

    def sb(self, name, shape, dt=F32):
        return self.ctx.enter_context(self.nc.sbuf_tensor(f"{self.name}_{name}", shape, dt))

    def ps(self, name, shape, dt=F32):
        return self.ctx.enter_context(self.nc.psum_tensor(f"{self.name}_{name}", shape, dt))

    def sem(self, name):
        self.sems.append(self.nc.alloc_semaphore(f"{self.name}_{name}"))
        return self.sems[-1]

    def block(self):
        return self.ctx.enter_context(self.nc.Block())


@contextmanager
def phase(nc, name):
    with ExitStack() as ctx:
        ph = Phase(nc, ctx, name)
        yield ph
    nc.clear_and_free_semaphores(ph.sems)
    nc.all_engine_barrier()


def chunked(dram, lo=0, hi=NP):
    return dram[lo:hi, :].rearrange("(c p) f -> p c f", p=P)


def column(vec):
    return vec.rearrange("(p o) -> p o", o=1)


def row(vec):
    return vec.rearrange("(o n) -> o n", o=1)


def spread_to_edges(pool, dram, keep, rows, heads, stored, spread):
    for c in range(NC):
        pool.indirect_dma_start(dram["spread"], bass.IndirectOffsetOnAxis(keep["first_idx"][:, c:c + 1].bitcast(U32), 0),
                                rows[:, c, :], None).then_inc(spread, 16)
    pool.wait_ge(stored, 32)
    pool.indirect_dma_start(heads[:, :], None, dram["table_dst"],
                            bass.IndirectOffsetOnAxis(keep["head_idx"][:, 0:1].bitcast(U32), 0)).then_inc(spread, 16)
    pool.wait_ge(spread, 16 * (NC + 1))
    pool.dma_start(dram["spread"][0:EP, :].rearrange("(q e) f -> q e f", q=4)[:, 0, :], heads[0:4, :]).then_inc(spread, 16)
    pool.wait_ge(spread, 16 * (NC + 2))


def setup_phase(nc, io, dram, keep):
    with phase(nc, "su") as ph:
        xT = ph.sb("xT", [F, NP])
        wab = ph.sb("wab", [F, 2 * M])
        proj = ph.sb("proj", [P, NC, M])
        zeros = ph.sb("zeros", [P, 4000])
        tile_last_i = ph.sb("tile_last_i", [P, T], I32)
        tile_last = ph.sb("tile_last", [P, T])
        hits = ph.sb("hits", [P, T])
        bound_tile = ph.sb("bound_tile", [P, 2, NC])
        bound_idx = ph.sb("bound_idx", [P, 2, NC], I32)
        rows = ph.sb("rows", [P, 2, NC, P], I32)
        below = ph.sb("below", [P, 2, NC, P])
        in_row = ph.sb("in_row", [P, 2, NC])
        nid_i = ph.sb("nid_i", [P, NC], I32)
        dump_i = ph.sb("dump_i", [P, 4], I32)
        dst_rows = ph.sb("dst_rows", [P, NC, M])
        heads = ph.sb("heads", [P, M])
        away, has = ph.sb("away", [P, NC]), ph.sb("has", [P, NC])
        pp = ph.ps("pp", [P, 4, 512])
        cleared, loaded, consts, projected = (ph.sem(n) for n in ("cleared", "loaded", "consts", "projected"))
        last_in, zeroed, got_rows, idx_ready, copied = (ph.sem(n) for n in ("last_in", "zeroed", "got_rows", "idx_ready", "copied"))
        stored, dv, po, first_ready, spread = (ph.sem(n) for n in ("stored", "dv", "po", "first_ready", "spread"))
        spread_zero = ph.sem("spread_zero")
        block = ph.block()

        @block.sync
        def _(sp):
            sp.dma_start(tile_last_i[:, :], row(io["dst_last"]).to_broadcast([P, T])).then_inc(last_in, 16)
            sp.dma_start(wab[:, 0:M], io["L0_gnn_W1"][0:F, :]).then_inc(loaded, 16)
            sp.dma_start(wab[:, M:2 * M], io["L0_gnn_W1"][F:2 * F, :]).then_inc(loaded, 16)
            sp.dma_start(keep["src"][:, :], io["src_pm"]).then_inc(loaded, 16)
            sp.dma_start(keep["dst"][:, :], io["dst_pm"]).then_inc(loaded, 16)
            sp.dma_start(keep["head_idx"][:, :], column(io["dst_heads"])).then_inc(loaded, 16)
            sp.wait_ge(cleared, 2)
            sp.dma_start(xT[:, 0:N], io["xT"]).then_inc(loaded, 16)
            sp.dma_start(keep["x"][:, 0:FULL, :], chunked(io["x"], 0, FULL * P)).then_inc(loaded, 16)
            sp.dma_start(keep["x"][0:REST, FULL, :], io["x"][FULL * P:N, :]).then_inc(loaded, 16)
            sp.wait_ge(copied, 1)
            sp.dma_start(chunked(dram["table_src"]), proj[:, :, :]).then_inc(stored, 16)
            sp.dma_start(chunked(dram["table_dst"]), dst_rows[:, :, :]).then_inc(stored, 16)
            sp.wait_ge(stored, 32)
            sp.wait_ge(loaded, 16 * 8)

        @block.scalar
        def _(act):
            act.wait_ge(cleared, 3)
            counts = dram["counts"][0:COUNTS, :].rearrange("(p n) o -> p (n o)", p=P)
            for k in range(COUNTS // P // 4000):
                act.dma_start(counts[:, 4000 * k:4000 * (k + 1)], zeros[:, :]).then_inc(zeroed, 16)
            act.dma_start(dram["counts"][COUNTS:COUNTS + 4 * P, :].rearrange("(p q) o -> p (q o)", p=P), zeros[:, 0:4]).then_inc(zeroed, 16)
            spread_d = dram["spread"][0:EP, :].rearrange("(p n) f -> p (n f)", p=P)
            for k in range(EP * M // P // 3200):
                act.dma_start(spread_d[:, 3200 * k:3200 * (k + 1)], zeros[:, 0:3200]).then_inc(spread_zero, 16)
            act.wait_ge(zeroed, 16 * (COUNTS // P // 4000 + 1))

        @block.gpsimd
        def _(pool):
            s = Steps(pool, po)
            pool.memset(keep["ident"][:, :], 0.0).then_inc(po, 1)
            pool.memset(keep["earlier"][:, 0:4 * P], OFTEN).then_inc(po, 1)
            pool.memset(keep["earlier"][:, 4 * P:7 * P], 1.0).then_inc(po, 1)
            s.n = 3
            pool.wait_ge(po, 3)
            s.mark(pool.affine_select(out=keep["ident"][:, :], in_=keep["ident"][:, :], compare_op=ALU.not_equal,
                                      fill=1.0, base=0, pattern=[[-1, P]], channel_multiplier=1))
            tri = keep["earlier"][:, 3 * P:4 * P]
            s.mark(pool.affine_select(out=tri, in_=tri, compare_op=ALU.is_gt,
                                      fill=1.0, base=0, pattern=[[-1, P]], channel_multiplier=1))
            s.mark(pool.iota(nid_i[:, :], [[P, NC]], 0, 1))
            s.mark(pool.iota(dump_i[:, :], [[P, 4]], COUNTS, 1))
            pool.wait_ge(idx_ready, 1)
            for k in range(2):
                for c in range(NC):
                    pool.indirect_dma_start(rows[:, k, c, :], None, io["dst_tiles"],
                                            bass.IndirectOffsetOnAxis(bound_idx[:, k, c:c + 1].bitcast(U32), 0)
                                            ).then_inc(got_rows, 16)
            pool.wait_ge(got_rows, 16 * 2 * NC)
            pool.wait_ge(spread_zero, 16 * (EP * M // P // 3200))
            pool.wait_ge(first_ready, 1)
            spread_to_edges(pool, dram, keep, dst_rows, heads, stored, spread)

        @block.tensor
        def _(pe):
            pe.wait_ge(loaded, 16 * 8)
            for c in range(NC):
                ins = pe.matmul(pp[:, c // 8, F * (c % 8):F * (c % 8 + 1)], xT[:, P * c:P * c + P], wab[:, :],
                                start=True, stop=True)
            ins.then_inc(projected, 1)

        @block.vector
        def _(dve):
            dve.memset(xT[:, :], 0.0).then_inc(cleared, 1)
            dve.memset(keep["x"][:, :, :], 0.0).then_inc(cleared, 1)
            dve.memset(zeros[:, :], 0.0).then_inc(cleared, 1)
            s = Steps(dve, dv)
            dve.wait_ge(last_in, 16)
            dve.wait_ge(po, 7)
            s.mark(dve.tensor_copy(tile_last[:, :], tile_last_i[:, :]))
            s.mark(dve.tensor_copy(keep["dump"][:, :], dump_i[:, :]))
            s.do(dve.tensor_copy(keep["nid"][:, :], nid_i[:, :]))
            for k, op in enumerate((ALU.is_lt, ALU.is_le)):
                for c in range(NC):
                    s.do(dve.tensor_scalar(hits[:, :], tile_last[:, :], keep["nid"][:, c:c + 1], None, op, ALU.add,
                                           accum_out=bound_tile[:, k, c:c + 1]))
            s.do(dve.tensor_scalar(bound_tile[:, :, :], bound_tile[:, :, :], float(T - 1), None, ALU.min))
            dve.tensor_copy(bound_idx[:, :, :], bound_tile[:, :, :]).then_inc(idx_ready, 1)
            dve.wait_ge(loaded, 16 * 8)
            s.mark(dve.scalar_tensor_tensor(keep["key"][:, :], keep["dst"][:, :], float(NP), keep["src"][:, :],
                                            ALU.mult, ALU.add))
            dve.wait_ge(projected, 1)
            for b in range(4):
                w = min(8, NC - 8 * b)
                of = pp[:, b, 0:F * w].rearrange("p (c f) -> p c f", f=F)
                dve.tensor_copy(dst_rows[:, 8 * b:8 * b + w, :], of[:, :, M:2 * M])
                ins = dve.tensor_copy(proj[:, 8 * b:8 * b + w, :], of[:, :, 0:M])
            ins.then_inc(copied, 1)
            dve.wait_ge(got_rows, 16 * 2 * NC)
            for k, op in enumerate((ALU.is_lt, ALU.is_le)):
                s.mark(dve.tensor_tensor(below[:, k, :, :], rows[:, k, :, :],
                                         keep["nid"][:, :].rearrange("p (c o) -> p c o", o=1).to_broadcast([P, NC, P]), op))
            dve.wait_ge(dv, s.n)
            for k in range(2):
                s.mark(dve.tensor_reduce(in_row[:, k, :], below[:, k, :, :], AX.X, ALU.add))
            dve.wait_ge(dv, s.n)
            for k, out in enumerate((keep["first"], keep["last"])):
                s.mark(dve.scalar_tensor_tensor(out[:, :], bound_tile[:, k, :], float(P), in_row[:, k, :],
                                                ALU.mult, ALU.add))
            dve.wait_ge(dv, s.n)
            s.mark(dve.tensor_tensor(keep["degree"][:, :], keep["last"][:, :], keep["first"][:, :], ALU.subtract))
            s.do(dve.tensor_scalar(keep["last"][:, :], keep["last"][:, :], -1.0, None, ALU.add))
            s.mark(dve.tensor_scalar(keep["last_idx"][:, :], keep["last"][:, :], 0.0, None, ALU.max))
            s.mark(dve.tensor_scalar(away[:, :], keep["nid"][:, :], float(EP), None, ALU.add))
            s.do(dve.tensor_scalar(has[:, :], keep["degree"][:, :], 0.0, None, ALU.is_gt))
            s.do(dve.tensor_tensor(bound_tile[:, 0, :], keep["first"][:, :], away[:, :], ALU.subtract))
            s.do(dve.tensor_tensor(bound_tile[:, 0, :], bound_tile[:, 0, :], has[:, :], ALU.mult))
            dve.tensor_tensor(keep["first_idx"][:, :], bound_tile[:, 0, :], away[:, :], ALU.add).then_inc(first_ready, 1)


def message_phase(nc, io, dram, keep):
    with phase(nc, "ms") as ph:
        w1 = ph.sb("w1", [P, P])
        w2 = ph.sb("w2", [P, P])
        w3 = ph.sb("w3", [P, P])
        b1 = ph.sb("b1", [P, 1])
        b2 = ph.sb("b2", [P, 1])
        b3 = ph.sb("b3", [P, 1])
        attr = [ph.sb(f"attr{u}", [P, BLK]) for u in range(2)]
        seq = [ph.sb(f"seq{u}", [P, BLK + 1], I32) for u in range(2)]
        st_src = [ph.sb(f"st_src{u}", [P, ST, 4], I32) for u in range(2)]
        st_key = [ph.sb(f"st_key{u}", [P, ST, 4]) for u in range(2)]
        place = [ph.sb(f"place{u}", [P, ST * 4], I32) for u in range(2)]
        mult = [ph.sb(f"mult{u}", [P, ST * 4]) for u in range(2)]
        lead = ph.sb("lead", [P, ST * 4])
        moved = ph.sb("moved", [P, ST * 4])
        same = ph.sb("same", [P, 4, 4 * P], BF16)
        got_s = [ph.sb(f"got_s{u}", [P, ST, 4, M]) for u in range(2)]
        first_rows = [ph.sb(f"first_rows{u}", [P, ST, 4, M]) for u in range(2)]
        of_dst = [ph.sb(f"of_dst{u}", [P, BLK]) for u in range(2)]
        h1 = ph.sb("h1", [P, BLK])
        h2 = ph.sb("h2", [P, BLK])
        h3 = ph.sb("h3", [P, BLK])
        cont = [ph.sb(f"cont{u}", [P, BLK]) for u in range(2)]
        gate = [ph.sb(f"gate{u}", [P, BLK]) for u in range(2)]
        run_sum = [ph.sb(f"run_sum{u}", [P, BLK]) for u in range(2)]
        run_max = [ph.sb(f"run_max{u}", [P, BLK]) for u in range(2)]
        out_t = ph.sb("out_t", [P, ST, 4, 2 * M])
        p1, p2, p3, pts, ptm, pd = (ph.ps(n, [P, BLK]) for n in ("p1", "p2", "p3", "pts", "ptm", "pd"))
        pkey = [ph.ps(f"pkey{u}", [P, 4, P]) for u in range(2)]
        wz, weights, staged, keyed, keyfree, placed = (ph.sem(n) for n in ("wz", "weights", "staged", "keyed", "keyfree", "placed"))
        multiplied, mm1, mm2, mm3, act1, act2, act3 = (ph.sem(n) for n in ("multiplied", "mm1", "mm2", "mm3", "act1", "act2", "act3"))
        scanned, turned, masked, turned_out, out_st = (ph.sem(n) for n in ("scanned", "turned", "masked", "turned_out", "out_st"))
        counted, dv, ds0, rows_turned, spread = (ph.sem(n) for n in ("counted", "dv", "ds0", "rows_turned", "spread"))
        rows_in = [ph.sem(f"rows_in{u}") for u in range(2)]
        attr_in = [ph.sem(f"attr_in{u}") for u in range(2)]
        seq_in = [ph.sem(f"seq_in{u}") for u in range(2)]
        got = [[ph.sem(f"got{u}_{i}") for i in range(ST)] for u in range(2)]
        block = ph.block()

        attr_d = io["edge_T"]
        seq_d = io["dst_seq"]
        spread_d = dram["spread"][0:EP, :].rearrange("(q b i p) f -> q b p i f", q=4, b=NB, i=ST)
        quarter = dram["runs"].rearrange("(q b i p) f -> q b p i f", q=4, b=NB, i=ST)

        def loop(eng, body, count=NB // 2):
            with eng.Fori(0, count - 1) as it:
                body(it, False)
            body(count - 1, True)

        @block.sync
        def _(sp):
            sp.wait_ge(wz, 1)
            k = 0
            for q in range(4):
                lo = M * q
                for w, b, ww, bb in ((w1, b1, io["L0_gnn_W1"][2 * F:2 * F + M, :], "L0_gnn_b1"),
                                     (w2, b2, io["L0_gnn_W2"], "L0_gnn_b2"), (w3, b3, io["L0_gnn_W3"], "L0_gnn_b3")):
                    sp.dma_start(w[lo:lo + M, lo:lo + M], ww).then_inc(weights, 16)
                    sp.dma_start(b[lo:lo + M, :], column(io[bb])).then_inc(weights, 16)
                    k += 2
            assert k == 24

            def load(b, at, u):
                for q in range(4):
                    sp.dma_start(first_rows[u][:, :, q, :], spread_d[q, b]).then_inc(rows_in[u], 16)
                sp.dma_start(attr[u][:, :], attr_d[:, ds(at, BLK)]).then_inc(attr_in[u], 16)
                for q in range(4):
                    sp.dma_start(seq[u][M * q:M * q + M, :],
                                 seq_d[q:q + 1, ds(at, BLK + 1)].to_broadcast([M, BLK + 1])).then_inc(seq_in[u], 16)

            load(0, 0, 0)
            load(1, BLK, 1)
            at, done = sp.alloc_register("edges_loaded"), sp.alloc_register("blocks_done")
            sp.reg_mov(at, BLK)
            sp.reg_mov(done, 0)
            with sp.Fori(0, NB // 2 - 1):
                for u in range(2):
                    sp.reg_add(at, at, BLK)
                    sp.reg_add(done, done, 1)
                    blocks = sp.snap(done)
                    sp.wait_ge(wz, 1)
                    sp.wait_ge(multiplied, blocks)
                    sp.wait_ge(masked, blocks)
                    sp.wait_ge(rows_turned, blocks)
                    load(blocks + 1, sp.snap(at), u)
            sp.wait_ge(weights, 16 * 24)

        @block.gpsimd
        def _(pool):
            turn = pool.alloc_register("block_turn")
            sent = pool.alloc_register("tiles_counted")
            pool.reg_mov(turn, 0)
            pool.reg_mov(sent, 0)

            def body(it, last):
                for u in range(2):
                    pool.reg_add(turn, turn, 1)
                    now = pool.snap(turn)
                    pool.wait_ge(ds0, 1)
                    pool.wait_ge(placed, now)
                    pool.wait_ge(mm1, now)
                    for i in range(ST):
                        for q in range(4):
                            j = 4 * i + q
                            pool.indirect_dma_start(
                                dram["counts"], bass.IndirectOffsetOnAxis(place[u][:, j:j + 1].bitcast(U32), 0),
                                mult[u][:, j:j + 1], None, compute_op=ALU.add).then_inc(counted, 16)
                        for q in range(4):
                            pool.indirect_dma_start(
                                got_s[u][:, i, q, :], None, dram["table_src"],
                                bass.IndirectOffsetOnAxis(st_src[u][:, i, q:q + 1].bitcast(U32), 0)).then_inc(got[u][i], 16)
                        pool.reg_add(sent, sent, 64)
                        so_far = pool.snap(sent)
                        pool.wait_ge(ds0, 1)
                        pool.wait_ge(counted, so_far)

            with pool.Fori(0, NB // 2) as it:
                body(it, False)

        @block.vector
        def _(dve):
            for w in (w1, w2, w3):
                ins = dve.memset(w[:, :], 0.0)
            ins.then_inc(wz, 1)
            dve.memset(run_sum[1][:, :], 0.0)
            dve.memset(of_dst[1][:, :], 0.0)
            dve.memset(run_max[1][:, :], 0.0).then_inc(ds0, 1)
            dve.wait_ge(ds0, 1)

            def stage(b, u):
                for st, of in ((st_src, "src"), (st_key, "key")):
                    ins = dve.tensor_copy(st[u][:, :, :].rearrange("p i q -> p q i"),
                                          keep[of][:, :].rearrange("p (q t) -> p q t", q=4)[:, :, ds(b * ST, ST)])
                ins.then_inc(staged, 1)

            def places(b, u, s):
                dve.wait_ge(staged, b + 1)
                for i in range(ST):
                    dve.wait_ge(keyed, ST * b + i + 1)
                    for q in range(4):
                        ins = dve.scalar_tensor_tensor(
                            same[:, q, :], pkey[i % 2][:, :, :].rearrange("p q n -> p (q n)"), st_key[u][:, i, q:q + 1],
                            keep["earlier"][:, (3 - q) * P:(7 - q) * P], ALU.is_equal, ALU.mult,
                            accum_out=mult[u][:, 4 * i + q:4 * i + q + 1])
                    s.do(ins)
                    dve.sem_inc(keyfree, 1)
                keys, spare = st_key[u][:, :, :], keep["dump"][:, :].rearrange("p (o q) -> p o q", o=1).to_broadcast([P, ST, 4])
                far = moved[:, :].rearrange("p (i q) -> p i q", q=4)
                s.mark(dve.tensor_scalar(lead[:, :], mult[u][:, :], OFTEN, None, ALU.is_lt))
                s.do(dve.tensor_tensor(far, keys, spare, ALU.subtract))
                s.do(dve.tensor_tensor(moved[:, :], moved[:, :], lead[:, :], ALU.mult))
                dve.tensor_tensor(place[u][:, :].rearrange("p (i q) -> p i q", q=4), far, spare, ALU.add).then_inc(placed, 1)

            def along(b, u, s, it):
                dve.wait_ge(seq_in[u], it * 64 + 64)
                s.do(dve.tensor_tensor(cont[u][:, :], seq[u][:, 1:BLK + 1], seq[u][:, 0:BLK], ALU.is_equal))
                s.do(dve.tensor_scalar(gate[u][:, :], cont[u][:, :], BIG, -BIG, ALU.mult, ALU.add))
                dve.sem_inc(masked, 1)
                dve.wait_ge(rows_turned, b + 1)
                dve.tensor_tensor_scan(of_dst[u][:, :], cont[u][:, :], pd[:, :], of_dst[1 - u][:, BLK - 1:BLK],
                                       ALU.mult, ALU.add).then_inc(spread, 1)
                dve.wait_ge(spread, b + 1)

            def scans(b, u):
                dve.wait_ge(act3, b + 1)
                dve.tensor_tensor_scan(run_sum[u][:, :], cont[u][:, :], h3[:, :], run_sum[1 - u][:, BLK - 1:BLK],
                                       ALU.mult, ALU.add)
                dve.tensor_tensor_scan(run_max[u][:, :], gate[u][:, :], h3[:, :], run_max[1 - u][:, BLK - 1:BLK],
                                       ALU.add, ALU.max).then_inc(scanned, 1)
                dve.wait_ge(scanned, b + 1)

            PER = ST + 3 + 2
            stage(0, 0)
            s0 = Steps(dve, dv)
            places(0, 0, s0)
            along(0, 0, s0, 0)
            assert s0.n == PER

            def body(it, last):
                for u in range(2):
                    b = it * 2 + u
                    if not (last and u == 1):
                        s = Steps(dve, dv, (b + 1) * PER)
                        stage(b + 1, 1 - u)
                        places(b + 1, 1 - u, s)
                        along(b + 1, 1 - u, s, it + u)
                        assert s.n == PER
                    scans(b, u)
                    dve.wait_ge(counted, (b + 1) * 16 * 4 * ST)

            loop(dve, body)

        @block.tensor
        def _(pe):
            pe.sem_inc(mm1, 2)
            pe.wait_ge(weights, 16 * 24)

            def keys(b, u):
                pe.wait_ge(staged, b + 1)
                for i in range(ST):
                    pe.wait_ge(keyfree, ST * b + i + 1)
                    for q in range(4):
                        ins = pe.matmul(pkey[i % 2][:, q, :], st_key[u][:, i, q:q + 1].to_broadcast([P, P]),
                                        keep["ident"][:, :], start=True, stop=True)
                    ins.then_inc(keyed, 1)

            def turn_rows(b, u, it):
                pe.wait_ge(rows_in[u], it * 64 + 64)
                for i in range(ST):
                    ins = pe.transpose(pd[:, P * i:P * i + P], first_rows[u][:, i, :, :].rearrange("p q m -> p (q m)"),
                                       keep["ident"][:, :])
                ins.then_inc(rows_turned, 1)

            pe.sem_inc(keyfree, 2)
            keys(0, 0)
            turn_rows(0, 0, 0)

            def body(it, last):
                for u in range(2):
                    b = it * 2 + u
                    if not (last and u == 1):
                        keys(b + 1, 1 - u)
                        pe.wait_ge(spread, b + 1)
                        turn_rows(b + 1, 1 - u, it + u)
                    pe.wait_ge(attr_in[u], it * 16 + 16)
                    pe.matmul(p1[:, :], w1[:, :], attr[u][:, :], start=True, stop=False).then_inc(multiplied, 1)
                    pe.wait_ge(spread, b + 1)
                    pe.matmul(p1[:, :], keep["ident"][:, :], of_dst[u][:, :], start=False, stop=False)
                    for i in range(ST):
                        pe.wait_ge(got[u][i], it * 64 + 64)
                        ins = pe.matmul(p1[:, P * i:P * i + P], got_s[u][:, i, :, :].rearrange("p q m -> p (q m)"),
                                        keep["ident"][:, :], start=False, stop=(i == ST - 1))
                    ins.then_inc(mm1, 1)
                    pe.wait_ge(act1, b + 1)
                    pe.matmul(p2[:, :], w2[:, :], h1[:, :], start=True, stop=True).then_inc(mm2, 1)
                    pe.wait_ge(act2, b + 1)
                    pe.matmul(p3[:, :], w3[:, :], h2[:, :], start=True, stop=True).then_inc(mm3, 1)
                    pe.wait_ge(scanned, b + 1)
                    for of, to in ((run_sum, pts), (run_max, ptm)):
                        for i in range(ST):
                            ins = pe.transpose(to[:, P * i:P * i + P], of[u][:, P * i:P * i + P], keep["ident"][:, :])
                    ins.then_inc(turned, 1)

            loop(pe, body)

        @block.scalar
        def _(act):
            act.wait_ge(weights, 16 * 24)

            def body(it, last):
                for u in range(2):
                    b = it * 2 + u
                    act.wait_ge(mm1, b + 3)
                    act.activation(h1[:, :], p1[:, :], ACT.Relu, bias=b1[:, 0:1]).then_inc(act1, 1)
                    act.wait_ge(mm2, b + 1)
                    act.activation(h2[:, :], p2[:, :], ACT.Relu, bias=b2[:, 0:1]).then_inc(act2, 1)
                    act.wait_ge(mm3, b + 1)
                    act.activation(h3[:, :], p3[:, :], ACT.Identity, bias=b3[:, 0:1]).then_inc(act3, 1)
                    act.wait_ge(turned, b + 1)
                    for of, lo in ((pts, 0), (ptm, M)):
                        ins = act.activation(out_t[:, :, :, lo:lo + M],
                                             of[:, :].rearrange("p (i q m) -> p i q m", i=ST, q=4), ACT.Copy)
                    ins.then_inc(turned_out, 1)
                    act.wait_ge(turned_out, b + 1)
                    for q in range(4):
                        act.dma_start(quarter[q, b], out_t[:, :, q, :]).then_inc(out_st, 16)
                    act.wait_ge(out_st, b * 64 + 64)

            with act.Fori(0, NB // 2) as it:
                body(it, False)


def spread(col, f=F):
    return col.rearrange("p (c o) -> p c o", o=1).to_broadcast([P, NC, f])


def norm_scratch(ph):
    w = {k: ph.sb(f"ln_{k}", [P, NC]) for k in ("mean", "var", "dev", "rstd")}
    w["mid"], w["square"] = (ph.sb(f"ln_{k}", [P, NC, F]) for k in ("mid", "square"))
    w["has_var"], w["has_dev"] = ph.sem("ln_has_var"), ph.sem("ln_has_dev")
    return w


def norm_vector(dve, s, w, k, x, out):
    s.do(dve.tensor_reduce(w["mean"][:, :], x, AX.X, ALU.add))
    s.do(dve.tensor_scalar(w["mean"][:, :], w["mean"][:, :], 1.0 / F, None, ALU.mult))
    s.do(dve.tensor_tensor(w["mid"][:, :, :], x, spread(w["mean"][:, :]), ALU.subtract))
    s.do(dve.tensor_tensor(w["square"][:, :, :], w["mid"][:, :, :], w["mid"][:, :, :], ALU.mult))
    s.do(dve.tensor_reduce(w["var"][:, :], w["square"][:, :, :], AX.X, ALU.add))
    dve.tensor_scalar(w["var"][:, :], w["var"][:, :], 1.0 / F, LN_EPS, ALU.mult, ALU.add).then_inc(w["has_var"], 1)
    dve.wait_ge(w["has_dev"], k)
    s.do(dve.reciprocal(w["rstd"][:, :], w["dev"][:, :]))
    s.mark(dve.tensor_tensor(out, w["mid"][:, :, :], spread(w["rstd"][:, :]), ALU.mult))


def norm_scalar(act, w, k):
    act.wait_ge(w["has_var"], k)
    act.activation(w["dev"][:, :], w["var"][:, :], ACT.Sqrt).then_inc(w["has_dev"], 1)


def node_phase(nc, io, dram, keep):
    with phase(nc, "nd") as ph:
        runs = ph.sb("runs", [P, NC, 2 * M])
        edge_rows = ph.sb("edge_rows", [P, 3, 2 * M])
        across = ph.sb("across", [P, 3, NC])
        off = ph.sb("off", [P, NC])
        part = ph.sb("part", [P, NC, 2 * M])
        has, inv = ph.sb("has", [P, NC]), ph.sb("inv", [P, NC])
        cat = ph.sb("cat", [P, NC, P])
        catT = ph.sb("catT", [P, NP])
        w4, w4u = ph.sb("w4", [P, M]), ph.sb("w4u", [M, M])
        w5, w6 = ph.sb("w5", [M, M]), ph.sb("w6", [M + 1, F])
        u0, b4, b5 = ph.sb("u0", [M, 1]), ph.sb("b4", [M, 1]), ph.sb("b5", [M, 1])
        b4u = ph.sb("b4u", [M, 1])
        a4, a5 = ph.sb("a4", [M, NP]), ph.sb("a5", [M + 1, NP])
        res = ph.sb("res", [P, NC, F])
        w = norm_scratch(ph)
        pt = ph.ps("pt", [P, 7 * 512])
        pu = ph.ps("pu", [P, 512])
        loaded, got, joined, turned, copied, mm, acted, dv, rows_in = (ph.sem(n) for n in (
            "loaded", "got", "joined", "turned", "copied", "mm", "acted", "dv", "rows_in"))
        block = ph.block()
        ends = [QE * (q + 1) - 1 for q in range(3)]

        @block.sync
        def _(sp):
            for q, e in enumerate(ends):
                sp.dma_start(edge_rows[:, q, :], dram["runs"][e:e + 1, :].to_broadcast([P, 2 * M])).then_inc(rows_in, 16)
            w4_d = io["L0_gnn_W4"]
            sp.dma_start(w4[:, :], w4_d[0:P, :]).then_inc(loaded, 16)
            sp.dma_start(w4u[:, :], w4_d[P:P + M, :]).then_inc(loaded, 16)
            sp.dma_start(w5[:, :], io["L0_gnn_W5"]).then_inc(loaded, 16)
            sp.dma_start(w6[0:M, :], io["L0_gnn_W6"]).then_inc(loaded, 16)
            sp.dma_start(w6[M:M + 1, :], row(io["L0_gnn_b6"])).then_inc(loaded, 16)
            sp.dma_start(u0[:, :], column(io["L0_gnn_u"][0, :])).then_inc(loaded, 16)
            sp.dma_start(b4[:, :], column(io["L0_gnn_b4"])).then_inc(loaded, 16)
            sp.dma_start(b5[:, :], column(io["L0_gnn_b5"])).then_inc(loaded, 16)

        @block.gpsimd
        def _(pool):
            for c in range(NC):
                pool.indirect_dma_start(runs[:, c, :], None, dram["runs"],
                                        bass.IndirectOffsetOnAxis(keep["last_idx"][:, c:c + 1].bitcast(U32), 0)).then_inc(got, 16)

        @block.vector
        def _(dve):
            s = Steps(dve, dv)
            s.mark(dve.memset(a5[M:M + 1, :], 1.0))
            for q, e in enumerate(ends):
                s.do(dve.tensor_scalar(across[:, q, :], keep["first"][:, :], float(e), None, ALU.is_le))
                s.do(dve.scalar_tensor_tensor(across[:, q, :], keep["last"][:, :], float(e), across[:, q, :],
                                              ALU.is_gt, ALU.mult))
            s.do(dve.tensor_scalar(inv[:, :], keep["degree"][:, :], 1.0, None, ALU.max))
            s.do(dve.reciprocal(inv[:, :], inv[:, :]))
            s.do(dve.tensor_scalar(has[:, :], keep["degree"][:, :], 0.0, None, ALU.is_gt))
            s.do(dve.tensor_tensor(inv[:, :], inv[:, :], has[:, :], ALU.mult))
            s.mark(dve.tensor_copy(cat[:, :, 0:F], keep["x"][:, :, :]))
            dve.wait_ge(rows_in, 48)
            dve.wait_ge(got, 16 * NC)
            for q in range(3):
                s.do(dve.tensor_scalar(off[:, :], across[:, q, :], BIG, -BIG, ALU.mult, ALU.add))
                s.do(dve.tensor_tensor(part[:, :, :], edge_rows[:, q:q + 1, :].to_broadcast([P, NC, 2 * M]),
                                       spread(across[:, q, :]), ALU.mult))
                s.do(dve.tensor_tensor(part[:, :, M:2 * M], part[:, :, M:2 * M], spread(off[:, :], M), ALU.add))
                s.do(dve.tensor_tensor(runs[:, :, 0:M], runs[:, :, 0:M], part[:, :, 0:M], ALU.add))
                s.do(dve.tensor_tensor(runs[:, :, M:2 * M], runs[:, :, M:2 * M], part[:, :, M:2 * M], ALU.max))
            s.do(dve.tensor_tensor(cat[:, :, F:F + M], runs[:, :, 0:M], spread(inv[:, :], M), ALU.mult))
            dve.tensor_tensor(cat[:, :, F + M:P], runs[:, :, M:2 * M], spread(has[:, :], M), ALU.mult).then_inc(joined, 1)
            dve.wait_ge(turned, 1)
            dve.tensor_copy(catT[:, :], pt[:, 0:NP]).then_inc(copied, 1)
            dve.wait_ge(loaded, 16 * 8)
            dve.wait_ge(mm, 1)
            dve.tensor_tensor(b4u[:, :], pu[0:M, 0:1], b4[:, :], ALU.add).then_inc(copied, 1)
            dve.wait_ge(mm, 4)
            s.do(dve.tensor_tensor(res[:, :, :].rearrange("p c f -> p (c f)"), pt[:, 0:NC * F],
                                   keep["x"][:, :, :].rearrange("p c f -> p (c f)"), ALU.add))
            norm_vector(dve, s, w, 1, res[:, :, :], keep["x"][:, :, :])

        @block.tensor
        def _(pe):
            pe.wait_ge(joined, 1)
            for c in range(NC):
                ins = pe.transpose(pt[:, P * c:P * c + P], cat[:, c, :], keep["ident"][:, :])
            ins.then_inc(turned, 1)
            pe.wait_ge(loaded, 16 * 8)
            pe.matmul(pu[0:M, 0:1], w4u[:, :], u0[:, :], start=True, stop=True).then_inc(mm, 1)

            def product(weight, of, rows_, m):
                for k in range(0, NP, 512):
                    n = min(512, NP - k)
                    ins = pe.matmul(pt[0:m, k:k + n], weight, of[0:rows_, k:k + n], start=True, stop=True)
                ins.then_inc(mm, 1)

            pe.wait_ge(copied, 2)
            product(w4[:, :], catT, P, M)
            pe.wait_ge(acted, 1)
            product(w5[:, :], a4, M, M)
            pe.wait_ge(acted, 2)
            for c in range(NC):
                ins = pe.matmul(pt[:, F * c:F * c + F], a5[:, P * c:P * c + P], w6[:, :], start=True, stop=True)
            ins.then_inc(mm, 1)

        @block.scalar
        def _(act):
            act.wait_ge(copied, 2)
            act.wait_ge(mm, 2)
            act.activation(a4[:, :], pt[0:M, 0:NP], ACT.Relu, bias=b4u[:, 0:1]).then_inc(acted, 1)
            act.wait_ge(dv, 1)
            act.wait_ge(mm, 3)
            act.activation(a5[0:M, :], pt[0:M, 0:NP], ACT.Relu, bias=b5[:, 0:1]).then_inc(acted, 1)
            norm_scalar(act, w, 1)


def dense_phase(nc, io, dram, keep):
    with phase(nc, "de") as ph:
        cnt = [ph.sb(f"cnt{u}", [P, NP]) for u in range(2)]
        logs = [ph.sb(f"logs{u}", [P, N]) for u in range(2)]
        tiny, ones = ph.sb("tiny", [P, 1]), ph.sb("ones", [P, 1])
        leave = [ph.ps(f"leave{u}", [P, 512]) for u in range(2)]
        loaded = [ph.sem(f"loaded{u}") for u in range(2)]
        stored = [ph.sem(f"stored{u}") for u in range(2)]
        summed, logged, evened, dv, ready = (ph.sem(n) for n in ("summed", "logged", "evened", "dv", "ready"))
        block = ph.block()
        counts = dram["counts"][0:COUNTS, :].rearrange("(c p s) o -> c p (s o)", p=P, s=NP)
        logs_d = dram["logs"].rearrange("(c p) s -> c p s", p=P)

        def loop(eng, body):
            with eng.Fori(0, NC // 2) as it:
                for u in range(2):
                    body(it * 2 + u, u, it)
            body(NC - 1, 0, NC // 2)

        @block.sync
        def _(sp):
            sp.dma_start(cnt[0][:, :], counts[0]).then_inc(loaded[0], 16)
            sp.dma_start(cnt[1][:, :], counts[1]).then_inc(loaded[1], 16)
            done = sp.alloc_register("chunks_done")
            sp.reg_mov(done, 0)

            def serve(u, more):
                sp.reg_add(done, done, 1)
                n_done = sp.snap(done)
                if more:
                    sp.wait_ge(ready, 1)
                    sp.wait_ge(logged, n_done)
                    sp.wait_ge(summed, n_done)
                    sp.dma_start(cnt[u][:, :], counts[n_done + 1]).then_inc(loaded[u], 16)
                sp.wait_ge(ready, 1)
                sp.wait_ge(evened, n_done)
                sp.dma_start(logs_d[n_done - 1], logs[u][:, :]).then_inc(stored[u], 16)

            with sp.Fori(0, (NC - 3) // 2):
                serve(0, True)
                serve(1, True)
            serve(0, True)
            serve(1, False)
            serve(0, False)
            sp.wait_ge(stored[0], 16 * (NC // 2 + 2))
            sp.wait_ge(stored[1], 16 * (NC // 2 + 1))

        @block.vector
        def _(dve):
            dve.memset(tiny[:, :], 1e-18)
            dve.memset(ones[:, :], 1.0)
            dve.memset(keep["out_deg"][:, :], 1.0).then_inc(ready, 1)
            dve.wait_ge(ready, 1)
            dve.sem_inc(dv, 2)

            def body(c, u, it):
                dve.wait_ge(summed, c + 1)
                dve.tensor_tensor(keep["out_deg"][:, :], keep["out_deg"][:, :], leave[u][:, 0:NC], ALU.add).then_inc(dv, 1)
                dve.wait_ge(dv, c + 3)
                dve.wait_ge(logged, c + 1)
                dve.scalar_tensor_tensor(logs[u][:, :], logs[u][:, :], OFF, logs[u][:, :], ALU.mult, ALU.min).then_inc(evened, 1)

            loop(dve, body)

        @block.tensor
        def _(pe):
            pe.wait_ge(ready, 1)

            def body(c, u, it):
                pe.wait_ge(loaded[u], it * 16 + 16)
                pe.wait_ge(dv, c + 1)
                for k in range(NC):
                    ins = pe.matmul(leave[u][:, k:k + 1], cnt[u][:, P * k:P * k + P], ones[:, :], start=True, stop=True)
                ins.then_inc(summed, 1)

            loop(pe, body)

        @block.scalar
        def _(act):
            act.wait_ge(ready, 1)
            act.sem_inc(stored[0], 16)
            act.sem_inc(stored[1], 16)

            def body(c, u, it):
                act.wait_ge(loaded[u], it * 16 + 16)
                act.wait_ge(stored[u], it * 16 + 16)
                act.activation(logs[u][:, :], cnt[u][:, 0:N], ACT.Ln, bias=tiny[:, 0:1], scale=float(np.e)).then_inc(logged, 1)

            loop(act, body)


SW = 512
NS = -(-N // SW)
NG = -(-NC // 4)
BLOCKS = [(SW * b, min(SW, N - SW * b)) for b in range(NS)]
GROUPS = [[(k, min(P, N - P * k)) for k in range(4 * g, min(4 * g + 4, NC))] for g in range(NG)]
AUG = F + 1


class Softmax:

    def __init__(self, nc, ph, dram, l, blocks=BLOCKS):
        self.l, self.blocks_at = l, blocks
        self.NS = len(blocks)
        self.logs_d = dram["logs"].rearrange("(c p) s -> c p s", p=P)
        self.logs = [ph.sb(f"logs{u}", [P, N]) for u in range(2)]
        self.xs = [ph.sb(f"xs{u}", [P, N]) for u in range(2)]
        self.esT = ph.sb("esT", [P, NC, P])
        self.v = ph.sb("v", [P, NC, AUG])
        self.sums = ph.sb("sums", [P, NC * AUG])
        self.den = ph.sb("den", [P, NC])
        self.peaks = ph.sb("peaks", [P, self.NS])
        self.neg = [ph.sb(f"neg{u}", [P, 1]) for u in range(2)]
        self.pa = ph.ps("pa", [P, 8, SW])
        self.flat = self.pa[:, :, :].rearrange("p b n -> p (b n)")
        self.logs_in = [ph.sem(f"logs_in{u}") for u in range(2)]
        self.ready, self.peaked, self.negated, self.exped, self.turned_es, self.even, self.odd, self.weighed, self.summed = (
            ph.sem(n) for n in ("ready", "peaked", "negated", "exped", "turned_es", "even", "odd", "weighed", "summed"))

    def loop(self, eng, body):
        with eng.Fori(0, NC // 2) as it:
            for u in range(2):
                body(it * 2 + u, u, True)
        body(NC - 1, 0, False)

    def load(self, sp):
        sp.dma_start(self.logs[0][:, :], self.logs_d[0]).then_inc(self.logs_in[0], 16)
        sp.dma_start(self.logs[1][:, :], self.logs_d[1]).then_inc(self.logs_in[1], 16)
        used, nxt = sp.alloc_register(f"logs_used{self.l}"), sp.alloc_register(f"next_logs{self.l}")
        sp.reg_mov(used, 0)
        sp.reg_mov(nxt, 1)

        def again(u):
            sp.reg_add(used, used, self.NS)
            sp.reg_add(nxt, nxt, 1)
            n_used = sp.snap(used)
            sp.wait_ge(self.ready, 1)
            sp.wait_ge(self.peaked, n_used)
            sp.dma_start(self.logs[u][:, :], self.logs_d[sp.snap(nxt)]).then_inc(self.logs_in[u], 16)

        with sp.Fori(0, (NC - 3) // 2):
            again(0)
            again(1)
        again(0)

    def weigh(self, pe, ident, c, u):
        pe.wait_ge(self.exped, c + 1)
        pe.wait_ge(self.summed, c + 1)
        for g in range(NG + 2):
            if g < NG:
                for j, (k, m) in enumerate(GROUPS[g]):
                    ins = pe.transpose(self.pa[0:m, 3 + g % 3, P * j:P * j + P], self.xs[u][:, P * k:P * k + m], ident)
                ins.then_inc(self.turned_es, 1)
            if g >= 2:
                w = g - 2
                if w % 2:
                    pe.wait_ge(self.odd, c * (NG // 2) + w // 2 + 1)
                else:
                    pe.wait_ge(self.even, c * (NG - NG // 2) + w // 2 + 1)
                for k, m in GROUPS[w]:
                    ins = pe.matmul(self.pa[:, 6 + u, 0:AUG], self.esT[0:m, k, :], self.v[0:m, k, :],
                                    start=(k == 0), stop=(k == NC - 1))
        ins.then_inc(self.weighed, 1)

    def group(self, g):
        k, m = GROUPS[g][0]
        n = len(GROUPS[g])
        return self.esT[0:m, k:k + n, :].rearrange("p k n -> p (k n)"), self.pa[0:m, 3 + g % 3, 0:P * n]

    def scalar_even(self, act, c):
        for g in range(0, NG, 2):
            act.wait_ge(self.turned_es, c * NG + g + 1)
            to, of = self.group(g)
            act.activation(to, of, ACT.Copy).then_inc(self.even, 1)

    def scalar_exp(self, act, c, u):
        act.wait_ge(self.negated, c + 1)
        act.activation(self.xs[u][:, :], self.xs[u][:, :], ACT.Exp, bias=self.neg[u][:, 0:1]).then_inc(self.exped, 1)

    def vector_counters(self, dve):
        self.blocks, self.loads, self.outs = (dve.alloc_register(f"{n}{self.l}") for n in ("blocks", "loads", "outs"))
        for r in (self.blocks, self.loads, self.outs):
            dve.reg_mov(r, 0)

    def vector_peak(self, dve, c, u, scores, scored):
        if u == 0:
            dve.reg_add(self.loads, self.loads, 16)
        for b, (lo, m) in enumerate(self.blocks_at):
            dve.reg_add(self.blocks, self.blocks, 1)
            n = dve.snap(self.blocks)
            n_in = dve.snap(self.loads)
            dve.wait_ge(self.ready, 1)
            if b == 0:
                dve.wait_ge(self.logs_in[u], n_in)
            dve.wait_ge(scored, n)
            dve.tensor_tensor_reduce(self.xs[u][:, lo:lo + m], scores(b, lo, m), self.logs[u][:, lo:lo + m],
                                     1.0, -3e38, ALU.add, ALU.max, self.peaks[:, b:b + 1]).then_inc(self.peaked, 1)
        dve.wait_ge(self.peaked, (c + 1) * self.NS)
        dve.tensor_reduce(self.neg[u][:, :], self.peaks[:, :], AX.X, ALU.max).then_inc(self.dv, 1)
        dve.wait_ge(self.dv, c + 1)
        dve.tensor_scalar(self.neg[u][:, :], self.neg[u][:, :], -1e29, -1.0, ALU.max, ALU.mult).then_inc(self.negated, 1)

    def vector_odd(self, dve, c):
        for g in range(1, NG, 2):
            dve.wait_ge(self.turned_es, c * NG + g + 1)
            to, of = self.group(g)
            dve.tensor_copy(to, of).then_inc(self.odd, 1)

    def vector_out(self, dve, c, u):
        dve.reg_add(self.outs, self.outs, 1)
        n = dve.snap(self.outs)
        dve.wait_ge(self.ready, 1)
        dve.wait_ge(self.weighed, n)
        dve.tensor_copy(self.sums[:, ds(c * AUG, AUG)], self.pa[:, 6 + u, 0:AUG]).then_inc(self.summed, 1)

    def vector_mean(self, dve, s, out):
        dve.wait_ge(self.summed, NC + 2)
        sums = self.sums[:, :].rearrange("p (c f) -> p c f", f=AUG)
        s.do(dve.tensor_scalar(self.den[:, :], sums[:, :, F], 1e-30, None, ALU.max))
        s.do(dve.reciprocal(self.den[:, :], self.den[:, :]))
        s.mark(dve.tensor_tensor(out, sums[:, :, 0:F], spread(self.den[:, :]), ALU.mult))


def conv_phase(nc, io, dram, keep, l):
    with phase(nc, f"c{l}") as ph:
        hT = ph.sb("hT", [P, NP])
        kT, qT = ph.sb("kT", [P, NP]), ph.sb("qT", [P, NP + P])
        wq, wk, wvs = ph.sb("wq", [P, F]), ph.sb("wk", [P, F]), ph.sb("wvs", [P, 2 * F])
        q_st = [ph.sb(f"q_st{u}", [P, P]) for u in range(2)]
        res, agg = ph.sb("res", [P, NC, F]), ph.sb("agg", [P, NC, F])
        gain, offset = ph.sb("gain", [P, F]), ph.sb("offset", [P, F])
        w = norm_scratch(ph)
        sm = Softmax(nc, ph, dram, l)
        sm.dv = ph.sem("peak_steps")
        v, pa, flat = sm.v, sm.pa, sm.flat
        (blank, zeroed, loaded, turned, copied, mm, acted, staged, scored, dv) = (ph.sem(n) for n in (
            "blank", "zeroed", "loaded", "turned", "copied", "mm", "acted", "staged", "scored", "dv"))
        block = ph.block()
        if l == 0:
            W = {k: io[f"L1_gnn_W{k}0"] for k in "qkvs"}
            B = {k: io[f"L1_gnn_b{k}0"] for k in "qkvs"}
            g_d, b_d = io["L1_gnn_ln0_g"], io["L1_gnn_ln0_b"]
        else:
            W = {k: io[f"L1_gnn_W{k}"][l - 1] for k in "qkvs"}
            B = {k: io[f"L1_gnn_b{k}"][l - 1, :] for k in "qkvs"}
            g_d, b_d = io["L1_gnn_ln_g"][l - 1, :], io["L1_gnn_ln_b"][l - 1, :]
        h = keep["x"] if l == 0 else keep["h"]

        @block.sync
        def _(sp):
            sp.wait_ge(blank, 1)
            for to, of in ((wq, "q"), (wk, "k")):
                sp.dma_start(to[0:F, :], W[of]).then_inc(loaded, 16)
                sp.dma_start(to[F:AUG, :], row(B[of])).then_inc(loaded, 16)
            for lo, of in ((0, "v"), (F, "s")):
                sp.dma_start(wvs[0:F, lo:lo + F], W[of]).then_inc(loaded, 16)
                sp.dma_start(wvs[F:AUG, lo:lo + F], row(B[of])).then_inc(loaded, 16)
            sp.dma_start(gain[:, :], row(g_d).to_broadcast([P, F])).then_inc(loaded, 16)
            sp.dma_start(offset[:, :], row(b_d).to_broadcast([P, F])).then_inc(loaded, 16)
            sm.load(sp)

        @block.gpsimd
        def _(pool):
            pool.memset(kT[F:P, :], 0.0).then_inc(zeroed, 1)
            for u in range(2):
                pool.memset(q_st[u][F:P, :], 0.0).then_inc(zeroed, 1)
            pool.memset(qT[0:F, NP:NP + P], 0.0).then_inc(zeroed, 1)

        @block.tensor
        def _(pe):
            for c in range(NC):
                ins = pe.transpose(flat[0:F, P * c:P * c + P], h[:, c, :], keep["ident"][:, :])
            ins.then_inc(turned, 1)
            pe.wait_ge(loaded, 16 * 10)
            pe.wait_ge(copied, 1)
            for n, weight in enumerate((wq, wk)):
                if n:
                    pe.wait_ge(acted, n)
                for k in range(0, NP, SW):
                    m = min(SW, NP - k)
                    ins = pe.matmul(flat[0:F, k:k + m], weight[:, :], hT[:, k:k + m], start=True, stop=True)
                ins.then_inc(mm, 1)
            pe.wait_ge(acted, 2)
            for c in range(NC):
                ins = pe.matmul(flat[:, P * c:P * c + P], hT[:, P * c:P * c + P], wvs[:, :], start=True, stop=True)
            ins.then_inc(mm, 1)
            pe.wait_ge(copied, 2)
            pe.wait_ge(zeroed, 4)
            pe.sem_inc(sm.summed, 2)

            def scores(c, u, first=False):
                pe.wait_ge(staged, c + 1)
                for b, (lo, m) in enumerate(BLOCKS):
                    if b == 0 and not first:
                        pe.wait_ge(sm.peaked, c * NS)
                    elif b >= 3:
                        pe.wait_ge(sm.peaked, c * NS + b - 2)
                    pe.matmul(pa[:, b % 3, 0:m], q_st[u][:, :], kT[:, lo:lo + m], start=True, stop=True).then_inc(scored, 1)

            scores(0, 0, first=True)

            def body(c, u, more):
                if more:
                    scores(c + 1, 1 - u)
                sm.weigh(pe, keep["ident"][:, :], c, u)

            sm.loop(pe, body)

        @block.vector
        def _(dve):
            for t in (wq, wk, wvs):
                ins = dve.memset(t[F:P, :], 0.0)
            ins.then_inc(blank, 1)
            dve.memset(hT[F:P, :], 1.0)
            dve.memset(v[:, :, F:AUG], 1.0).then_inc(sm.ready, 1)
            dve.wait_ge(turned, 1)
            dve.tensor_copy(hT[0:F, :], flat[0:F, 0:NP]).then_inc(copied, 1)
            dve.wait_ge(mm, 3)
            vs = flat[:, 0:NC * P].rearrange("p (c f) -> p c f", f=P)
            dve.tensor_copy(v[:, :, 0:F], vs[:, :, 0:F])
            dve.tensor_copy(res[:, :, :], vs[:, :, F:P]).then_inc(copied, 1)
            sm.vector_counters(dve)

            def of_block(b, lo, m):
                return pa[:, b % 3, 0:m]

            sm.vector_peak(dve, 0, 0, of_block, scored)

            def body(c, u, more):
                if more:
                    sm.vector_peak(dve, c + 1, 1 - u, of_block, scored)
                sm.vector_odd(dve, c)
                sm.vector_out(dve, c, u)

            sm.loop(dve, body)
            s = Steps(dve, dv)
            sm.vector_mean(dve, s, agg[:, :, :])
            dve.wait_ge(dv, s.n)
            s.do(dve.tensor_tensor(res[:, :, :], res[:, :, :], agg[:, :, :], ALU.add))
            if l:
                s.do(dve.tensor_tensor(res[:, :, :], res[:, :, :], h[:, :, :], ALU.add))
            norm_vector(dve, s, w, 1, res[:, :, :], agg[:, :, :])
            dve.wait_ge(dv, s.n)

            def per_feature(vec):
                return vec[:, :].rearrange("p (o f) -> p o f", o=1).to_broadcast([P, NC, F])

            dve.wait_ge(loaded, 16 * 10)
            s.do(dve.tensor_tensor(agg[:, :, :], agg[:, :, :], per_feature(gain), ALU.mult))
            s.do(dve.tensor_tensor(agg[:, :, :], agg[:, :, :], per_feature(offset), ALU.add))
            s.do(dve.tensor_scalar(keep["h"][:, :, :], agg[:, :, :], 0.0, None, ALU.max))
            if l == 3:
                s.do(dve.tensor_tensor(res[:, :, :], keep["x"][:, :, :], keep["h"][:, :, :], ALU.add))
                norm_vector(dve, s, w, 2, res[:, :, :], keep["x"][:, :, :])

        @block.scalar
        def _(act):
            act.wait_ge(mm, 1)
            act.activation(qT[0:F, 0:NP], flat[0:F, 0:NP], ACT.Copy, scale=float(F) ** -0.5).then_inc(acted, 1)
            act.wait_ge(mm, 2)
            act.activation(kT[0:F, :], flat[0:F, 0:NP], ACT.Copy).then_inc(acted, 1)
            act.wait_ge(acted, 1)
            act.wait_ge(zeroed, 4)

            def stage(c, u):
                act.activation(q_st[u][0:F, :], qT[0:F, ds(c * P, P)], ACT.Copy).then_inc(staged, 1)

            stage(0, 0)
            stage(1, 1)
            sm.scalar_exp(act, 0, 0)

            def body(c, u, more):
                if more:
                    act.wait_ge(scored, (c + 1) * NS)
                    stage(c + 2, u)
                sm.scalar_even(act, c)
                if more:
                    sm.scalar_exp(act, c + 1, 1 - u)

            sm.loop(act, body)
            norm_scalar(act, w, 1)
            if l == 3:
                norm_scalar(act, w, 2)


D4 = 4
H16 = F // D4
WS = 2 * H16 + F + 4
WD = 2 * H16 + 4
PAIRS_B = 16
TB = 2 * PAIRS_B
HB = EP // 2 // (PAIRS_B * P)
HE = EP // 2


def sheaf_tables_phase(nc, io, dram, keep):
    with phase(nc, "st") as ph:
        xT, yT, zT = (ph.sb(n, [F, NP]) for n in ("xT", "yT", "zT"))
        w1c = ph.sb("w1c", [F, D4])
        same = ph.sb("same", [F, H16])
        w1x, w2x = ph.sb("w1x", [F, D4, H16]), ph.sb("w2x", [F, F])
        mix = ph.sb("mix", [F, 2 * H16 + F])
        root = ph.sb("root", [P, NC])
        pt = ph.ps("pt", [P, 7 * 512])
        zero, loaded, turned, copied, mm, rooted, dv, stored = (ph.sem(n) for n in (
            "zero", "loaded", "turned", "copied", "mm", "rooted", "dv", "stored"))
        block = ph.block()
        src_tab, dst_tab = keep["src_tab"], keep["dst_tab"]

        @block.sync
        def _(sp):
            for d in range(D4):
                sp.dma_start(w1c[H16 * d:H16 * d + H16, :], io["L2_gnn_W1"][d:d + 1, :].to_broadcast([H16, D4])).then_inc(loaded, 16)
            sp.dma_start(mix[:, 0:H16], io["mlp1_T"][0:F, :]).then_inc(loaded, 16)
            sp.dma_start(mix[:, H16:2 * H16], io["mlp1_T"][F:2 * F, :]).then_inc(loaded, 16)
            sp.wait_ge(zero, 1)
            for d in range(D4):
                lo = H16 * d
                sp.dma_start(w2x[lo:lo + H16, lo:lo + H16], io["L2_gnn_W2"]).then_inc(loaded, 16)
            sp.wait_ge(copied, 4)
            sp.dma_start(chunked(dram["sheaf_src"]), src_tab[:, :, :]).then_inc(stored, 16)
            sp.dma_start(chunked(dram["sheaf_dst"]), dst_tab[:, :, :]).then_inc(stored, 16)
            sp.wait_ge(stored, 32)

        @block.tensor
        def _(pe):
            for c in range(NC):
                ins = pe.transpose(pt[0:F, P * c:P * c + P], keep["x"][:, c, :], keep["ident"][:, :])
            ins.then_inc(turned, 1)
            pe.wait_ge(loaded, 16 * 10)
            pe.wait_ge(dv, 2)
            for n, (weight, of) in enumerate(((w1x[:, :, :].rearrange("p k f -> p (k f)"), xT), (w2x[:, :], yT))):
                pe.wait_ge(copied, n + 1)
                for k in range(0, NP, 512):
                    m = min(512, NP - k)
                    ins = pe.matmul(pt[0:F, k:k + m], weight, of[:, k:k + m], start=True, stop=True)
                ins.then_inc(mm, 1)
            pe.wait_ge(copied, 3)
            for c in range(NC):
                ins = pe.matmul(pt[:, P * c:P * c + 2 * H16 + F], zT[:, P * c:P * c + P], mix[:, :], start=True, stop=True)
            ins.then_inc(mm, 1)

        @block.scalar
        def _(act):
            act.activation(root[:, :], keep["out_deg"][:, :], ACT.Sqrt).then_inc(rooted, 1)

        @block.vector
        def _(dve):
            dve.memset(w2x[:, :], 0.0).then_inc(zero, 1)
            dve.memset(src_tab[:, :, :], 0.0)
            dve.memset(dst_tab[:, :, :], 0.0)
            s = Steps(dve, dv)
            dve.tensor_copy(mix[:, 2 * H16:2 * H16 + F], keep["ident"][0:F, 0:F])
            s.do(dve.tensor_reduce(same[:, :], keep["ident"][0:F, 0:F].rearrange("p (d f) -> p f d", d=D4), AX.X, ALU.add))
            dve.wait_ge(loaded, 16 * 10)
            s.do(dve.tensor_tensor(w1x[:, :, :], w1c[:, :].rearrange("p (k o) -> p k o", o=1).to_broadcast([F, D4, H16]),
                                   same[:, :].rearrange("p (o f) -> p o f", o=1).to_broadcast([F, D4, H16]), ALU.mult))
            dve.wait_ge(turned, 1)
            dve.tensor_copy(xT[:, :], pt[0:F, 0:NP]).then_inc(copied, 1)
            for n, to in enumerate((yT, zT)):
                dve.wait_ge(mm, n + 1)
                dve.tensor_copy(to[:, :], pt[0:F, 0:NP]).then_inc(copied, 1)
            dve.wait_ge(rooted, 1)
            for tab, at in ((src_tab, 2 * H16 + F), (dst_tab, 2 * H16)):
                s.mark(dve.reciprocal(tab[:, :, at], root[:, :]))
            dve.wait_ge(mm, 3)
            out = pt[:, 0:NC * P].rearrange("p (c f) -> p c f", f=P)
            dve.tensor_copy(src_tab[:, :, 0:2 * H16 + F], out[:, :, 0:2 * H16 + F])
            dve.tensor_copy(dst_tab[:, :, 0:H16], out[:, :, H16:2 * H16])
            dve.tensor_copy(dst_tab[:, :, H16:2 * H16], out[:, :, 0:H16]).then_inc(copied, 1)


def sheaf_phase(nc, io, dram, keep):
    with phase(nc, "sh") as ph:
        got_s = [ph.sb(f"got_s{u}", [P, TB, WS]) for u in range(2)]
        got_d = [ph.sb(f"got_d{u}", [P, TB, WD]) for u in range(2)]
        st_src = [ph.sb(f"st_src{u}", [P, PAIRS_B, 2], I32) for u in range(2)]
        st_dst = [ph.sb(f"st_dst{u}", [P, PAIRS_B, 2], I32) for u in range(2)]
        NSEQ = PAIRS_B * P
        seq = [ph.sb(f"seq{u}", [P, NSEQ + 1], I32) for u in range(2)]
        cont = ph.sb("cont", [P, NSEQ])
        bias1 = ph.sb("bias1", [P, 1])
        bias2 = ph.sb("bias2", [P, 6])
        w2 = ph.sb("w2", [P, 48])
        zin = ph.sb("zin", [P, TB, 2 * H16])
        hz = ph.sb("hz", [P, TB // 4, P])
        MT = 2 * TB
        tri = ph.sb("tri", [P, MT, 4, 4])
        q = ph.sb("q", [P, MT, 4, 4])
        prod = ph.sb("prod", [P, MT, 3, 4])
        dot = ph.sb("dot", [P, MT, 3])
        norm2, norm1, inv = (ph.sb(n, [P, MT]) for n in ("norm2", "norm1", "inv"))
        scale = ph.sb("scale", [P, TB])
        gprod = ph.sb("gprod", [P, TB, 4, 16])
        g = ph.sb("g", [P, TB, 16])
        msg = ph.sb("msg", [P, TB, F])
        term = ph.sb("term", [P, TB, F])
        run = [ph.sb(f"run{k}", [P, 512]) for k in range(2)]
        out_t = ph.sb("out_t", [P, PAIRS_B, 2, F])
        pz = ph.ps("pz", [P, TB // 4, P])
        pp = ph.ps("pp", [P, TB // 4, 8, 6])
        pin = [ph.ps(f"pin{k}", [P, 512]) for k in range(2)]
        pout = [ph.ps(f"pout{k}", [P, 512]) for k in range(2)]
        (zero, loaded, ready, staged, messaged, zed, hidden, parred, sized, rooted, turned, scanned, backed, copied,
         stored, masked, added, dv) = (ph.sem(n) for n in (
             "zero", "loaded", "ready", "staged", "messaged", "zed",  "hidden", "parred", "sized", "rooted", "turned",
             "scanned", "backed", "copied", "stored", "masked", "added", "dv"))
        got = [ph.sem(f"got{u}") for u in range(2)]
        seq_in = [ph.sem(f"seq_in{u}") for u in range(2)]
        block = ph.block()
        sums_d = dram["sums"].rearrange("(h b i p) f -> h b p i f", h=2, b=HB, i=PAIRS_B)
        NB4 = PAIRS_B // 4
        assert HB % 2 == 1

        def loop(eng, body):
            body(1, 1, 0)
            with eng.Fori(0, HB // 2) as it:
                body(it * 2 + 2, 0, it)
                body(it * 2 + 3, 1, it + 1)

        @block.sync
        def _(sp):
            for k in range(8):
                sp.dma_start(bias1[H16 * k:H16 * k + H16, :], column(io["L2_gnn_mlp1_b"])).then_inc(loaded, 16)
            sp.dma_start(bias2[:, :], row(io["mlp2_b"]).to_broadcast([P, 6])).then_inc(loaded, 16)
            sp.wait_ge(zero, 1)
            for k in range(8):
                sp.dma_start(w2[H16 * k:H16 * k + H16, 6 * k:6 * k + 6], io["mlp2_T"]).then_inc(loaded, 16)

            def load(at, u):
                for h in range(2):
                    sp.dma_start(seq[u][F * h:F * h + F, :],
                                 io["dst_half"][h:h + 1, ds(at, NSEQ + 1)].to_broadcast([F, NSEQ + 1])).then_inc(seq_in[u], 16)

            load(0, 1)
            load(NSEQ, 0)
            at, masks = sp.alloc_register("edges_at"), sp.alloc_register("masks_done")
            sp.reg_mov(at, NSEQ)
            sp.reg_mov(masks, 0)

            def again(u):
                sp.reg_add(at, at, NSEQ)
                sp.reg_add(masks, masks, 1)
                n_masks = sp.snap(masks)
                sp.wait_ge(zero, 1)
                sp.wait_ge(masked, n_masks)
                load(sp.snap(at), u)

            with sp.Fori(0, (HB - 3) // 2):
                again(1)
                again(0)
            again(1)

        @block.gpsimd
        def _(pool):
            turn = pool.alloc_register("sheaf_turn")
            pool.reg_mov(turn, 0)

            def body(n, u, it):
                pool.reg_add(turn, turn, 1)
                now = pool.snap(turn)
                pool.wait_ge(ready, 1)
                pool.wait_ge(staged, now)
                pool.wait_ge(messaged, now)
                for i in range(PAIRS_B):
                    for h in range(2):
                        for to, st, tab in ((got_s, st_src, "sheaf_src"), (got_d, st_dst, "sheaf_dst")):
                            pool.indirect_dma_start(
                                to[u][:, 2 * i + h, :], None, dram[tab],
                                bass.IndirectOffsetOnAxis(st[u][:, i, h:h + 1].bitcast(U32), 0)).then_inc(got[u], 16)

            loop(pool, body)

        @block.vector
        def _(dve):
            dve.memset(w2[:, :], 0.0).then_inc(zero, 1)
            dve.memset(got_s[0][:, :, :], 0.0)
            dve.memset(got_d[0][:, :, :], 0.0)
            dve.memset(tri[:, :, :, :], 0.0)
            dve.memset(run[1][:, :], 0.0).then_inc(ready, 1)
            dve.sem_inc(messaged, 1)
            dve.wait_ge(ready, 1)
            s = Steps(dve, dv)
            for k in range(4):
                s.mark(dve.memset(tri[:, :, k, k], 1.0))
            s.mark(dve.tensor_copy(got_s[0][:, 0:NC, :], keep["src_tab"][:, :, :]))
            s.mark(dve.tensor_copy(got_d[0][:, 0:NC, :], keep["dst_tab"][:, :, :]))
            dve.wait_ge(dv, 6)
            dve.sem_inc(ready, 1)

            def stage(b, u):
                for st, of in ((st_src, "src"), (st_dst, "dst")):
                    ins = dve.tensor_copy(st[u][:, :, :].rearrange("p i h -> p h i"),
                                          keep[of][:, :].rearrange("p (h t) -> p h t", h=2)[:, :, ds(b * PAIRS_B, PAIRS_B)])
                ins.then_inc(staged, 1)

            def messages(n, u, s):
                dve.tensor_tensor(zin[:, :, :], got_s[u][:, :, 0:2 * H16], got_d[u][:, :, 0:2 * H16], ALU.add).then_inc(added, 1)
                dve.wait_ge(parred, n + 1)
                for col, lo, hi in ((0, 0, 3), (1, 3, 5), (2, 5, 6)):
                    w = hi - lo
                    ins = dve.tensor_tensor(
                        tri[:, :, col, 4 - w:4], pp[:, :, :, lo:hi].rearrange("p a b k -> p (a b) k"),
                        bias2[:, lo:hi].rearrange("p (o k) -> p o k", o=1).to_broadcast([P, MT, w]), ALU.add)
                    s.mark(ins)
                s.do(dve.tensor_tensor(scale[:, :], got_s[u][:, :, 2 * H16 + F], got_d[u][:, :, 2 * H16], ALU.mult))
                left = tri
                for k in range(4):
                    a = left[:, :, k, :]
                    s.do(dve.tensor_tensor(prod[:, :, 0, :], a, a, ALU.mult))
                    dve.tensor_reduce(norm2[:, :], prod[:, :, 0, :], AX.X, ALU.add).then_inc(sized, 1)
                    dve.wait_ge(rooted, 4 * n + k + 1)
                    s.do(dve.reciprocal(inv[:, :], norm1[:, :]))
                    s.do(dve.tensor_tensor(q[:, :, k, :], a, inv[:, :].rearrange("p (m o) -> p m o", o=1).to_broadcast([P, MT, 4]),
                                           ALU.mult))
                    if k < 3:
                        m = 3 - k
                        qk = q[:, :, k:k + 1, :].to_broadcast([P, MT, m, 4])
                        s.do(dve.tensor_tensor(prod[:, :, 0:m, :], left[:, :, k + 1:4, :], qk, ALU.mult))
                        s.do(dve.tensor_reduce(dot[:, :, 0:m], prod[:, :, 0:m, :], AX.X, ALU.add))
                        s.do(dve.tensor_tensor(prod[:, :, 0:m, :], qk, dot[:, :, 0:m].rearrange("p m (j o) -> p m j o", o=1)
                                               .to_broadcast([P, MT, m, 4]), ALU.mult))
                        s.do(dve.tensor_tensor(q[:, :, k + 1:4, :], left[:, :, k + 1:4, :], prod[:, :, 0:m, :], ALU.subtract))
                    left = q
                both = q[:, :, :, :].rearrange("p (t v) c r -> p t v (c r)", v=2)
                ue, ve = both[:, :, 0, :], both[:, :, 1, :]
                s.do(dve.tensor_tensor(ve, ve, scale[:, :].rearrange("p (t o) -> p t o", o=1).to_broadcast([P, TB, 16]), ALU.mult))
                for a in range(4):
                    s.mark(dve.tensor_tensor(
                        gprod[:, :, a, :].rearrange("p t (b k) -> p t b k", k=4), ue.rearrange("p t (b k) -> p t b k", k=4),
                        ve[:, :, 4 * a:4 * a + 4].rearrange("p t (o k) -> p t o k", o=1).to_broadcast([P, TB, 4, 4]), ALU.mult))
                dve.wait_ge(dv, s.base + s.n)
                s.do(dve.tensor_reduce(g[:, :, :], gprod[:, :, :, :].rearrange("p t a (b k) -> p t (a b) k", k=4), AX.X, ALU.add))
                ga = g[:, :, :].rearrange("p t (a b) -> p t a b", b=4)
                stalks = [got_s[u][:, :, 2 * H16 + H16 * b:2 * H16 + H16 * (b + 1)].rearrange("p t (o h) -> p t o h", o=1)
                          .to_broadcast([P, TB, 4, H16]) for b in range(4)]
                m4 = msg[:, :, :].rearrange("p t (a h) -> p t a h", a=4)
                t4 = term[:, :, :].rearrange("p t (a h) -> p t a h", a=4)
                for b in range(4):
                    s.do(dve.tensor_tensor(t4 if b else m4, stalks[b], ga[:, :, :, b:b + 1].to_broadcast([P, TB, 4, H16]), ALU.mult))
                    if b:
                        s.do(dve.tensor_tensor(msg[:, :, :], msg[:, :, :], term[:, :, :], ALU.add))
                dve.sem_inc(messaged, 1)

            PER = 4 + 4 * 3 + 3 * 4 + 1 + 4 + 1 + 7
            stage(0, 1)
            s = Steps(dve, dv, 6)
            messages(0, 0, s)
            assert s.n == PER, (s.n, PER)
            s.do(dve.tensor_copy(keep["loops"][:, :, :], msg[:, 0:NC, :]))

            def body(n, u, it, ahead=True):
                s = Steps(dve, dv, n * PER + 7)
                dve.wait_ge(got[u], it * 1024 + 1024)
                if ahead:
                    stage(n, 1 - u)
                messages(n, u, s)
                assert s.n == PER
                dve.wait_ge(seq_in[u], it * 32 + 32)
                dve.tensor_tensor(cont[:, :], seq[u][:, 1:NSEQ + 1], seq[u][:, 0:NSEQ], ALU.is_equal).then_inc(masked, 1)
                dve.wait_ge(masked, n)
                for k in range(NB4):
                    dve.wait_ge(turned, (n - 1) * NB4 + k + 1)
                    dve.tensor_tensor_scan(run[k % 2][:, :], cont[:, 512 * k:512 * k + 512], pin[k % 2][:, :],
                                           run[1 - k % 2][:, 511:512], ALU.mult, ALU.add).then_inc(scanned, 1)
                    dve.wait_ge(scanned, (n - 1) * NB4 + k + 1)

            body(1, 1, 0)
            with dve.Fori(0, HB // 2 - 1) as it:
                body(it * 2 + 2, 0, it)
                body(it * 2 + 3, 1, it + 1)
            it = HB // 2 - 1
            body(it * 2 + 2, 0, it)
            body(it * 2 + 3, 1, it + 1, ahead=False)

        @block.tensor
        def _(pe):
            pe.wait_ge(loaded, 16 * 17)
            pe.wait_ge(ready, 2)

            def hidden_and_entries(n):
                pe.wait_ge(added, n + 1)
                for k in range(TB // 4):
                    ins = pe.transpose(pz[:, k, :], zin[:, 4 * k:4 * k + 4, :].rearrange("p t f -> p (t f)"), keep["ident"][:, :])
                ins.then_inc(zed, 1)
                pe.wait_ge(hidden, n + 1)
                for k in range(TB // 4):
                    ins = pe.matmul(pp[:, k, :, :].rearrange("p a b -> p (a b)"), hz[:, k, :], w2[:, :], start=True, stop=True)
                ins.then_inc(parred, 1)

            hidden_and_entries(0)
            pe.sem_inc(copied, 2)

            def body(n, u, it):
                pe.wait_ge(messaged, n + 1)
                hidden_and_entries(n)
                pe.wait_ge(messaged, n + 2)
                for k in range(NB4 + 1):
                    if k < NB4:
                        for j in range(4):
                            i = 4 * k + j
                            ins = pe.transpose(pin[k % 2][:, P * j:P * j + P],
                                               msg[:, 2 * i:2 * i + 2, :].rearrange("p t f -> p (t f)"), keep["ident"][:, :])
                        ins.then_inc(turned, 1)
                    if k:
                        m = k - 1
                        pe.wait_ge(scanned, (n - 1) * NB4 + m + 1)
                        pe.wait_ge(copied, (n - 1) * NB4 + m + 1)
                        for j in range(4):
                            ins = pe.transpose(pout[m % 2][:, P * j:P * j + P], run[m % 2][:, P * j:P * j + P], keep["ident"][:, :])
                        ins.then_inc(backed, 1)

            loop(pe, body)

        @block.scalar
        def _(act):
            act.wait_ge(loaded, 16 * 17)

            def roots(n):
                act.wait_ge(zed, n + 1)
                act.activation(hz[:, :, :], pz[:, :, :], ACT.Relu, bias=bias1[:, 0:1]).then_inc(hidden, 1)
                for k in range(4):
                    act.wait_ge(sized, 4 * n + k + 1)
                    act.activation(norm1[:, :], norm2[:, :], ACT.Sqrt).then_inc(rooted, 1)

            roots(0)

            def body(n, u, it):
                roots(n)
                for k in range(NB4):
                    act.wait_ge(backed, (n - 1) * NB4 + k + 1)
                    act.activation(out_t[:, 4 * k:4 * k + 4, :, :], pout[k % 2][:, :].rearrange("p (i h f) -> p i h f", i=4, h=2),
                                   ACT.Copy).then_inc(copied, 1)
                act.wait_ge(copied, n * NB4 + 2)
                for h in range(2):
                    act.dma_start(sums_d[h, n - 1], out_t[:, :, h, :]).then_inc(stored, 16)
                act.wait_ge(stored, n * 32)

            loop(act, body)


def sheaf_node_phase(nc, io, dram, keep):
    with phase(nc, "sn") as ph:
        agg = ph.sb("agg", [P, NC, F])
        edge_row = ph.sb("edge_row", [P, 1, F])
        across, has = ph.sb("across", [P, NC]), ph.sb("has", [P, NC])
        part, low, grown = (ph.sb(n, [P, NC, F]) for n in ("part", "low", "grown"))
        coeff = ph.sb("coeff", [P, D4])
        w = norm_scratch(ph)
        loaded, got, dv, lowered, grew, tanhed = (ph.sem(n) for n in ("loaded", "got", "dv", "lowered", "grew", "tanhed"))
        block = ph.block()

        @block.sync
        def _(sp):
            sp.dma_start(edge_row[:, 0, :], dram["sums"][HE - 1:HE, :].to_broadcast([P, F])).then_inc(loaded, 16)
            sp.dma_start(coeff[:, :], row(io["L2_gnn_epsilons"]).to_broadcast([P, D4])).then_inc(loaded, 16)

        @block.gpsimd
        def _(pool):
            for c in range(NC):
                pool.indirect_dma_start(agg[:, c, :], None, dram["sums"],
                                        bass.IndirectOffsetOnAxis(keep["last_idx"][:, c:c + 1].bitcast(U32), 0)).then_inc(got, 16)

        @block.vector
        def _(dve):
            s = Steps(dve, dv)
            s.do(dve.tensor_scalar(across[:, :], keep["first"][:, :], float(HE - 1), None, ALU.is_le))
            s.do(dve.scalar_tensor_tensor(across[:, :], keep["last"][:, :], float(HE - 1), across[:, :], ALU.is_gt, ALU.mult))
            s.do(dve.tensor_scalar(has[:, :], keep["degree"][:, :], 0.0, None, ALU.is_gt))
            dve.wait_ge(loaded, 32)
            s.do(dve.tensor_tensor(part[:, :, :], edge_row[:, :, :].to_broadcast([P, NC, F]), spread(across[:, :]), ALU.mult))
            dve.wait_ge(got, 16 * NC)
            s.do(dve.tensor_tensor(agg[:, :, :], agg[:, :, :], part[:, :, :], ALU.add))
            s.do(dve.tensor_tensor(agg[:, :, :], agg[:, :, :], spread(has[:, :]), ALU.mult))
            s.do(dve.tensor_tensor(agg[:, :, :], agg[:, :, :], keep["loops"][:, :, :], ALU.add))
            dve.tensor_scalar(low[:, :, :], agg[:, :, :], 0.0, None, ALU.min).then_inc(lowered, 1)
            s.do(dve.tensor_scalar(agg[:, :, :], agg[:, :, :], 0.0, None, ALU.max))
            dve.wait_ge(tanhed, 1)
            s.do(dve.tensor_scalar(coeff[:, :], coeff[:, :], 2.0, None, ALU.add))
            for d in range(D4):
                s.mark(dve.tensor_scalar(part[:, :, H16 * d:H16 * d + H16], keep["x"][:, :, H16 * d:H16 * d + H16],
                                         coeff[:, d:d + 1], 1.0, ALU.mult, ALU.add))
            dve.wait_ge(dv, s.n)
            s.do(dve.tensor_tensor(part[:, :, :], part[:, :, :], agg[:, :, :], ALU.subtract))
            dve.wait_ge(grew, 1)
            s.do(dve.tensor_tensor(part[:, :, :], part[:, :, :], grown[:, :, :], ALU.subtract))
            norm_vector(dve, s, w, 1, part[:, :, :], keep["x"][:, :, :])

        @block.scalar
        def _(act):
            act.wait_ge(loaded, 32)
            act.activation(coeff[:, :], coeff[:, :], ACT.Tanh).then_inc(tanhed, 1)
            act.wait_ge(lowered, 1)
            act.activation(grown[:, :, :], low[:, :, :], ACT.Exp).then_inc(grew, 1)
            norm_scalar(act, w, 1)


def attention_phase(nc, io, dram, keep, out):
    with phase(nc, "at") as ph:
        SLOPE = 0.01
        rs = [ph.sb(f"rs{u}", [P, NP]) for u in range(2)]
        fT = rs[1][0:F, :]
        wa = ph.sb("wa", [F, 2])
        lin_w, lin_b = ph.sb("lin_w", [P, F]), ph.sb("lin_b", [P, F])
        src_all, src_low = ph.sb("src_all", [P, NP]), ph.sb("src_low", [P, N])
        catT = src_all
        col = ph.sb("col", [P, NC + 1])
        cat = ph.sb("cat", [P, NC, P])
        res = ph.sb("res", [P, NC, F])
        w = norm_scratch(ph)
        sm = Softmax(nc, ph, dram, "a", [(0, N)])
        sm.dv = ph.sem("peak_steps")
        v, pa, flat = sm.v, sm.pa, sm.flat
        (loaded, turned, copied, mm, low_made, relued, scored, dv, joined, back, normed, done) = (ph.sem(n) for n in (
            "loaded", "turned", "copied", "mm", "low_made", "relued", "scored", "dv", "joined", "back", "normed", "done"))
        block = ph.block()

        @block.sync
        def _(sp):
            sp.dma_start(wa[:, 0:1], io["L3_gnn_attn_w"][0:F, :]).then_inc(loaded, 16)
            sp.dma_start(wa[:, 1:2], io["L3_gnn_attn_w"][F:2 * F, :]).then_inc(loaded, 16)
            sp.dma_start(lin_w[:, :], io["lin_T"]).then_inc(loaded, 16)
            sp.dma_start(lin_b[:, :], row(io["L3_gnn_lin_b"]).to_broadcast([P, F])).then_inc(loaded, 16)
            sm.load(sp)
            sp.wait_ge(normed, 1)
            sp.dma_start(chunked(out, 0, FULL * P), keep["x"][:, 0:FULL, :]).then_inc(done, 16)
            sp.dma_start(out[FULL * P:N, :], keep["x"][0:REST, FULL, :]).then_inc(done, 16)
            sp.wait_ge(done, 32)

        @block.tensor
        def _(pe):
            for c in range(NC):
                ins = pe.transpose(flat[0:F, P * c:P * c + P], keep["x"][:, c, :], keep["ident"][:, :])
            ins.then_inc(turned, 1)
            pe.wait_ge(loaded, 64)
            pe.wait_ge(copied, 1)
            for c in range(NC):
                pe.matmul(pa[:, 7, c:c + 1], fT[:, P * c:P * c + P], wa[:, 1:2], start=True, stop=True)
            for k in range(0, NP, SW):
                m = min(SW, NP - k)
                ins = pe.matmul(flat[:, k:k + m], wa[:, 0:1].to_broadcast([F, P]), fT[:, k:k + m], start=True, stop=True)
            ins.then_inc(mm, 1)
            pe.wait_ge(copied, 2)
            pe.wait_ge(low_made, 1)
            pe.sem_inc(sm.summed, 2)
            sm.loop(pe, lambda c, u, more: sm.weigh(pe, keep["ident"][:, :], c, u))
            pe.wait_ge(sm.summed, NC + 2)
            pe.wait_ge(joined, 1)
            for c in range(NC):
                ins = pe.transpose(flat[:, P * c:P * c + P], cat[:, c, :], keep["ident"][:, :])
            ins.then_inc(back, 1)
            pe.wait_ge(copied, 3)
            for c in range(NC):
                ins = pe.matmul(flat[:, F * c:F * c + F], catT[:, P * c:P * c + P], lin_w[:, :], start=True, stop=True)
            ins.then_inc(back, 1)

        @block.vector
        def _(dve):
            dve.memset(v[:, :, F:AUG], 1.0)
            dve.memset(col[:, NC:NC + 1], 0.0)
            dve.tensor_copy(cat[:, :, 0:F], keep["x"][:, :, :])
            dve.tensor_copy(v[:, :, 0:F], keep["x"][:, :, :]).then_inc(sm.ready, 1)
            dve.wait_ge(turned, 1)
            dve.tensor_copy(fT, flat[0:F, 0:NP]).then_inc(copied, 1)
            dve.wait_ge(mm, 1)
            dve.tensor_copy(col[:, 0:NC], pa[:, 7, 0:NC])
            dve.tensor_copy(src_all[:, :], flat[:, 0:NP]).then_inc(copied, 1)
            dve.wait_ge(low_made, 1)
            sm.vector_counters(dve)

            def peak(c, u):
                dve.wait_ge(relued, c + 1)
                dve.scalar_tensor_tensor(rs[u][:, 0:N], rs[u][:, 0:N], 1.0 - SLOPE, src_low[:, :], ALU.mult, ALU.add
                                         ).then_inc(scored, 1)
                sm.vector_peak(dve, c, u, lambda b, lo, m: rs[u][:, lo:lo + m], scored)

            peak(0, 0)

            def body(c, u, more):
                if more:
                    peak(c + 1, 1 - u)
                sm.vector_odd(dve, c)
                sm.vector_out(dve, c, u)

            sm.loop(dve, body)
            s = Steps(dve, dv)
            sm.vector_mean(dve, s, cat[:, :, F:P])
            dve.wait_ge(dv, s.n)
            dve.sem_inc(joined, 1)
            dve.wait_ge(back, 1)
            dve.tensor_copy(catT[:, :], flat[:, 0:NP]).then_inc(copied, 1)
            dve.wait_ge(back, 2)
            s.do(dve.tensor_tensor(res[:, :, :], flat[:, 0:NC * F].rearrange("p (c f) -> p c f", f=F),
                                   lin_b[:, :].rearrange("p (o f) -> p o f", o=1).to_broadcast([P, NC, F]), ALU.add))
            s.do(dve.scalar_tensor_tensor(res[:, :, :], res[:, :, :], 0.0, keep["x"][:, :, :], ALU.max, ALU.add))
            norm_vector(dve, s, w, 1, res[:, :, :], keep["x"][:, :, :])
            dve.wait_ge(dv, s.n)
            dve.sem_inc(normed, 1)

        @block.scalar
        def _(act):
            act.wait_ge(mm, 1)
            act.wait_ge(copied, 2)
            act.activation(src_low[:, :], flat[:, 0:N], ACT.Copy, scale=SLOPE).then_inc(low_made, 1)
            relus = act.alloc_register("relus")
            act.reg_mov(relus, 0)

            def relu(c, u):
                act.activation(rs[u][:, 0:N], src_all[:, 0:N], ACT.Relu, bias=col[:, ds(c, 1)] if type(c) is not int
                               else col[:, c:c + 1]).then_inc(relued, 1)

            relu(0, 0)
            relu(1, 1)
            sm.scalar_exp(act, 0, 0)

            def body(c, u, more):
                if more:
                    act.reg_add(relus, relus, 1)
                    n = act.snap(relus)
                    act.wait_ge(mm, 1)
                    act.wait_ge(sm.peaked, n)
                    relu(c + 2, u)
                sm.scalar_even(act, c)
                if more:
                    sm.scalar_exp(act, c + 1, 1 - u)

            sm.loop(act, body)
            norm_scalar(act, w, 1)


def program(nc, io, out):
    def scratch(name, shape, dt=F32):
        return nc.dram_tensor(name, shape, dt, kind="Internal").ap()

    dram = {
        "table_src": scratch("table_src", (NP, M)), "table_dst": scratch("table_dst", (NP, M)),
        "counts": scratch("counts", (COUNTS + 4 * P, 1)), "runs": scratch("runs", (EP, 2 * M)),
        "logs": scratch("logs", (NP, N)),
        "sheaf_src": scratch("sheaf_src", (NP, WS)), "sheaf_dst": scratch("sheaf_dst", (NP, WD)),
        "spread": scratch("spread", (EP + NP, M)),
        "sums": scratch("sums", (EP, F)),
    }
    with ExitStack() as ctx:
        def sb(name, shape, dt=F32):
            return ctx.enter_context(nc.sbuf_tensor(name, shape, dt))

        keep = {n: sb(n, [P, NC]) for n in ("nid", "first", "last", "degree", "out_deg")}
        keep.update({n: sb(n, [P, T], I32) for n in ("src", "dst")})
        keep["last_idx"], keep["first_idx"] = sb("last_idx", [P, NC], I32), sb("first_idx", [P, NC], I32)
        keep["head_idx"] = sb("head_idx", [P, 1], I32)
        keep["ident"] = sb("ident", [P, P])
        keep["x"] = sb("x", [P, NC, F])
        with ExitStack() as ctx:
            keep["key"], keep["dump"], keep["earlier"] = sb("key", [P, T]), sb("dump", [P, 4]), sb("earlier", [P, 7 * P])
            setup_phase(nc, io, dram, keep)
            message_phase(nc, io, dram, keep)
        node_phase(nc, io, dram, keep)
        dense_phase(nc, io, dram, keep)
        with ExitStack() as ctx:
            keep["h"] = sb("h", [P, NC, F])
            for l in range(4):
                conv_phase(nc, io, dram, keep, l)
        with ExitStack() as ctx:
            keep["src_tab"], keep["dst_tab"] = sb("src_tab", [P, NC, WS]), sb("dst_tab", [P, NC, WD])
            keep["loops"] = sb("loops", [P, NC, F])
            sheaf_tables_phase(nc, io, dram, keep)
            sheaf_phase(nc, io, dram, keep)
            sheaf_node_phase(nc, io, dram, keep)
        attention_phase(nc, io, dram, keep, out)


SHAPE = (N, F)


def kernel(**inputs):
    import concourse.bacc as _bacc
    from concourse.bass_utils import run_bass_kernel_spmd as _run

    nc = _bacc.Bacc("TRN2", target_bir_lowering=False, num_devices=1)
    a = {k: np.ascontiguousarray(v) for k, v in inputs.items()}
    x, src, dst, attr = (a[k] for k in ("x", "src", "dst", "edge_attr_32"))
    node = np.full(EP, PAD_NODE, dst.dtype)
    node[:E] = dst
    of = np.full(EP, PAD_NODE, src.dtype)
    of[:E] = src
    feats = np.zeros((EP, M), attr.dtype)
    feats[:E] = attr
    arrays = {k: v for k, v in a.items() if k[0] == "L"}
    arrays["x"] = x
    arrays["xT"] = x.T
    arrays["src_pm"] = of.reshape(T, P).T
    arrays["dst_pm"] = node.reshape(T, P).T
    arrays["dst_tiles"] = node.reshape(T, P)
    arrays["dst_last"] = node.reshape(T, P)[:, P - 1]
    arrays["dst_heads"] = np.tile(node[::QE], P // 4)
    seq = np.full((4, QE + 1), -1, dst.dtype)
    seq[:, 1:] = node.reshape(4, QE)
    arrays["dst_seq"] = seq
    half = np.full((2, 2 * QE + 1), -1, dst.dtype)
    half[:, 1:] = node.reshape(2, 2 * QE)
    arrays["dst_half"] = half
    arrays["edge_T"] = feats.reshape(4, QE, M).transpose(0, 2, 1).reshape(4 * M, QE)
    arrays["mlp1_T"] = a["L2_gnn_mlp1_w"].T
    order = [0, 1, 3, 2, 4, 5]
    arrays["mlp2_T"] = a["L2_gnn_mlp2_w"][order].T
    arrays["mlp2_b"] = a["L2_gnn_mlp2_b"][order]
    arrays["lin_T"] = a["L3_gnn_lin_w"].T
    arrays = {k: np.ascontiguousarray(v) for k, v in arrays.items()}
    io = {k: nc.dram_tensor(f"in_{k}", v.shape, mybir.dt.from_np(v.dtype), kind="ExternalInput").ap()
          for k, v in arrays.items()}
    out = nc.dram_tensor("out", SHAPE, F32, kind="ExternalOutput").ap()
    program(nc, io, out)
    r = _run(nc, [{f"in_{k}": v for k, v in arrays.items()}], core_ids=[0])
    return r.results[0]["out"]
```

```python
from contextlib import ExitStack, contextmanager

import numpy as np

import concourse.bass as bass
from concourse import mybir
from concourse.alu_op_type import AluOpType as ALU

F32 = mybir.dt.float32
I32 = mybir.dt.int32
U32 = mybir.dt.uint32
BF16 = mybir.dt.bfloat16
ACT = mybir.ActivationFunctionType
AX = mybir.AxisListType
ds = bass.ds

P = 128
N = 3125
F = 64
M = 32
NC = -(-N // P)
NP = NC * P
FULL = N // P
REST = N - FULL * P
E = 100000
BLK = 512
NB = 50
QE = NB * BLK
EP = 4 * QE
T = EP // P
QT = T // 4
ST = BLK // P
PAD_NODE = N
COUNTS = NP * NP
DB = 448
ND = 7
BIG = 1e38
OFTEN = 4.0 * P * 2
OFF = 1e30
LN_EPS = 1e-5
assert ND * DB >= N and EP >= E and ND * DB <= NP


class Steps:

    def __init__(self, eng, sem, base=0):
        self.eng, self.sem, self.base, self.n = eng, sem, base, 0

    def mark(self, ins):
        ins.then_inc(self.sem, 1)
        self.n += 1

    def do(self, ins):
        self.mark(ins)
        self.eng.wait_ge(self.sem, self.base + self.n)


class Phase:

    def __init__(self, nc, ctx, name):
        self.nc, self.ctx, self.name = nc, ctx, name
        self.sems = []

    def sb(self, name, shape, dt=F32):
        return self.ctx.enter_context(self.nc.sbuf_tensor(f"{self.name}_{name}", shape, dt))

    def ps(self, name, shape, dt=F32):
        return self.ctx.enter_context(self.nc.psum_tensor(f"{self.name}_{name}", shape, dt))

    def sem(self, name):
        self.sems.append(self.nc.alloc_semaphore(f"{self.name}_{name}"))
        return self.sems[-1]

    def block(self):
        return self.ctx.enter_context(self.nc.Block())


@contextmanager
def phase(nc, name):
    with ExitStack() as ctx:
        ph = Phase(nc, ctx, name)
        yield ph
    nc.clear_and_free_semaphores(ph.sems)
    nc.all_engine_barrier()


def chunked(dram, lo=0, hi=NP):
    return dram[lo:hi, :].rearrange("(c p) f -> p c f", p=P)


def column(vec):
    return vec.rearrange("(p o) -> p o", o=1)


def row(vec):
    return vec.rearrange("(o n) -> o n", o=1)


def spread_to_edges(pool, dram, keep, rows, heads, stored, spread):
    for c in range(NC):
        pool.indirect_dma_start(dram["spread"], bass.IndirectOffsetOnAxis(keep["first_idx"][:, c:c + 1].bitcast(U32), 0),
                                rows[:, c, :], None).then_inc(spread, 16)
    pool.wait_ge(stored, 32)
    pool.indirect_dma_start(heads[:, :], None, dram["table_dst"],
                            bass.IndirectOffsetOnAxis(keep["head_idx"][:, 0:1].bitcast(U32), 0)).then_inc(spread, 16)
    pool.wait_ge(spread, 16 * (NC + 1))
    pool.dma_start(dram["spread"][0:EP, :].rearrange("(q e) f -> q e f", q=4)[:, 0, :], heads[0:4, :]).then_inc(spread, 16)
    pool.wait_ge(spread, 16 * (NC + 2))


def setup_phase(nc, io, dram, keep):
    with phase(nc, "su") as ph:
        xT = ph.sb("xT", [F, NP])
        wab = ph.sb("wab", [F, 2 * M])
        proj = ph.sb("proj", [P, NC, M])
        zeros = ph.sb("zeros", [P, 4000])
        tile_last_i = ph.sb("tile_last_i", [P, T], I32)
        tile_last = ph.sb("tile_last", [P, T])
        hits = ph.sb("hits", [P, T])
        bound_tile = ph.sb("bound_tile", [P, 2, NC])
        bound_idx = ph.sb("bound_idx", [P, 2, NC], I32)
        rows = ph.sb("rows", [P, 2, NC, P], I32)
        below = ph.sb("below", [P, 2, NC, P])
        in_row = ph.sb("in_row", [P, 2, NC])
        nid_i = ph.sb("nid_i", [P, NC], I32)
        dump_i = ph.sb("dump_i", [P, 4], I32)
        dst_rows = ph.sb("dst_rows", [P, NC, M])
        heads = ph.sb("heads", [P, M])
        away, has = ph.sb("away", [P, NC]), ph.sb("has", [P, NC])
        pp = ph.ps("pp", [P, 4, 512])
        cleared, loaded, projected = (ph.sem(n) for n in ("cleared", "loaded", "projected"))
        last_in, zeroed, got_rows, idx_ready, copied = (ph.sem(n) for n in ("last_in", "zeroed", "got_rows", "idx_ready", "copied"))
        stored, dv, po, first_ready, spread = (ph.sem(n) for n in ("stored", "dv", "po", "first_ready", "spread"))
        spread_zero = ph.sem("spread_zero")
        block = ph.block()

        @block.sync
        def _(sp):
            sp.dma_start(tile_last_i[:, :], row(io["dst_last"]).to_broadcast([P, T])).then_inc(last_in, 16)
            sp.dma_start(wab[:, 0:M], io["L0_gnn_W1"][0:F, :]).then_inc(loaded, 16)
            sp.dma_start(wab[:, M:2 * M], io["L0_gnn_W1"][F:2 * F, :]).then_inc(loaded, 16)
            sp.dma_start(keep["src"][:, :], io["src_pm"]).then_inc(loaded, 16)
            sp.dma_start(keep["dst"][:, :], io["dst_pm"]).then_inc(loaded, 16)
            sp.dma_start(keep["head_idx"][:, :], column(io["dst_heads"])).then_inc(loaded, 16)
            sp.wait_ge(cleared, 2)
            sp.dma_start(xT[:, 0:N], io["xT"]).then_inc(loaded, 16)
            sp.dma_start(keep["x"][:, 0:FULL, :], chunked(io["x"], 0, FULL * P)).then_inc(loaded, 16)
            sp.dma_start(keep["x"][0:REST, FULL, :], io["x"][FULL * P:N, :]).then_inc(loaded, 16)
            sp.wait_ge(copied, 1)
            sp.dma_start(chunked(dram["table_src"]), proj[:, :, :]).then_inc(stored, 16)
            sp.dma_start(chunked(dram["table_dst"]), dst_rows[:, :, :]).then_inc(stored, 16)
            sp.wait_ge(stored, 32)
            sp.wait_ge(loaded, 16 * 8)

        @block.scalar
        def _(act):
            act.wait_ge(cleared, 3)
            spread_d = dram["spread"][0:EP, :].rearrange("(p n) f -> p (n f)", p=P)
            for k in range(EP * M // P // 3200):
                act.dma_start(spread_d[:, 3200 * k:3200 * (k + 1)], zeros[:, 0:3200]).then_inc(spread_zero, 16)
            counts = dram["counts"][0:COUNTS, :].rearrange("(p n) o -> p (n o)", p=P)
            for k in range(COUNTS // P // 4000):
                act.dma_start(counts[:, 4000 * k:4000 * (k + 1)], zeros[:, :]).then_inc(zeroed, 16)
            act.dma_start(dram["counts"][COUNTS:COUNTS + 4 * P, :].rearrange("(p q) o -> p (q o)", p=P), zeros[:, 0:4]).then_inc(zeroed, 16)
            act.wait_ge(zeroed, 16 * (COUNTS // P // 4000 + 1))

        @block.gpsimd
        def _(pool):
            s = Steps(pool, po)
            pool.memset(keep["ident"][:, :], 0.0).then_inc(po, 1)
            pool.memset(keep["earlier"][:, 0:4 * P], OFTEN).then_inc(po, 1)
            pool.memset(keep["earlier"][:, 4 * P:7 * P], 1.0).then_inc(po, 1)
            s.n = 3
            pool.wait_ge(po, 3)
            s.mark(pool.affine_select(out=keep["ident"][:, :], in_=keep["ident"][:, :], compare_op=ALU.not_equal,
                                      fill=1.0, base=0, pattern=[[-1, P]], channel_multiplier=1))
            tri = keep["earlier"][:, 3 * P:4 * P]
            s.mark(pool.affine_select(out=tri, in_=tri, compare_op=ALU.is_gt,
                                      fill=1.0, base=0, pattern=[[-1, P]], channel_multiplier=1))
            s.mark(pool.iota(nid_i[:, :], [[P, NC]], 0, 1))
            s.mark(pool.iota(dump_i[:, :], [[P, 4]], COUNTS, 1))
            pool.wait_ge(idx_ready, 1)
            for k in range(2):
                for c in range(NC):
                    pool.indirect_dma_start(rows[:, k, c, :], None, io["dst_tiles"],
                                            bass.IndirectOffsetOnAxis(bound_idx[:, k, c:c + 1].bitcast(U32), 0)
                                            ).then_inc(got_rows, 16)
            pool.wait_ge(got_rows, 16 * 2 * NC)
            pool.wait_ge(spread_zero, 16 * (EP * M // P // 3200))
            pool.wait_ge(first_ready, 1)
            spread_to_edges(pool, dram, keep, dst_rows, heads, stored, spread)

        @block.tensor
        def _(pe):
            pe.wait_ge(loaded, 16 * 8)
            for c in range(NC):
                ins = pe.matmul(pp[:, c // 8, F * (c % 8):F * (c % 8 + 1)], xT[:, P * c:P * c + P], wab[:, :],
                                start=True, stop=True)
            ins.then_inc(projected, 1)

        @block.vector
        def _(dve):
            dve.memset(xT[:, :], 0.0).then_inc(cleared, 1)
            dve.memset(keep["x"][:, :, :], 0.0).then_inc(cleared, 1)
            dve.memset(zeros[:, :], 0.0).then_inc(cleared, 1)
            s = Steps(dve, dv)
            dve.wait_ge(last_in, 16)
            dve.wait_ge(po, 7)
            s.mark(dve.tensor_copy(tile_last[:, :], tile_last_i[:, :]))
            s.mark(dve.tensor_copy(keep["dump"][:, :], dump_i[:, :]))
            s.do(dve.tensor_copy(keep["nid"][:, :], nid_i[:, :]))
            for k, op in enumerate((ALU.is_lt, ALU.is_le)):
                for c in range(NC):
                    s.do(dve.tensor_scalar(hits[:, :], tile_last[:, :], keep["nid"][:, c:c + 1], None, op, ALU.add,
                                           accum_out=bound_tile[:, k, c:c + 1]))
            s.do(dve.tensor_scalar(bound_tile[:, :, :], bound_tile[:, :, :], float(T - 1), None, ALU.min))
            dve.tensor_copy(bound_idx[:, :, :], bound_tile[:, :, :]).then_inc(idx_ready, 1)
            dve.wait_ge(loaded, 16 * 8)
            s.mark(dve.scalar_tensor_tensor(keep["key"][:, :], keep["dst"][:, :], float(NP), keep["src"][:, :],
                                            ALU.mult, ALU.add))
            dve.wait_ge(projected, 1)
            for b in range(4):
                w = min(8, NC - 8 * b)
                of = pp[:, b, 0:F * w].rearrange("p (c f) -> p c f", f=F)
                dve.tensor_copy(dst_rows[:, 8 * b:8 * b + w, :], of[:, :, M:2 * M])
                ins = dve.tensor_copy(proj[:, 8 * b:8 * b + w, :], of[:, :, 0:M])
            ins.then_inc(copied, 1)
            dve.wait_ge(got_rows, 16 * 2 * NC)
            for k, op in enumerate((ALU.is_lt, ALU.is_le)):
                s.mark(dve.tensor_tensor(below[:, k, :, :], rows[:, k, :, :],
                                         keep["nid"][:, :].rearrange("p (c o) -> p c o", o=1).to_broadcast([P, NC, P]), op))
            dve.wait_ge(dv, s.n)
            for k in range(2):
                s.mark(dve.tensor_reduce(in_row[:, k, :], below[:, k, :, :], AX.X, ALU.add))
            dve.wait_ge(dv, s.n)
            for k, out in enumerate((keep["first"], keep["last"])):
                s.mark(dve.scalar_tensor_tensor(out[:, :], bound_tile[:, k, :], float(P), in_row[:, k, :],
                                                ALU.mult, ALU.add))
            dve.wait_ge(dv, s.n)
            s.mark(dve.tensor_tensor(keep["degree"][:, :], keep["last"][:, :], keep["first"][:, :], ALU.subtract))
            s.do(dve.tensor_scalar(keep["last"][:, :], keep["last"][:, :], -1.0, None, ALU.add))
            s.mark(dve.tensor_scalar(keep["last_idx"][:, :], keep["last"][:, :], 0.0, None, ALU.max))
            s.mark(dve.tensor_scalar(away[:, :], keep["nid"][:, :], float(EP), None, ALU.add))
            s.do(dve.tensor_scalar(has[:, :], keep["degree"][:, :], 0.0, None, ALU.is_gt))
            s.do(dve.tensor_tensor(bound_tile[:, 0, :], keep["first"][:, :], away[:, :], ALU.subtract))
            s.do(dve.tensor_tensor(bound_tile[:, 0, :], bound_tile[:, 0, :], has[:, :], ALU.mult))
            dve.tensor_tensor(keep["first_idx"][:, :], bound_tile[:, 0, :], away[:, :], ALU.add).then_inc(first_ready, 1)


def message_phase(nc, io, dram, keep):
    with phase(nc, "ms") as ph:
        w1 = ph.sb("w1", [P, P])
        w2 = ph.sb("w2", [P, P])
        w3 = ph.sb("w3", [P, P])
        b1 = ph.sb("b1", [P, 1])
        b2 = ph.sb("b2", [P, 1])
        b3 = ph.sb("b3", [P, 1])
        attr = [ph.sb(f"attr{u}", [P, BLK]) for u in range(2)]
        seq = [ph.sb(f"seq{u}", [P, BLK + 1], I32) for u in range(2)]
        st_src = [ph.sb(f"st_src{u}", [P, ST, 4], I32) for u in range(2)]
        st_key = [ph.sb(f"st_key{u}", [P, ST, 4]) for u in range(2)]
        place = [ph.sb(f"place{u}", [P, ST * 4], I32) for u in range(2)]
        mult = [ph.sb(f"mult{u}", [P, ST * 4]) for u in range(2)]
        lead = ph.sb("lead", [P, ST * 4])
        moved = ph.sb("moved", [P, ST * 4])
        same = ph.sb("same", [P, 4, 4 * P], BF16)
        got_s = [ph.sb(f"got_s{u}", [P, ST, 4, M]) for u in range(2)]
        first_rows = [ph.sb(f"first_rows{u}", [P, ST, 4, M]) for u in range(2)]
        of_dst = [ph.sb(f"of_dst{u}", [P, BLK]) for u in range(2)]
        h1 = ph.sb("h1", [P, BLK])
        h2 = ph.sb("h2", [P, BLK])
        h3 = ph.sb("h3", [P, BLK])
        cont = [ph.sb(f"cont{u}", [P, BLK]) for u in range(2)]
        gate = [ph.sb(f"gate{u}", [P, BLK]) for u in range(2)]
        run_sum = [ph.sb(f"run_sum{u}", [P, BLK]) for u in range(2)]
        run_max = [ph.sb(f"run_max{u}", [P, BLK]) for u in range(2)]
        out_t = ph.sb("out_t", [P, ST, 4, 2 * M])
        p1, p2, p3, pts, ptm, pd = (ph.ps(n, [P, BLK]) for n in ("p1", "p2", "p3", "pts", "ptm", "pd"))
        pkey = [ph.ps(f"pkey{u}", [P, 4, P]) for u in range(2)]
        wz, weights, staged, keyed, keyfree, placed = (ph.sem(n) for n in ("wz", "weights", "staged", "keyed", "keyfree", "placed"))
        multiplied, mm1, mm2, mm3, act1, act2, act3 = (ph.sem(n) for n in ("multiplied", "mm1", "mm2", "mm3", "act1", "act2", "act3"))
        scanned, turned, masked, turned_out, out_st = (ph.sem(n) for n in ("scanned", "turned", "masked", "turned_out", "out_st"))
        counted, dv, ds0, rows_turned, spread = (ph.sem(n) for n in ("counted", "dv", "ds0", "rows_turned", "spread"))
        rows_in = [ph.sem(f"rows_in{u}") for u in range(2)]
        attr_in = [ph.sem(f"attr_in{u}") for u in range(2)]
        seq_in = [ph.sem(f"seq_in{u}") for u in range(2)]
        got = [[ph.sem(f"got{u}_{i}") for i in range(ST)] for u in range(2)]
        block = ph.block()

        attr_d = io["edge_T"]
        seq_d = io["dst_seq"]
        spread_d = dram["spread"][0:EP, :].rearrange("(q b i p) f -> q b p i f", q=4, b=NB, i=ST)
        quarter = dram["runs"].rearrange("(q b i p) f -> q b p i f", q=4, b=NB, i=ST)

        def loop(eng, body):
            with eng.Fori(0, NB // 2 - 1) as it:
                body(it, False)
            body(NB // 2 - 1, True)

        @block.sync
        def _(sp):
            sp.wait_ge(wz, 1)
            k = 0
            for q in range(4):
                lo = M * q
                for w, b, ww, bb in ((w1, b1, io["L0_gnn_W1"][2 * F:2 * F + M, :], "L0_gnn_b1"),
                                     (w2, b2, io["L0_gnn_W2"], "L0_gnn_b2"), (w3, b3, io["L0_gnn_W3"], "L0_gnn_b3")):
                    sp.dma_start(w[lo:lo + M, lo:lo + M], ww).then_inc(weights, 16)
                    sp.dma_start(b[lo:lo + M, :], column(io[bb])).then_inc(weights, 16)
                    k += 2
            assert k == 24

            def load(b, at, u):
                for q in range(4):
                    sp.dma_start(first_rows[u][:, :, q, :], spread_d[q, b]).then_inc(rows_in[u], 16)
                sp.dma_start(attr[u][:, :], attr_d[:, ds(at, BLK)]).then_inc(attr_in[u], 16)
                for q in range(4):
                    sp.dma_start(seq[u][M * q:M * q + M, :],
                                 seq_d[q:q + 1, ds(at, BLK + 1)].to_broadcast([M, BLK + 1])).then_inc(seq_in[u], 16)

            load(0, 0, 0)
            load(1, BLK, 1)
            at, done = sp.alloc_register("edges_loaded"), sp.alloc_register("blocks_done")
            sp.reg_mov(at, BLK)
            sp.reg_mov(done, 0)
            with sp.Fori(0, NB // 2 - 1):
                for u in range(2):
                    sp.reg_add(at, at, BLK)
                    sp.reg_add(done, done, 1)
                    blocks = sp.snap(done)
                    sp.wait_ge(wz, 1)
                    sp.wait_ge(multiplied, blocks)
                    sp.wait_ge(masked, blocks)
                    sp.wait_ge(rows_turned, blocks)
                    load(blocks + 1, sp.snap(at), u)
            sp.wait_ge(weights, 16 * 24)

        @block.gpsimd
        def _(pool):
            turn = pool.alloc_register("block_turn")
            sent = pool.alloc_register("tiles_counted")
            pool.reg_mov(turn, 0)
            pool.reg_mov(sent, 0)

            def body(it, last):
                for u in range(2):
                    pool.reg_add(turn, turn, 1)
                    now = pool.snap(turn)
                    pool.wait_ge(ds0, 1)
                    pool.wait_ge(placed, now)
                    pool.wait_ge(mm1, now)
                    for i in range(ST):
                        for q in range(4):
                            j = 4 * i + q
                            pool.indirect_dma_start(
                                dram["counts"], bass.IndirectOffsetOnAxis(place[u][:, j:j + 1].bitcast(U32), 0),
                                mult[u][:, j:j + 1], None, compute_op=ALU.add).then_inc(counted, 16)
                        for q in range(4):
                            pool.indirect_dma_start(
                                got_s[u][:, i, q, :], None, dram["table_src"],
                                bass.IndirectOffsetOnAxis(st_src[u][:, i, q:q + 1].bitcast(U32), 0)).then_inc(got[u][i], 16)
                        pool.reg_add(sent, sent, 64)
                        so_far = pool.snap(sent)
                        pool.wait_ge(ds0, 1)
                        pool.wait_ge(counted, so_far)

            with pool.Fori(0, NB // 2) as it:
                body(it, False)

        @block.vector
        def _(dve):
            for w in (w1, w2, w3):
                ins = dve.memset(w[:, :], 0.0)
            ins.then_inc(wz, 1)
            dve.memset(run_sum[1][:, :], 0.0)
            dve.memset(of_dst[1][:, :], 0.0)
            dve.memset(run_max[1][:, :], 0.0).then_inc(ds0, 1)
            dve.wait_ge(ds0, 1)

            def stage(b, u):
                for st, of in ((st_src, "src"), (st_key, "key")):
                    ins = dve.tensor_copy(st[u][:, :, :].rearrange("p i q -> p q i"),
                                          keep[of][:, :].rearrange("p (q t) -> p q t", q=4)[:, :, ds(b * ST, ST)])
                ins.then_inc(staged, 1)

            def places(b, u, s):
                dve.wait_ge(staged, b + 1)
                for i in range(ST):
                    dve.wait_ge(keyed, ST * b + i + 1)
                    for q in range(4):
                        ins = dve.scalar_tensor_tensor(
                            same[:, q, :], pkey[i % 2][:, :, :].rearrange("p q n -> p (q n)"), st_key[u][:, i, q:q + 1],
                            keep["earlier"][:, (3 - q) * P:(7 - q) * P], ALU.is_equal, ALU.mult,
                            accum_out=mult[u][:, 4 * i + q:4 * i + q + 1])
                    s.do(ins)
                    dve.sem_inc(keyfree, 1)
                keys, spare = st_key[u][:, :, :], keep["dump"][:, :].rearrange("p (o q) -> p o q", o=1).to_broadcast([P, ST, 4])
                far = moved[:, :].rearrange("p (i q) -> p i q", q=4)
                s.mark(dve.tensor_scalar(lead[:, :], mult[u][:, :], OFTEN, None, ALU.is_lt))
                s.do(dve.tensor_tensor(far, keys, spare, ALU.subtract))
                s.do(dve.tensor_tensor(moved[:, :], moved[:, :], lead[:, :], ALU.mult))
                dve.tensor_tensor(place[u][:, :].rearrange("p (i q) -> p i q", q=4), far, spare, ALU.add).then_inc(placed, 1)

            def along(b, u, s, it):
                dve.wait_ge(seq_in[u], it * 64 + 64)
                s.do(dve.tensor_tensor(cont[u][:, :], seq[u][:, 1:BLK + 1], seq[u][:, 0:BLK], ALU.is_equal))
                s.do(dve.tensor_scalar(gate[u][:, :], cont[u][:, :], BIG, -BIG, ALU.mult, ALU.add))
                dve.sem_inc(masked, 1)
                dve.wait_ge(rows_turned, b + 1)
                dve.tensor_tensor_scan(of_dst[u][:, :], cont[u][:, :], pd[:, :], of_dst[1 - u][:, BLK - 1:BLK],
                                       ALU.mult, ALU.add).then_inc(spread, 1)
                dve.wait_ge(spread, b + 1)

            def scans(b, u):
                dve.wait_ge(act3, b + 1)
                dve.tensor_tensor_scan(run_sum[u][:, :], cont[u][:, :], h3[:, :], run_sum[1 - u][:, BLK - 1:BLK],
                                       ALU.mult, ALU.add)
                dve.tensor_tensor_scan(run_max[u][:, :], gate[u][:, :], h3[:, :], run_max[1 - u][:, BLK - 1:BLK],
                                       ALU.add, ALU.max).then_inc(scanned, 1)
                dve.wait_ge(scanned, b + 1)

            PER = ST + 3 + 2
            stage(0, 0)
            s0 = Steps(dve, dv)
            places(0, 0, s0)
            along(0, 0, s0, 0)
            assert s0.n == PER

            def body(it, last):
                for u in range(2):
                    b = it * 2 + u
                    if not (last and u == 1):
                        s = Steps(dve, dv, (b + 1) * PER)
                        stage(b + 1, 1 - u)
                        places(b + 1, 1 - u, s)
                        along(b + 1, 1 - u, s, it + u)
                        assert s.n == PER
                    scans(b, u)
                    dve.wait_ge(counted, (b + 1) * 16 * 4 * ST)

            loop(dve, body)

        @block.tensor
        def _(pe):
            pe.sem_inc(mm1, 2)
            pe.wait_ge(weights, 16 * 24)

            def keys(b, u):
                pe.wait_ge(staged, b + 1)
                for i in range(ST):
                    pe.wait_ge(keyfree, ST * b + i + 1)
                    for q in range(4):
                        ins = pe.matmul(pkey[i % 2][:, q, :], st_key[u][:, i, q:q + 1].to_broadcast([P, P]),
                                        keep["ident"][:, :], start=True, stop=True)
                    ins.then_inc(keyed, 1)

            def turn_rows(b, u, it):
                pe.wait_ge(rows_in[u], it * 64 + 64)
                for i in range(ST):
                    ins = pe.transpose(pd[:, P * i:P * i + P], first_rows[u][:, i, :, :].rearrange("p q m -> p (q m)"),
                                       keep["ident"][:, :])
                ins.then_inc(rows_turned, 1)

            pe.sem_inc(keyfree, 2)
            keys(0, 0)
            turn_rows(0, 0, 0)

            def body(it, last):
                for u in range(2):
                    b = it * 2 + u
                    if not (last and u == 1):
                        keys(b + 1, 1 - u)
                        pe.wait_ge(spread, b + 1)
                        turn_rows(b + 1, 1 - u, it + u)
                    pe.wait_ge(attr_in[u], it * 16 + 16)
                    pe.matmul(p1[:, :], w1[:, :], attr[u][:, :], start=True, stop=False).then_inc(multiplied, 1)
                    pe.wait_ge(spread, b + 1)
                    pe.matmul(p1[:, :], keep["ident"][:, :], of_dst[u][:, :], start=False, stop=False)
                    for i in range(ST):
                        pe.wait_ge(got[u][i], it * 64 + 64)
                        ins = pe.matmul(p1[:, P * i:P * i + P], got_s[u][:, i, :, :].rearrange("p q m -> p (q m)"),
                                        keep["ident"][:, :], start=False, stop=(i == ST - 1))
                    ins.then_inc(mm1, 1)
                    pe.wait_ge(act1, b + 1)
                    pe.matmul(p2[:, :], w2[:, :], h1[:, :], start=True, stop=True).then_inc(mm2, 1)
                    pe.wait_ge(act2, b + 1)
                    pe.matmul(p3[:, :], w3[:, :], h2[:, :], start=True, stop=True).then_inc(mm3, 1)
                    pe.wait_ge(scanned, b + 1)
                    for of, to in ((run_sum, pts), (run_max, ptm)):
                        for i in range(ST):
                            ins = pe.transpose(to[:, P * i:P * i + P], of[u][:, P * i:P * i + P], keep["ident"][:, :])
                    ins.then_inc(turned, 1)

            loop(pe, body)

        @block.scalar
        def _(act):
            act.wait_ge(weights, 16 * 24)

            def body(it, last):
                for u in range(2):
                    b = it * 2 + u
                    act.wait_ge(mm1, b + 3)
                    act.activation(h1[:, :], p1[:, :], ACT.Relu, bias=b1[:, 0:1]).then_inc(act1, 1)
                    act.wait_ge(mm2, b + 1)
                    act.activation(h2[:, :], p2[:, :], ACT.Relu, bias=b2[:, 0:1]).then_inc(act2, 1)
                    act.wait_ge(mm3, b + 1)
                    act.activation(h3[:, :], p3[:, :], ACT.Identity, bias=b3[:, 0:1]).then_inc(act3, 1)
                    act.wait_ge(turned, b + 1)
                    for of, lo in ((pts, 0), (ptm, M)):
                        ins = act.activation(out_t[:, :, :, lo:lo + M],
                                             of[:, :].rearrange("p (i q m) -> p i q m", i=ST, q=4), ACT.Copy)
                    ins.then_inc(turned_out, 1)
                    act.wait_ge(turned_out, b + 1)
                    for q in range(4):
                        act.dma_start(quarter[q, b], out_t[:, :, q, :]).then_inc(out_st, 16)
                    act.wait_ge(out_st, b * 64 + 64)

            with act.Fori(0, NB // 2) as it:
                body(it, False)


def spread(col, f=F):
    return col.rearrange("p (c o) -> p c o", o=1).to_broadcast([P, NC, f])


def norm_scratch(ph):
    w = {k: ph.sb(f"ln_{k}", [P, NC]) for k in ("mean", "var", "dev", "rstd")}
    w["mid"], w["square"] = (ph.sb(f"ln_{k}", [P, NC, F]) for k in ("mid", "square"))
    w["has_var"], w["has_dev"] = ph.sem("ln_has_var"), ph.sem("ln_has_dev")
    return w


def norm_vector(dve, s, w, k, x, out):
    s.do(dve.tensor_reduce(w["mean"][:, :], x, AX.X, ALU.add))
    s.do(dve.tensor_scalar(w["mean"][:, :], w["mean"][:, :], 1.0 / F, None, ALU.mult))
    s.do(dve.tensor_tensor(w["mid"][:, :, :], x, spread(w["mean"][:, :]), ALU.subtract))
    s.do(dve.tensor_tensor(w["square"][:, :, :], w["mid"][:, :, :], w["mid"][:, :, :], ALU.mult))
    s.do(dve.tensor_reduce(w["var"][:, :], w["square"][:, :, :], AX.X, ALU.add))
    dve.tensor_scalar(w["var"][:, :], w["var"][:, :], 1.0 / F, LN_EPS, ALU.mult, ALU.add).then_inc(w["has_var"], 1)
    dve.wait_ge(w["has_dev"], k)
    s.do(dve.reciprocal(w["rstd"][:, :], w["dev"][:, :]))
    s.mark(dve.tensor_tensor(out, w["mid"][:, :, :], spread(w["rstd"][:, :]), ALU.mult))


def norm_scalar(act, w, k):
    act.wait_ge(w["has_var"], k)
    act.activation(w["dev"][:, :], w["var"][:, :], ACT.Sqrt).then_inc(w["has_dev"], 1)


def node_phase(nc, io, dram, keep):
    with phase(nc, "nd") as ph:
        runs = ph.sb("runs", [P, NC, 2 * M])
        edge_rows = ph.sb("edge_rows", [P, 3, 2 * M])
        across = ph.sb("across", [P, 3, NC])
        off = ph.sb("off", [P, NC])
        part = ph.sb("part", [P, NC, 2 * M])
        has, inv = ph.sb("has", [P, NC]), ph.sb("inv", [P, NC])
        cat = ph.sb("cat", [P, NC, P])
        catT = ph.sb("catT", [P, NP])
        w4, w4u = ph.sb("w4", [P, M]), ph.sb("w4u", [M, M])
        w5, w6 = ph.sb("w5", [M, M]), ph.sb("w6", [M + 1, F])
        u0, b4, b5 = ph.sb("u0", [M, 1]), ph.sb("b4", [M, 1]), ph.sb("b5", [M, 1])
        b4u = ph.sb("b4u", [M, 1])
        a4, a5 = ph.sb("a4", [M, NP]), ph.sb("a5", [M + 1, NP])
        res = ph.sb("res", [P, NC, F])
        w = norm_scratch(ph)
        pt = ph.ps("pt", [P, 7 * 512])
        pu = ph.ps("pu", [P, 512])
        loaded, got, joined, turned, copied, mm, acted, dv, rows_in = (ph.sem(n) for n in (
            "loaded", "got", "joined", "turned", "copied", "mm", "acted", "dv", "rows_in"))
        block = ph.block()
        ends = [QE * (q + 1) - 1 for q in range(3)]

        @block.sync
        def _(sp):
            for q, e in enumerate(ends):
                sp.dma_start(edge_rows[:, q, :], dram["runs"][e:e + 1, :].to_broadcast([P, 2 * M])).then_inc(rows_in, 16)
            w4_d = io["L0_gnn_W4"]
            sp.dma_start(w4[:, :], w4_d[0:P, :]).then_inc(loaded, 16)
            sp.dma_start(w4u[:, :], w4_d[P:P + M, :]).then_inc(loaded, 16)
            sp.dma_start(w5[:, :], io["L0_gnn_W5"]).then_inc(loaded, 16)
            sp.dma_start(w6[0:M, :], io["L0_gnn_W6"]).then_inc(loaded, 16)
            sp.dma_start(w6[M:M + 1, :], row(io["L0_gnn_b6"])).then_inc(loaded, 16)
            sp.dma_start(u0[:, :], column(io["L0_gnn_u"][0, :])).then_inc(loaded, 16)
            sp.dma_start(b4[:, :], column(io["L0_gnn_b4"])).then_inc(loaded, 16)
            sp.dma_start(b5[:, :], column(io["L0_gnn_b5"])).then_inc(loaded, 16)

        @block.gpsimd
        def _(pool):
            for c in range(NC):
                pool.indirect_dma_start(runs[:, c, :], None, dram["runs"],
                                        bass.IndirectOffsetOnAxis(keep["last_idx"][:, c:c + 1].bitcast(U32), 0)).then_inc(got, 16)

        @block.vector
        def _(dve):
            s = Steps(dve, dv)
            s.mark(dve.memset(a5[M:M + 1, :], 1.0))
            for q, e in enumerate(ends):
                s.do(dve.tensor_scalar(across[:, q, :], keep["first"][:, :], float(e), None, ALU.is_le))
                s.do(dve.scalar_tensor_tensor(across[:, q, :], keep["last"][:, :], float(e), across[:, q, :],
                                              ALU.is_gt, ALU.mult))
            s.do(dve.tensor_scalar(inv[:, :], keep["degree"][:, :], 1.0, None, ALU.max))
            s.do(dve.reciprocal(inv[:, :], inv[:, :]))
            s.do(dve.tensor_scalar(has[:, :], keep["degree"][:, :], 0.0, None, ALU.is_gt))
            s.do(dve.tensor_tensor(inv[:, :], inv[:, :], has[:, :], ALU.mult))
            s.mark(dve.tensor_copy(cat[:, :, 0:F], keep["x"][:, :, :]))
            dve.wait_ge(rows_in, 48)
            dve.wait_ge(got, 16 * NC)
            for q in range(3):
                s.do(dve.tensor_scalar(off[:, :], across[:, q, :], BIG, -BIG, ALU.mult, ALU.add))
                s.do(dve.tensor_tensor(part[:, :, :], edge_rows[:, q:q + 1, :].to_broadcast([P, NC, 2 * M]),
                                       spread(across[:, q, :]), ALU.mult))
                s.do(dve.tensor_tensor(part[:, :, M:2 * M], part[:, :, M:2 * M], spread(off[:, :], M), ALU.add))
                s.do(dve.tensor_tensor(runs[:, :, 0:M], runs[:, :, 0:M], part[:, :, 0:M], ALU.add))
                s.do(dve.tensor_tensor(runs[:, :, M:2 * M], runs[:, :, M:2 * M], part[:, :, M:2 * M], ALU.max))
            s.do(dve.tensor_tensor(cat[:, :, F:F + M], runs[:, :, 0:M], spread(inv[:, :], M), ALU.mult))
            dve.tensor_tensor(cat[:, :, F + M:P], runs[:, :, M:2 * M], spread(has[:, :], M), ALU.mult).then_inc(joined, 1)
            dve.wait_ge(turned, 1)
            dve.tensor_copy(catT[:, :], pt[:, 0:NP]).then_inc(copied, 1)
            dve.wait_ge(loaded, 16 * 8)
            dve.wait_ge(mm, 1)
            dve.tensor_tensor(b4u[:, :], pu[0:M, 0:1], b4[:, :], ALU.add).then_inc(copied, 1)
            dve.wait_ge(mm, 4)
            s.do(dve.tensor_tensor(res[:, :, :].rearrange("p c f -> p (c f)"), pt[:, 0:NC * F],
                                   keep["x"][:, :, :].rearrange("p c f -> p (c f)"), ALU.add))
            norm_vector(dve, s, w, 1, res[:, :, :], keep["x"][:, :, :])

        @block.tensor
        def _(pe):
            pe.wait_ge(joined, 1)
            for c in range(NC):
                ins = pe.transpose(pt[:, P * c:P * c + P], cat[:, c, :], keep["ident"][:, :])
            ins.then_inc(turned, 1)
            pe.wait_ge(loaded, 16 * 8)
            pe.matmul(pu[0:M, 0:1], w4u[:, :], u0[:, :], start=True, stop=True).then_inc(mm, 1)

            def product(weight, of, rows_, m):
                for k in range(0, NP, 512):
                    n = min(512, NP - k)
                    ins = pe.matmul(pt[0:m, k:k + n], weight, of[0:rows_, k:k + n], start=True, stop=True)
                ins.then_inc(mm, 1)

            pe.wait_ge(copied, 2)
            product(w4[:, :], catT, P, M)
            pe.wait_ge(acted, 1)
            product(w5[:, :], a4, M, M)
            pe.wait_ge(acted, 2)
            for c in range(NC):
                ins = pe.matmul(pt[:, F * c:F * c + F], a5[:, P * c:P * c + P], w6[:, :], start=True, stop=True)
            ins.then_inc(mm, 1)

        @block.scalar
        def _(act):
            act.wait_ge(copied, 2)
            act.wait_ge(mm, 2)
            act.activation(a4[:, :], pt[0:M, 0:NP], ACT.Relu, bias=b4u[:, 0:1]).then_inc(acted, 1)
            act.wait_ge(dv, 1)
            act.wait_ge(mm, 3)
            act.activation(a5[0:M, :], pt[0:M, 0:NP], ACT.Relu, bias=b5[:, 0:1]).then_inc(acted, 1)
            norm_scalar(act, w, 1)


SW = 512
NS = -(-N // SW)
NG = -(-NC // 4)
BLOCKS = [(SW * b, min(SW, N - SW * b)) for b in range(NS)]
GROUPS = [[(k, min(P, N - P * k)) for k in range(4 * g, min(4 * g + 4, NC))] for g in range(NG)]
HALVES = [(0, 3 * SW), (3 * SW, N)]
AUG = F + 1


class Softmax:

    def __init__(self, nc, ph, dram, l, ring, ahead, counts=False):
        self.l, self.ring, self.ahead, self.counts = l, ring, ahead, counts
        self.buffers = 4 if counts else 2
        self.unroll = max(ring, self.buffers)
        self.counts_d = dram["counts"][0:COUNTS, :].rearrange("(c p s) o -> c p (s o)", p=P, s=NP)[:, :, 0:N]
        self.logs_d = dram["logs"].rearrange("(c p) s -> c p s", p=P)
        self.logs = [ph.sb(f"logs{k}", [P, N]) for k in range(self.buffers)]
        self.xs = [ph.sb(f"xs{u}", [P, N]) for u in range(ring)]
        self.esT = ph.sb("esT", [P, NC, P])
        self.v = ph.sb("v", [P, NC, AUG])
        self.sums = ph.sb("sums", [P, NC * AUG])
        self.den = ph.sb("den", [P, NC])
        self.peaks = ph.sb("peaks", [P, NS])
        self.neg = [ph.sb(f"neg{u}", [P, 1]) for u in range(2)]
        self.pa = ph.ps("pa", [P, 8, SW])
        self.flat = self.pa[:, :, :].rearrange("p b n -> p (b n)")
        self.logs_in = [ph.sem(f"logs_in{k}") for k in range(self.buffers)]
        if counts:
            self.tiny, self.ones = ph.sb("tiny", [P, 1]), ph.sb("ones", [P, 1])
            self.leaving = ph.sb("leaving", [P, N])
            self.rows_summed, self.logged, self.evened = (ph.sem(n) for n in ("rows_summed", "logged", "evened"))
            self.stored = [ph.sem(f"stored{k}") for k in range(self.buffers)]
        self.ready, self.peaked, self.negated, self.exped, self.turned_es, self.even, self.odd, self.weighed, self.summed = (
            ph.sem(n) for n in ("ready", "peaked", "negated", "exped", "turned_es", "even", "odd", "weighed", "summed"))

    def loop(self, eng, body):
        turns = (NC - self.ahead) // self.unroll
        with eng.Fori(0, turns) as it:
            for i in range(self.unroll):
                body(it * self.unroll + i, i)
        for c in range(turns * self.unroll, NC):
            body(c, c % self.unroll)

    def has(self, c):
        return type(c) is not int or c < NC

    def load(self, sp):
        of, n = (self.counts_d if self.counts else self.logs_d), self.buffers
        for k in range(n):
            sp.dma_start(self.logs[k][:, :], of[k]).then_inc(self.logs_in[k], 16)
        used, done, stores = (sp.alloc_register(f"{name}{self.l}") for name in ("logs_used", "chunks_done", "logs_stored"))
        sp.reg_mov(used, 0)
        sp.reg_mov(done, 0)
        sp.reg_mov(stores, 0)

        def again(k, more=True):
            sp.reg_add(used, used, NS)
            sp.reg_add(done, done, 1)
            n_used, n_done = sp.snap(used), sp.snap(done)
            if self.counts:
                if k == 0:
                    sp.reg_add(stores, stores, 16)
                n_stored = sp.snap(stores)
                sp.wait_ge(self.ready, 1)
                sp.wait_ge(self.evened, n_done * 2)
                sp.dma_start(self.logs_d[n_done - 1], self.logs[k][:, :]).then_inc(self.stored[k], 16)
            if more:
                sp.wait_ge(self.ready, 1)
                sp.wait_ge(self.peaked, n_used)
                if self.counts:
                    sp.wait_ge(self.stored[k], n_stored)
                sp.dma_start(self.logs[k][:, :], of[n_done + (n - 1)]).then_inc(self.logs_in[k], 16)

        with sp.Fori(0, (NC - n) // n):
            for k in range(n):
                again(k)
        for c in range((NC - n) // n * n, NC):
            if c + n < NC:
                again(c % n)
            elif self.counts:
                again(c % n, more=False)
        if self.counts:
            for k in range(n):
                sp.wait_ge(self.stored[k], 16 * len(range(k, NC, n)))

    def pool_sums(self, pool):
        pool.wait_ge(self.ready, 1)
        pool.sem_inc(self.rows_summed, 1)
        turn, loads = pool.alloc_register("sum_turn"), pool.alloc_register("sum_loads")
        pool.reg_mov(turn, 0)
        pool.reg_mov(loads, 0)

        def body(c, i):
            pool.reg_add(turn, turn, 1)
            if i == 0:
                pool.reg_add(loads, loads, 16)
            now, n_in = pool.snap(turn), pool.snap(loads)
            pool.wait_ge(self.ready, 1)
            pool.wait_ge(self.rows_summed, now)
            pool.wait_ge(self.logs_in[i], n_in)
            pool.tensor_tensor(self.leaving[:, :], self.leaving[:, :], self.logs[i][:, :], ALU.add).then_inc(self.rows_summed, 1)

        self.loop(pool, body)

    def leave(self, pe):
        pe.wait_ge(self.rows_summed, NC + 1)
        pe.wait_ge(self.summed, NC + 2)
        for k in range(NC):
            m = min(P, N - P * k)
            ins = pe.matmul(self.pa[0:m, 7, P + k:P + k + 1], self.leaving[:, P * k:P * k + m], self.ones[:, :],
                            start=True, stop=True)
        ins.then_inc(self.weighed, 1)

    def scalar_logs(self, act, c, i, halves=(0, 1)):
        if 0 in halves:
            act.wait_ge(self.rows_summed, c + 2)
        for h in halves:
            part = self.logs[i % self.buffers][:, HALVES[h][0]:HALVES[h][1]]
            act.activation(part, part, ACT.Ln, bias=self.tiny[:, 0:1], scale=float(np.e)).then_inc(self.logged, 1)

    def vector_logs(self, dve, c, i, halves=(0, 1)):
        for h in halves:
            dve.wait_ge(self.logged, c * 2 + h + 1)
            part = self.logs[i % self.buffers][:, HALVES[h][0]:HALVES[h][1]]
            dve.scalar_tensor_tensor(part, part, OFF, part, ALU.mult, ALU.min).then_inc(self.evened, 1)

    def weigh(self, pe, ident, c, i):
        pe.wait_ge(self.exped, c + 1)
        pe.wait_ge(self.summed, c + 1)
        for g in range(NG + 2):
            if g < NG:
                for j, (k, m) in enumerate(GROUPS[g]):
                    ins = pe.transpose(self.pa[0:m, 3 + g % 3, P * j:P * j + P], self.xs[i % self.ring][:, P * k:P * k + m], ident)
                ins.then_inc(self.turned_es, 1)
            if g >= 2:
                w = g - 2
                if w % 2:
                    pe.wait_ge(self.odd, c * (NG // 2) + w // 2 + 1)
                else:
                    pe.wait_ge(self.even, c * (NG - NG // 2) + w // 2 + 1)
                for k, m in GROUPS[w]:
                    ins = pe.matmul(self.pa[:, 6 + i % 2, 0:AUG], self.esT[0:m, k, :], self.v[0:m, k, :],
                                    start=(k == 0), stop=(k == NC - 1))
        ins.then_inc(self.weighed, 1)

    def group(self, g):
        k, m = GROUPS[g][0]
        n = len(GROUPS[g])
        return self.esT[0:m, k:k + n, :].rearrange("p k n -> p (k n)"), self.pa[0:m, 3 + g % 3, 0:P * n]

    def scalar_even(self, act, c, groups=range(0, NG, 2)):
        for g in groups:
            act.wait_ge(self.turned_es, c * NG + g + 1)
            to, of = self.group(g)
            act.activation(to, of, ACT.Copy).then_inc(self.even, 1)

    def scalar_exp(self, act, c, i, halves=(0, 1)):
        if 0 in halves:
            act.wait_ge(self.negated, c + 1)
        for h in halves:
            part = self.xs[i % self.ring][:, HALVES[h][0]:HALVES[h][1]]
            ins = act.activation(part, part, ACT.Exp, bias=self.neg[i % 2][:, 0:1])
        if 1 in halves:
            ins.then_inc(self.exped, 1)

    def vector_counters(self, dve):
        self.blocks, self.loads, self.outs = (dve.alloc_register(f"{n}{self.l}") for n in ("blocks", "loads", "outs"))
        for r in (self.blocks, self.loads, self.outs):
            dve.reg_mov(r, 0)

    def vector_peak(self, dve, c, i, scores, scored, prepare=lambda b: None, between=lambda b: None):
        u, xs, logs = i % 2, self.xs[i % self.ring], self.logs[i % self.buffers]
        if self.counts:
            dve.reg_add(self.loads, self.loads, 2)
        elif u == 0:
            dve.reg_add(self.loads, self.loads, 16)
        prepare(0)
        for b, (lo, m) in enumerate(BLOCKS):
            if b + 1 < NS:
                prepare(b + 1)
            dve.reg_add(self.blocks, self.blocks, 1)
            n = dve.snap(self.blocks)
            n_in = dve.snap(self.loads)
            dve.wait_ge(self.ready, 1)
            if b == 0:
                dve.wait_ge(self.evened if self.counts else self.logs_in[u], n_in)
            dve.wait_ge(scored, n)
            dve.tensor_tensor_reduce(xs[:, lo:lo + m], scores(b, lo, m), logs[:, lo:lo + m],
                                     1.0, -3e38, ALU.add, ALU.max, self.peaks[:, b:b + 1]).then_inc(self.peaked, 1)
            between(b)
        dve.wait_ge(self.peaked, (c + 1) * NS)
        dve.tensor_reduce(self.neg[u][:, :], self.peaks[:, :], AX.X, ALU.max).then_inc(self.dv, 1)
        dve.wait_ge(self.dv, c + 1)
        dve.tensor_scalar(self.neg[u][:, :], self.neg[u][:, :], -1e29, -1.0, ALU.max, ALU.mult).then_inc(self.negated, 1)

    def vector_odd(self, dve, c, groups=range(1, NG, 2)):
        for g in groups:
            dve.wait_ge(self.turned_es, c * NG + g + 1)
            to, of = self.group(g)
            dve.tensor_copy(to, of).then_inc(self.odd, 1)

    def vector_out(self, dve, c, i):
        dve.reg_add(self.outs, self.outs, 1)
        n = dve.snap(self.outs)
        dve.wait_ge(self.ready, 1)
        dve.wait_ge(self.weighed, n)
        dve.tensor_copy(self.sums[:, ds(c * AUG, AUG)], self.pa[:, 6 + i % 2, 0:AUG]).then_inc(self.summed, 1)

    def vector_mean(self, dve, s, out):
        dve.wait_ge(self.summed, NC + 2)
        sums = self.sums[:, :].rearrange("p (c f) -> p c f", f=AUG)
        s.do(dve.tensor_scalar(self.den[:, :], sums[:, :, F], 1e-30, None, ALU.max))
        s.do(dve.reciprocal(self.den[:, :], self.den[:, :]))
        s.mark(dve.tensor_tensor(out, sums[:, :, 0:F], spread(self.den[:, :]), ALU.mult))


def conv_phase(nc, io, dram, keep, l):
    with phase(nc, f"c{l}") as ph:
        kT, qT = ph.sb("kT", [P, NP]), ph.sb("qT", [P, NP + P])
        wq, wk, wvs = ph.sb("wq", [P, F]), ph.sb("wk", [P, F]), ph.sb("wvs", [P, 2 * F])
        q_st = [ph.sb(f"q_st{u}", [P, P]) for u in range(2)]
        res, agg = ph.sb("res", [P, NC, F]), ph.sb("agg", [P, NC, F])
        gain, offset = ph.sb("gain", [P, F]), ph.sb("offset", [P, F])
        w = norm_scratch(ph)
        sm = Softmax(nc, ph, dram, l, ring=2, ahead=2 if l == 0 else 1, counts=(l == 0))
        sm.dv = ph.sem("peak_steps")
        v, pa, flat = sm.v, sm.pa, sm.flat
        hT = sm.esT[:, :, :].rearrange("p k n -> p (k n)")
        (blank, zeroed, loaded, turned, copied, mm, acted, staged, scored, dv) = (ph.sem(n) for n in (
            "blank", "zeroed", "loaded", "turned", "copied", "mm", "acted", "staged", "scored", "dv"))
        block = ph.block()
        if l == 0:
            W = {k: io[f"L1_gnn_W{k}0"] for k in "qkvs"}
            B = {k: io[f"L1_gnn_b{k}0"] for k in "qkvs"}
            g_d, b_d = io["L1_gnn_ln0_g"], io["L1_gnn_ln0_b"]
        else:
            W = {k: io[f"L1_gnn_W{k}"][l - 1] for k in "qkvs"}
            B = {k: io[f"L1_gnn_b{k}"][l - 1, :] for k in "qkvs"}
            g_d, b_d = io["L1_gnn_ln_g"][l - 1, :], io["L1_gnn_ln_b"][l - 1, :]
        h = keep["x"] if l == 0 else keep["h"]

        @block.sync
        def _(sp):
            sp.wait_ge(blank, 1)
            for to, of in ((wq, "q"), (wk, "k")):
                sp.dma_start(to[0:F, :], W[of]).then_inc(loaded, 16)
                sp.dma_start(to[F:AUG, :], row(B[of])).then_inc(loaded, 16)
            for lo, of in ((0, "v"), (F, "s")):
                sp.dma_start(wvs[0:F, lo:lo + F], W[of]).then_inc(loaded, 16)
                sp.dma_start(wvs[F:AUG, lo:lo + F], row(B[of])).then_inc(loaded, 16)
            sp.dma_start(gain[:, :], row(g_d).to_broadcast([P, F])).then_inc(loaded, 16)
            sp.dma_start(offset[:, :], row(b_d).to_broadcast([P, F])).then_inc(loaded, 16)
            sm.load(sp)

        @block.gpsimd
        def _(pool):
            pool.memset(kT[F:P, :], 0.0).then_inc(zeroed, 1)
            for u in range(2):
                pool.memset(q_st[u][F:P, :], 0.0).then_inc(zeroed, 1)
            pool.memset(qT[0:F, NP:NP + P], 0.0).then_inc(zeroed, 1)
            if l == 0:
                pool.wait_ge(zeroed, 4)
                sm.pool_sums(pool)

        @block.tensor
        def _(pe):
            for c in range(NC):
                ins = pe.transpose(flat[0:F, P * c:P * c + P], h[:, c, :], keep["ident"][:, :])
            ins.then_inc(turned, 1)
            pe.wait_ge(loaded, 16 * 10)
            pe.wait_ge(copied, 1)
            for n, weight in enumerate((wq, wk)):
                if n:
                    pe.wait_ge(acted, n)
                for k in range(0, NP, SW):
                    m = min(SW, NP - k)
                    ins = pe.matmul(flat[0:F, k:k + m], weight[:, :], hT[:, k:k + m], start=True, stop=True)
                ins.then_inc(mm, 1)
            pe.wait_ge(acted, 2)
            for c in range(NC):
                ins = pe.matmul(flat[:, P * c:P * c + P], hT[:, P * c:P * c + P], wvs[:, :], start=True, stop=True)
            ins.then_inc(mm, 1)
            pe.wait_ge(copied, 2)
            pe.wait_ge(zeroed, 4)
            pe.sem_inc(sm.summed, 2)

            def scores(c, u, first=False):
                pe.wait_ge(staged, c + 1)
                for b, (lo, m) in enumerate(BLOCKS):
                    if b == 0 and not first:
                        pe.wait_ge(sm.peaked, c * NS)
                    elif b >= 3:
                        pe.wait_ge(sm.peaked, c * NS + b - 2)
                    pe.matmul(pa[:, b % 3, 0:m], q_st[u][:, :], kT[:, lo:lo + m], start=True, stop=True).then_inc(scored, 1)

            scores(0, 0, first=True)

            def body(c, i):
                u = i % 2
                if sm.has(c + 1):
                    scores(c + 1, 1 - u)
                sm.weigh(pe, keep["ident"][:, :], c, i)

            sm.loop(pe, body)
            if l == 0:
                sm.leave(pe)

        @block.vector
        def _(dve):
            for t in (wq, wk, wvs):
                ins = dve.memset(t[F:P, :], 0.0)
            ins.then_inc(blank, 1)
            dve.memset(hT[F:P, :], 1.0)
            if l == 0:
                dve.memset(sm.tiny[:, :], 1e-18)
                dve.memset(sm.ones[:, :], 1.0)
                dve.memset(sm.leaving[:, :], 0.0)
                dve.memset(keep["out_deg"][:, :], 1.0)
            dve.memset(v[:, :, F:AUG], 1.0).then_inc(sm.ready, 1)
            dve.wait_ge(turned, 1)
            dve.tensor_copy(hT[0:F, :], flat[0:F, 0:NP]).then_inc(copied, 1)
            dve.wait_ge(mm, 3)
            vs = flat[:, 0:NC * P].rearrange("p (c f) -> p c f", f=P)
            dve.tensor_copy(v[:, :, 0:F], vs[:, :, 0:F])
            dve.tensor_copy(res[:, :, :], vs[:, :, F:P]).then_inc(copied, 1)
            sm.vector_counters(dve)
            if l == 0:
                for u in range(2):
                    sm.vector_logs(dve, u, u)

            def of_block(b, lo, m):
                return pa[:, b % 3, 0:m]

            sm.vector_peak(dve, 0, 0, of_block, scored)

            def body(c, i):
                u = i % 2
                if sm.has(c + 1):
                    sm.vector_peak(dve, c + 1, i + 1, of_block, scored)
                if l == 0 and sm.has(c + 2):
                    sm.vector_odd(dve, c, [1, 3])
                    sm.vector_logs(dve, c + 2, i + 2, [0])
                    sm.vector_odd(dve, c, [5])
                    sm.vector_logs(dve, c + 2, i + 2, [1])
                else:
                    sm.vector_odd(dve, c)
                sm.vector_out(dve, c, u)

            sm.loop(dve, body)
            s = Steps(dve, dv)
            if l == 0:
                dve.wait_ge(sm.weighed, NC + 1)
                for m, lo, hi in ((P, 0, FULL), (REST, FULL, NC)):
                    s.mark(dve.tensor_scalar(keep["out_deg"][0:m, lo:hi], pa[0:m, 7, P + lo:P + hi], 1.0, None, ALU.add))
            sm.vector_mean(dve, s, agg[:, :, :])
            dve.wait_ge(dv, s.n)
            s.do(dve.tensor_tensor(res[:, :, :], res[:, :, :], agg[:, :, :], ALU.add))
            if l:
                s.do(dve.tensor_tensor(res[:, :, :], res[:, :, :], h[:, :, :], ALU.add))
            norm_vector(dve, s, w, 1, res[:, :, :], agg[:, :, :])
            dve.wait_ge(dv, s.n)

            def per_feature(vec):
                return vec[:, :].rearrange("p (o f) -> p o f", o=1).to_broadcast([P, NC, F])

            dve.wait_ge(loaded, 16 * 10)
            s.do(dve.tensor_tensor(agg[:, :, :], agg[:, :, :], per_feature(gain), ALU.mult))
            s.do(dve.tensor_tensor(agg[:, :, :], agg[:, :, :], per_feature(offset), ALU.add))
            s.do(dve.tensor_scalar(keep["h"][:, :, :], agg[:, :, :], 0.0, None, ALU.max))
            if l == 3:
                s.do(dve.tensor_tensor(res[:, :, :], keep["x"][:, :, :], keep["h"][:, :, :], ALU.add))
                norm_vector(dve, s, w, 2, res[:, :, :], keep["x"][:, :, :])

        @block.scalar
        def _(act):
            act.wait_ge(mm, 1)
            act.activation(qT[0:F, 0:NP], flat[0:F, 0:NP], ACT.Copy, scale=float(F) ** -0.5).then_inc(acted, 1)
            act.wait_ge(mm, 2)
            act.activation(kT[0:F, :], flat[0:F, 0:NP], ACT.Copy).then_inc(acted, 1)
            act.wait_ge(acted, 1)
            act.wait_ge(zeroed, 4)

            def stage(c, u):
                act.activation(q_st[u][0:F, :], qT[0:F, ds(c * P, P)], ACT.Copy).then_inc(staged, 1)

            stage(0, 0)
            stage(1, 1)
            if l == 0:
                sm.scalar_logs(act, 0, 0)
                sm.scalar_logs(act, 1, 1)
            sm.scalar_exp(act, 0, 0)

            def body(c, i):
                u = i % 2
                if sm.has(c + 1):
                    act.wait_ge(scored, (c + 1) * NS)
                    stage(c + 2, u)
                if l == 0 and sm.has(c + 2):
                    sm.scalar_even(act, c, [0])
                    sm.scalar_logs(act, c + 2, i + 2, [0])
                    sm.scalar_even(act, c, [2])
                    sm.scalar_logs(act, c + 2, i + 2, [1])
                    sm.scalar_even(act, c, [4, 6])
                else:
                    sm.scalar_even(act, c)
                if sm.has(c + 1):
                    sm.scalar_exp(act, c + 1, i + 1)

            sm.loop(act, body)
            norm_scalar(act, w, 1)
            if l == 3:
                norm_scalar(act, w, 2)


D4 = 4
H16 = F // D4
WS = 2 * H16 + F + 4
SB = 8
TB = 4 * SB
HB = QT // SB
SBLK = SB * P
assert NC <= TB and HB % 2 == 1 and HB * SB == QT and 2 * H16 == M


def sheaf_tables_phase(nc, io, dram, keep):
    with phase(nc, "st") as ph:
        xT, yT, zT = (ph.sb(n, [F, NP]) for n in ("xT", "yT", "zT"))
        w1c = ph.sb("w1c", [F, D4])
        same = ph.sb("same", [F, H16])
        w1x, w2x = ph.sb("w1x", [F, D4, H16]), ph.sb("w2x", [F, F])
        mix = ph.sb("mix", [F, 2 * H16 + F])
        root = ph.sb("root", [P, NC])
        heads = ph.sb("heads", [P, M])
        pt = ph.ps("pt", [P, 7 * 512])
        zero, loaded, turned, copied, mm, rooted, dv, stored, spread = (ph.sem(n) for n in (
            "zero", "loaded", "turned", "copied", "mm", "rooted", "dv", "stored", "spread"))
        block = ph.block()
        src_tab, dst_tab = keep["src_tab"], keep["dst_tab"]

        @block.sync
        def _(sp):
            for d in range(D4):
                sp.dma_start(w1c[H16 * d:H16 * d + H16, :], io["L2_gnn_W1"][d:d + 1, :].to_broadcast([H16, D4])).then_inc(loaded, 16)
            sp.dma_start(mix[:, 0:H16], io["mlp1_T"][0:F, :]).then_inc(loaded, 16)
            sp.dma_start(mix[:, H16:2 * H16], io["mlp1_T"][F:2 * F, :]).then_inc(loaded, 16)
            sp.wait_ge(zero, 1)
            for d in range(D4):
                lo = H16 * d
                sp.dma_start(w2x[lo:lo + H16, lo:lo + H16], io["L2_gnn_W2"]).then_inc(loaded, 16)
            sp.wait_ge(copied, 4)
            sp.dma_start(chunked(dram["sheaf_src"]), src_tab[:, :, :]).then_inc(stored, 16)
            sp.dma_start(chunked(dram["table_dst"]), dst_tab[:, :, :]).then_inc(stored, 16)
            sp.wait_ge(stored, 32)

        @block.gpsimd
        def _(pool):
            pool.wait_ge(copied, 4)
            spread_to_edges(pool, dram, keep, dst_tab, heads, stored, spread)

        @block.tensor
        def _(pe):
            for c in range(NC):
                ins = pe.transpose(pt[0:F, P * c:P * c + P], keep["x"][:, c, :], keep["ident"][:, :])
            ins.then_inc(turned, 1)
            pe.wait_ge(loaded, 16 * 10)
            pe.wait_ge(dv, 2)
            for n, (weight, of) in enumerate(((w1x[:, :, :].rearrange("p k f -> p (k f)"), xT), (w2x[:, :], yT))):
                pe.wait_ge(copied, n + 1)
                for k in range(0, NP, 512):
                    m = min(512, NP - k)
                    ins = pe.matmul(pt[0:F, k:k + m], weight, of[:, k:k + m], start=True, stop=True)
                ins.then_inc(mm, 1)
            pe.wait_ge(copied, 3)
            for c in range(NC):
                ins = pe.matmul(pt[:, P * c:P * c + 2 * H16 + F], zT[:, P * c:P * c + P], mix[:, :], start=True, stop=True)
            ins.then_inc(mm, 1)

        @block.scalar
        def _(act):
            act.activation(root[:, :], keep["out_deg"][:, :], ACT.Sqrt).then_inc(rooted, 1)

        @block.vector
        def _(dve):
            dve.memset(w2x[:, :], 0.0).then_inc(zero, 1)
            dve.memset(src_tab[:, :, 2 * H16 + F:WS], 0.0)
            s = Steps(dve, dv)
            dve.tensor_copy(mix[:, 2 * H16:2 * H16 + F], keep["ident"][0:F, 0:F])
            s.do(dve.tensor_reduce(same[:, :], keep["ident"][0:F, 0:F].rearrange("p (d f) -> p f d", d=D4), AX.X, ALU.add))
            dve.wait_ge(loaded, 16 * 10)
            s.do(dve.tensor_tensor(w1x[:, :, :], w1c[:, :].rearrange("p (k o) -> p k o", o=1).to_broadcast([F, D4, H16]),
                                   same[:, :].rearrange("p (o f) -> p o f", o=1).to_broadcast([F, D4, H16]), ALU.mult))
            dve.wait_ge(turned, 1)
            dve.tensor_copy(xT[:, :], pt[0:F, 0:NP]).then_inc(copied, 1)
            for n, to in enumerate((yT, zT)):
                dve.wait_ge(mm, n + 1)
                dve.tensor_copy(to[:, :], pt[0:F, 0:NP]).then_inc(copied, 1)
            dve.wait_ge(rooted, 1)
            s.do(dve.reciprocal(keep["dis"][:, :], root[:, :]))
            s.mark(dve.tensor_copy(src_tab[:, :, 2 * H16 + F], keep["dis"][:, :]))
            dve.wait_ge(mm, 3)
            out = pt[:, 0:NC * P].rearrange("p (c f) -> p c f", f=P)
            dve.tensor_copy(src_tab[:, :, 0:2 * H16 + F], out[:, :, 0:2 * H16 + F])
            dve.tensor_copy(dst_tab[:, :, 0:H16], out[:, :, H16:2 * H16])
            dve.tensor_copy(dst_tab[:, :, H16:2 * H16], out[:, :, 0:H16]).then_inc(copied, 1)


def sheaf_phase(nc, io, dram, keep):
    with phase(nc, "sh") as ph:
        got_s = [ph.sb(f"got_s{u}", [P, TB, WS]) for u in range(2)]
        st_src = [ph.sb(f"st_src{u}", [P, SB, 4], I32) for u in range(2)]
        seq4 = [ph.sb(f"seq4{u}", [P, SBLK + 1], I32) for u in range(2)]
        seq2 = [[ph.sb(f"seq2{g}_{u}", [P, SBLK + 1], I32) for u in range(2)] for g in range(2)]
        cont4 = ph.sb("cont4", [P, SBLK])
        cont2 = [[ph.sb(f"cont2{g}_{u}", [P, SBLK]) for u in range(2)] for g in range(2)]
        first_rows = [ph.sb(f"first_rows{u}", [P, SB, 4, M]) for u in range(2)]
        of_dst = [ph.sb(f"of_dst{u}", [P, SBLK]) for u in range(2)]
        bias1 = ph.sb("bias1", [P, 1])
        bias2 = ph.sb("bias2", [P, 6])
        w2 = ph.sb("w2", [P, 48])
        zin = ph.sb("zin", [P, TB, M])
        hz = ph.sb("hz", [P, SB, P])
        MT = 2 * TB
        tri = ph.sb("tri", [P, MT, 4, 4])
        q = ph.sb("q", [P, MT, 4, 4])
        prod = ph.sb("prod", [P, MT, 4, 4])
        dot = ph.sb("dot", [P, MT, 4, 4])
        inv, coef = ph.sb("inv", [P, MT]), ph.sb("coef", [P, MT, 3])
        norm, rnorm = ph.sb("norm", [P, MT, 4]), ph.sb("rnorm", [P, MT, 4])
        gprod = ph.sb("gprod", [P, TB, 4, 16])
        g = ph.sb("g", [P, TB, 16])
        gnorm = ph.sb("gnorm", [P, TB, 16])
        msg = ph.sb("msg", [P, TB, F])
        term = ph.sb("term", [P, TB, F])
        run = [[ph.sb(f"run{k}_{h}", [P, 512]) for h in range(2)] for k in range(2)]
        out_t = ph.sb("out_t", [P, SB, 4, F])
        pz = ph.ps("pz", [P, SB, P])
        pd = ph.ps("pd", [P, SBLK])
        pp = ph.ps("pp", [P, 512])
        pin = [ph.ps(f"pin{k}", [P, 512]) for k in range(2)]
        pout = ph.ps("pout", [P, 512])
        (zero, loaded, ready, staged, messaged, zed, zined, hidden, parred, filled, sized, rooted, turned, scanned, backed,
         copied, stored, masked, rows_turned, spread, dv) = (ph.sem(n) for n in (
             "zero", "loaded", "ready", "staged", "messaged", "zed", "zined", "hidden", "parred", "filled", "sized", "rooted",
             "turned", "scanned", "backed", "copied", "stored", "masked", "rows_turned", "spread", "dv"))
        got = [ph.sem(f"got{u}") for u in range(2)]
        seq_in = [ph.sem(f"seq_in{u}") for u in range(2)]
        rows_in = [ph.sem(f"rows_in{u}") for u in range(2)]
        block = ph.block()
        sums_d = dram["sums"].rearrange("(q b i p) f -> q b p i f", q=4, b=HB, i=SB)
        spread_d = dram["spread"][0:EP, :].rearrange("(q b i p) f -> q b p i f", q=4, b=HB, i=SB)
        PIECES = [(k, h) for k in range(2) for h in range(2)]
        entries = pp[:, 0:SB * 48].rearrange("p (m k) -> p m k", k=6)

        def loop(eng, body):
            body(1, 1, 0)
            with eng.Fori(0, HB // 2 - 1) as it:
                body(it * 2 + 2, 0, it)
                body(it * 2 + 3, 1, it + 1)
            body(HB - 1, 0, HB // 2 - 1)
            body(HB, 1, HB // 2)

        def is_block(n, *blocks):
            return type(n) is int and n in blocks

        @block.sync
        def _(sp):
            for k in range(8):
                sp.dma_start(bias1[H16 * k:H16 * k + H16, :], column(io["L2_gnn_mlp1_b"])).then_inc(loaded, 16)
            sp.dma_start(bias2[:, :], row(io["mlp2_b"]).to_broadcast([P, 6])).then_inc(loaded, 16)
            sp.wait_ge(zero, 1)
            for k in range(8):
                sp.dma_start(w2[H16 * k:H16 * k + H16, 6 * k:6 * k + 6], io["mlp2_T"]).then_inc(loaded, 16)

            def load(b, at, u):
                for k in range(4):
                    of = io["dst_seq"][k:k + 1, ds(at, SBLK + 1)]
                    sp.dma_start(first_rows[u][:, :, k, :], spread_d[k, b]).then_inc(rows_in[u], 16)
                    sp.dma_start(seq4[u][M * k:M * k + M, :], of.to_broadcast([M, SBLK + 1])).then_inc(seq_in[u], 16)
                    sp.dma_start(seq2[k // 2][u][F * (k % 2):F * (k % 2) + F, :],
                                 of.to_broadcast([F, SBLK + 1])).then_inc(seq_in[u], 16)

            load(0, 0, 1)
            load(1, SBLK, 0)
            at, done, masks = (sp.alloc_register(n) for n in ("sheaf_edges_at", "sheaf_blocks_done", "sheaf_masks_done"))
            sp.reg_mov(at, SBLK)
            sp.reg_mov(done, 0)
            sp.reg_mov(masks, 0)

            def again(u):
                sp.reg_add(at, at, SBLK)
                sp.reg_add(done, done, 1)
                sp.reg_add(masks, masks, 3)
                n_done, n_masks = sp.snap(done), sp.snap(masks)
                sp.wait_ge(zero, 1)
                sp.wait_ge(masked, n_masks)
                sp.wait_ge(rows_turned, n_done)
                load(n_done + 1, sp.snap(at), u)

            with sp.Fori(0, (HB - 3) // 2):
                again(1)
                again(0)
            again(1)

        @block.gpsimd
        def _(pool):
            turn = pool.alloc_register("sheaf_turn")
            pool.reg_mov(turn, 0)

            def body(n, u, it):
                pool.reg_add(turn, turn, 1)
                now = pool.snap(turn)
                pool.wait_ge(ready, 1)
                pool.wait_ge(staged, now)
                pool.wait_ge(messaged, now)
                for i in range(SB):
                    for k in range(4):
                        pool.indirect_dma_start(
                            got_s[u][:, 4 * i + k, :], None, dram["sheaf_src"],
                            bass.IndirectOffsetOnAxis(st_src[u][:, i, k:k + 1].bitcast(U32), 0)).then_inc(got[u], 16)

            loop(pool, body)

        @block.vector
        def _(dve):
            dve.memset(w2[:, :], 0.0).then_inc(zero, 1)
            dve.memset(got_s[0][:, :, :], 0.0)
            dve.memset(zin[:, :, :], 0.0)
            dve.memset(tri[:, :, :, :], 0.0)
            dve.memset(q[:, :, :, :], 0.0)
            dve.memset(dot[:, :, :, :], 0.0)
            dve.memset(of_dst[0][:, :], 0.0)
            for k in range(2):
                ins = dve.memset(run[k][1][:, :], 0.0)
            ins.then_inc(ready, 1)
            dve.wait_ge(ready, 1)
            dve.memset(q[:, :, 0, 0], 1.0)
            for k in range(1, 4):
                dve.memset(tri[:, :, k, k], 1.0)
            dve.tensor_copy(got_s[0][:, 0:NC, :], keep["src_tab"][:, :, :])
            dve.tensor_tensor(zin[:, 0:NC, :], keep["src_tab"][:, :, 0:M], keep["dst_tab"][:, :, :], ALU.add).then_inc(ready, 1)
            dve.wait_ge(ready, 2)
            dve.sem_inc(messaged, 1)

            def stage(b, u):
                dve.tensor_copy(st_src[u][:, :, :].rearrange("p i k -> p k i"),
                                keep["src"][:, :].rearrange("p (k t) -> p k t", k=4)[:, :, ds(b * SB, SB)]).then_inc(staged, 1)

            def along(n, u, it):
                dve.wait_ge(seq_in[u], it * 128 + 128)
                for to, of in ((cont4, seq4[u]), (cont2[0][u], seq2[0][u]), (cont2[1][u], seq2[1][u])):
                    dve.tensor_tensor(to[:, :], of[:, 1:SBLK + 1], of[:, 0:SBLK], ALU.is_equal).then_inc(masked, 1)
                dve.wait_ge(masked, n * 3)
                dve.wait_ge(rows_turned, n)
                dve.tensor_tensor_scan(of_dst[u][:, :], cont4[:, :], pd[:, :], of_dst[1 - u][:, SBLK - 1:SBLK],
                                       ALU.mult, ALU.add).then_inc(spread, 1)
                dve.wait_ge(spread, n)

            def messages(n, u, s):
                dve.wait_ge(parred, n + 1)
                seen = [0, 0]

                def each(*steps):
                    for z in range(2):
                        if seen[z]:
                            dve.wait_ge(dv, s.base + seen[z])
                        for step in steps:
                            s.mark(step(z))
                        seen[z] = s.n

                HM, HT = MT // 2, TB // 2

                def mats(t, z):
                    return t[:, HM * z:HM * (z + 1)]

                def tiles(t, z):
                    return t[:, HT * z:HT * (z + 1)]

                def fill(to, at, lo, hi):
                    w = hi - lo
                    return lambda z: dve.tensor_tensor(
                        mats(to, z)[:, :, at, 4 - w:4], mats(entries, z)[:, :, lo:hi],
                        bias2[:, lo:hi].rearrange("p (o k) -> p o k", o=1).to_broadcast([P, HM, w]), ALU.add)

                each(fill(q, 0, 0, 3), fill(tri, 1, 3, 5), fill(tri, 2, 5, 6))
                left = tri
                for k in range(4):
                    m = 3 - k

                    def column_k(z):
                        return mats(q, z)[:, :, k:k + 1, :]

                    if k == 0:
                        each(lambda z: dve.tensor_tensor(mats(prod, z)[:, :, 0:1, :], column_k(z), column_k(z), ALU.mult),
                             lambda z: dve.tensor_tensor(mats(prod, z)[:, :, 1:4, :], mats(tri, z)[:, :, 1:4, :],
                                                         column_k(z).to_broadcast([P, HM, m, 4]), ALU.mult))
                        dve.sem_inc(filled, 1)
                    else:
                        each(lambda z: dve.tensor_tensor(mats(prod, z)[:, :, 0:m + 1, :], mats(q, z)[:, :, k:4, :],
                                                         column_k(z).to_broadcast([P, HM, m + 1, 4]), ALU.mult))
                    each(lambda z: dve.tensor_reduce(mats(dot, z)[:, :, k, 0:m + 1], mats(prod, z)[:, :, 0:m + 1, :], AX.X, ALU.add))
                    if k < 3:
                        each(lambda z: dve.reciprocal(mats(inv, z), mats(dot, z)[:, :, k, 0]))
                        each(lambda z: dve.tensor_tensor(
                            mats(coef, z)[:, :, 0:m], mats(dot, z)[:, :, k, 1:m + 1],
                            mats(inv, z).rearrange("p (m o) -> p m o", o=1).to_broadcast([P, HM, m]), ALU.mult))
                        each(lambda z: dve.tensor_tensor(
                            mats(prod, z)[:, :, 0:m, :], column_k(z).to_broadcast([P, HM, m, 4]),
                            mats(coef, z)[:, :, 0:m].rearrange("p m (j o) -> p m j o", o=1).to_broadcast([P, HM, m, 4]),
                            ALU.mult))
                        each(lambda z: dve.tensor_tensor(mats(q, z)[:, :, k + 1:4, :], mats(left, z)[:, :, k + 1:4, :],
                                                         mats(prod, z)[:, :, 0:m, :], ALU.subtract))
                    left = q
                both = q[:, :, :, :].rearrange("p (t v) c r -> p t v (c r)", v=2)
                lengths = rnorm[:, :, :].rearrange("p (t v) c -> p t v c", v=2)
                ga, gn = (t[:, :, :].rearrange("p t (a b) -> p t a b", b=4) for t in (g, gnorm))

                def multiply(a):
                    return lambda z: dve.tensor_tensor(
                        tiles(gprod, z)[:, :, a, :].rearrange("p t (b k) -> p t b k", k=4),
                        tiles(both, z)[:, :, 0, :].rearrange("p t (b k) -> p t b k", k=4),
                        tiles(both, z)[:, :, 1, 4 * a:4 * a + 4].rearrange("p t (o k) -> p t o k", o=1)
                        .to_broadcast([P, HT, 4, 4]), ALU.mult)

                each(*(multiply(a) for a in range(4)))
                dve.sem_inc(sized, 1)
                each(lambda z: dve.tensor_reduce(tiles(g, z), tiles(gprod, z).rearrange("p t a (b k) -> p t (a b) k", k=4),
                                                 AX.X, ALU.add))
                dve.wait_ge(rooted, n + 1)
                each(lambda z: dve.reciprocal(mats(rnorm, z), mats(norm, z)))
                each(lambda z: dve.tensor_tensor(
                    tiles(lengths, z)[:, :, 1, :], tiles(lengths, z)[:, :, 1, :],
                    tiles(got_s[u], z)[:, :, 2 * H16 + F:2 * H16 + F + 1].to_broadcast([P, HT, 4]), ALU.mult))
                each(lambda z: dve.tensor_tensor(
                    tiles(gn, z), tiles(lengths, z)[:, :, 1, :].rearrange("p t (a o) -> p t a o", o=1).to_broadcast([P, HT, 4, 4]),
                    tiles(lengths, z)[:, :, 0:1, :].to_broadcast([P, HT, 4, 4]), ALU.mult))
                each(lambda z: dve.tensor_tensor(tiles(g, z), tiles(g, z), tiles(gnorm, z), ALU.mult))
                m4 = msg[:, :, :].rearrange("p t (a h) -> p t a h", a=4)
                t4 = term[:, :, :].rearrange("p t (a h) -> p t a h", a=4)
                for b in range(4):
                    each(lambda z: dve.tensor_tensor(
                        tiles(t4 if b else m4, z),
                        tiles(got_s[u], z)[:, :, 2 * H16 + H16 * b:2 * H16 + H16 * (b + 1)].rearrange("p t (o h) -> p t o h", o=1)
                        .to_broadcast([P, HT, 4, H16]), tiles(ga, z)[:, :, :, b:b + 1].to_broadcast([P, HT, 4, H16]), ALU.mult))
                    if b:
                        each(lambda z: dve.tensor_tensor(tiles(msg, z), tiles(msg, z), tiles(term, z), ALU.add))
                dve.wait_ge(dv, s.base + s.n)
                dve.sem_inc(messaged, 1)

            stage(0, 1)
            stage(1, 0)
            dve.wait_ge(loaded, 16 * 17)
            s = Steps(dve, dv)
            messages(0, 0, s)
            PER = s.n
            s.do(dve.tensor_copy(keep["loops"][:, :, :], msg[:, 0:NC, :]))
            along(1, 1, 0)

            def body(n, u, it):
                dve.wait_ge(got[u], it * 512 + 512)
                if not is_block(n, HB - 1, HB):
                    stage(n + 1, u)
                if not is_block(n, HB):
                    along(n + 1, 1 - u, it + (1 - u))
                s = Steps(dve, dv, n * PER + 1)
                messages(n, u, s)
                assert s.n == PER
                for j, (k, h) in enumerate(PIECES):
                    dve.wait_ge(turned, n * 4 + j - 3)
                    dve.tensor_tensor_scan(run[k][h][:, :], cont2[k][u][:, 512 * h:512 * h + 512], pin[j % 2][:, :],
                                           run[k][1 - h][:, 511:512], ALU.mult, ALU.add).then_inc(scanned, 1)
                    dve.wait_ge(scanned, n * 4 + j - 3)

            loop(dve, body)

        @block.tensor
        def _(pe):
            pe.wait_ge(loaded, 16 * 17)
            pe.wait_ge(ready, 2)

            def turn_rows(n, u, it):
                pe.wait_ge(rows_in[u], it * 64 + 64)
                for i in range(SB):
                    ins = pe.transpose(pd[:, P * i:P * i + P], first_rows[u][:, i, :, :].rearrange("p k m -> p (k m)"),
                                       keep["ident"][:, :])
                ins.then_inc(rows_turned, 1)

            def hidden_and_entries(n, u):
                loops = is_block(n, 0)
                if not loops:
                    pe.wait_ge(spread, n)
                    for h in range(2):
                        pe.matmul(pz[:, 4 * h:4 * h + 4, :].rearrange("p i n -> p (i n)"), keep["ident"][:, :],
                                  of_dst[u][:, 512 * h:512 * h + 512], start=True, stop=False)
                    pe.wait_ge(zined, n)
                for i in range(SB):
                    ins = pe.matmul(pz[:, i, :], zin[:, 4 * i:4 * i + 4, :].rearrange("p t f -> p (t f)"), keep["ident"][:, :],
                                    start=loops, stop=loops or i % 4 == 3)
                ins.then_inc(zed, 1)
                pe.wait_ge(hidden, n + 1)
                if not loops:
                    pe.wait_ge(filled, n)
                for i in range(SB):
                    ins = pe.matmul(pp[:, 48 * i:48 * i + 48], hz[:, i, :], w2[:, :], start=True, stop=True)
                ins.then_inc(parred, 1)

            hidden_and_entries(0, 0)
            turn_rows(1, 1, 0)
            hidden_and_entries(1, 1)
            pe.sem_inc(copied, 1)

            def body(n, u, it):
                if not is_block(n, HB):
                    turn_rows(n + 1, 1 - u, it + (1 - u))
                    hidden_and_entries(n + 1, 1 - u)
                pe.wait_ge(messaged, n + 2)

                def to_scan(j):
                    k, h = PIECES[j]
                    for i in range(4 * h, 4 * h + 4):
                        ins = pe.transpose(pin[j % 2][:, P * (i % 4):P * (i % 4) + P],
                                           msg[:, 4 * i + 2 * k:4 * i + 2 * k + 2, :].rearrange("p t f -> p (t f)"),
                                           keep["ident"][:, :])
                    ins.then_inc(turned, 1)

                to_scan(0)
                to_scan(1)
                for j, (k, h) in enumerate(PIECES):
                    pe.wait_ge(scanned, n * 4 + j - 3)
                    if j + 2 < len(PIECES):
                        to_scan(j + 2)
                    pe.wait_ge(copied, n * 4 + j - 3)
                    for i in range(4):
                        ins = pe.transpose(pout[:, P * i:P * i + P], run[k][h][:, P * i:P * i + P], keep["ident"][:, :])
                    ins.then_inc(backed, 1)

            loop(pe, body)

        @block.scalar
        def _(act):
            act.wait_ge(loaded, 16 * 17)

            def hide(n):
                act.wait_ge(zed, n + 1)
                act.activation(hz[:, :, :], pz[:, :, :], ACT.Relu, bias=bias1[:, 0:1]).then_inc(hidden, 1)

            def sources(n, u, it):
                act.wait_ge(got[u], it * 512 + 512)
                act.activation(zin[:, :, :], got_s[u][:, :, 0:M], ACT.Copy).then_inc(zined, 1)

            def roots(n):
                act.wait_ge(sized, n + 1)
                act.activation(norm[:, :, :], dot[:, :, :, 0], ACT.Sqrt).then_inc(rooted, 1)

            hide(0)
            roots(0)
            sources(1, 1, 0)
            hide(1)

            def body(n, u, it):
                roots(n)
                if not is_block(n, HB):
                    sources(n + 1, 1 - u, it + (1 - u))
                    hide(n + 1)
                if not is_block(n, 1):
                    act.wait_ge(stored, n * 64 - 64)
                for j, (k, h) in enumerate(PIECES):
                    act.wait_ge(backed, n * 4 + j - 3)
                    act.activation(out_t[:, 4 * h:4 * h + 4, 2 * k:2 * k + 2, :],
                                   pout[:, :].rearrange("p (i k f) -> p i k f", i=4, k=2), ACT.Copy).then_inc(copied, 1)
                act.wait_ge(copied, n * 4 + 1)
                for k in range(4):
                    act.dma_start(sums_d[k, n - 1], out_t[:, :, k, :]).then_inc(stored, 16)

            loop(act, body)
            act.wait_ge(stored, HB * 64)


def sheaf_node_phase(nc, io, dram, keep):
    with phase(nc, "sn") as ph:
        agg = ph.sb("agg", [P, NC, F])
        edge_rows = ph.sb("edge_rows", [P, 3, F])
        across, has = ph.sb("across", [P, 3, NC]), ph.sb("has", [P, NC])
        part, low, grown = (ph.sb(n, [P, NC, F]) for n in ("part", "low", "grown"))
        coeff = ph.sb("coeff", [P, D4])
        w = norm_scratch(ph)
        loaded, got, dv, lowered, grew, tanhed = (ph.sem(n) for n in ("loaded", "got", "dv", "lowered", "grew", "tanhed"))
        block = ph.block()
        ends = [QE * (q + 1) - 1 for q in range(3)]

        @block.sync
        def _(sp):
            for q, e in enumerate(ends):
                sp.dma_start(edge_rows[:, q, :], dram["sums"][e:e + 1, :].to_broadcast([P, F])).then_inc(loaded, 16)
            sp.dma_start(coeff[:, :], row(io["L2_gnn_epsilons"]).to_broadcast([P, D4])).then_inc(loaded, 16)

        @block.gpsimd
        def _(pool):
            for c in range(NC):
                pool.indirect_dma_start(agg[:, c, :], None, dram["sums"],
                                        bass.IndirectOffsetOnAxis(keep["last_idx"][:, c:c + 1].bitcast(U32), 0)).then_inc(got, 16)

        @block.vector
        def _(dve):
            s = Steps(dve, dv)
            for q, e in enumerate(ends):
                s.do(dve.tensor_scalar(across[:, q, :], keep["first"][:, :], float(e), None, ALU.is_le))
                s.do(dve.scalar_tensor_tensor(across[:, q, :], keep["last"][:, :], float(e), across[:, q, :], ALU.is_gt, ALU.mult))
            s.do(dve.tensor_scalar(has[:, :], keep["degree"][:, :], 0.0, None, ALU.is_gt))
            dve.wait_ge(loaded, 64)
            dve.wait_ge(got, 16 * NC)
            for q in range(3):
                s.do(dve.tensor_tensor(part[:, :, :], edge_rows[:, q:q + 1, :].to_broadcast([P, NC, F]), spread(across[:, q, :]),
                                       ALU.mult))
                s.do(dve.tensor_tensor(agg[:, :, :], agg[:, :, :], part[:, :, :], ALU.add))
            s.do(dve.tensor_tensor(agg[:, :, :], agg[:, :, :], spread(has[:, :]), ALU.mult))
            s.do(dve.tensor_tensor(agg[:, :, :], agg[:, :, :], keep["loops"][:, :, :], ALU.add))
            s.do(dve.tensor_tensor(agg[:, :, :], agg[:, :, :], spread(keep["dis"][:, :]), ALU.mult))
            dve.tensor_scalar(low[:, :, :], agg[:, :, :], 0.0, None, ALU.min).then_inc(lowered, 1)
            s.do(dve.tensor_scalar(agg[:, :, :], agg[:, :, :], 0.0, None, ALU.max))
            dve.wait_ge(tanhed, 1)
            s.do(dve.tensor_scalar(coeff[:, :], coeff[:, :], 2.0, None, ALU.add))
            for d in range(D4):
                s.mark(dve.tensor_scalar(part[:, :, H16 * d:H16 * d + H16], keep["x"][:, :, H16 * d:H16 * d + H16],
                                         coeff[:, d:d + 1], 1.0, ALU.mult, ALU.add))
            dve.wait_ge(dv, s.n)
            s.do(dve.tensor_tensor(part[:, :, :], part[:, :, :], agg[:, :, :], ALU.subtract))
            dve.wait_ge(grew, 1)
            s.do(dve.tensor_tensor(part[:, :, :], part[:, :, :], grown[:, :, :], ALU.subtract))
            norm_vector(dve, s, w, 1, part[:, :, :], keep["x"][:, :, :])

        @block.scalar
        def _(act):
            act.wait_ge(loaded, 64)
            act.activation(coeff[:, :], coeff[:, :], ACT.Tanh).then_inc(tanhed, 1)
            act.wait_ge(lowered, 1)
            act.activation(grown[:, :, :], low[:, :, :], ACT.Exp).then_inc(grew, 1)
            norm_scalar(act, w, 1)


def attention_phase(nc, io, dram, keep, out):
    with phase(nc, "at") as ph:
        SLOPE = 0.01
        wa = ph.sb("wa", [F, 2])
        lin_w, lin_b = ph.sb("lin_w", [P, F]), ph.sb("lin_b", [P, F])
        src_all, src_low = ph.sb("src_all", [P, NP]), ph.sb("src_low", [P, N])
        catT = src_all
        col = ph.sb("col", [P, NC + 1])
        cat = ph.sb("cat", [P, NC, P])
        res = ph.sb("res", [P, NC, F])
        w = norm_scratch(ph)
        sm = Softmax(nc, ph, dram, "a", ring=4, ahead=3)
        fT = sm.esT[0:F, :, :].rearrange("p k n -> p (k n)")
        sm.dv = ph.sem("peak_steps")
        v, pa, flat = sm.v, sm.pa, sm.flat
        (loaded, turned, copied, mm, low_made, relued, scored, dv, joined, back, normed, done) = (ph.sem(n) for n in (
            "loaded", "turned", "copied", "mm", "low_made", "relued", "scored", "dv", "joined", "back", "normed", "done"))
        block = ph.block()

        @block.sync
        def _(sp):
            sp.dma_start(wa[:, 0:1], io["L3_gnn_attn_w"][0:F, :]).then_inc(loaded, 16)
            sp.dma_start(wa[:, 1:2], io["L3_gnn_attn_w"][F:2 * F, :]).then_inc(loaded, 16)
            sp.dma_start(lin_w[:, :], io["lin_T"]).then_inc(loaded, 16)
            sp.dma_start(lin_b[:, :], row(io["L3_gnn_lin_b"]).to_broadcast([P, F])).then_inc(loaded, 16)
            sm.load(sp)
            sp.wait_ge(normed, 1)
            sp.dma_start(chunked(out, 0, FULL * P), keep["x"][:, 0:FULL, :]).then_inc(done, 16)
            sp.dma_start(out[FULL * P:N, :], keep["x"][0:REST, FULL, :]).then_inc(done, 16)
            sp.wait_ge(done, 32)

        @block.tensor
        def _(pe):
            for c in range(NC):
                ins = pe.transpose(flat[0:F, P * c:P * c + P], keep["x"][:, c, :], keep["ident"][:, :])
            ins.then_inc(turned, 1)
            pe.wait_ge(loaded, 64)
            pe.wait_ge(copied, 1)
            for c in range(NC):
                pe.matmul(pa[:, 7, c:c + 1], fT[:, P * c:P * c + P], wa[:, 1:2], start=True, stop=True)
            for k in range(0, NP, SW):
                m = min(SW, NP - k)
                ins = pe.matmul(flat[:, k:k + m], wa[:, 0:1].to_broadcast([F, P]), fT[:, k:k + m], start=True, stop=True)
            ins.then_inc(mm, 1)
            pe.wait_ge(copied, 2)
            pe.wait_ge(low_made, 1)
            pe.sem_inc(sm.summed, 2)
            sm.loop(pe, lambda c, i: sm.weigh(pe, keep["ident"][:, :], c, i))
            pe.wait_ge(sm.summed, NC + 2)
            pe.wait_ge(joined, 1)
            for c in range(NC):
                ins = pe.transpose(flat[:, P * c:P * c + P], cat[:, c, :], keep["ident"][:, :])
            ins.then_inc(back, 1)
            pe.wait_ge(copied, 3)
            for c in range(NC):
                ins = pe.matmul(flat[:, F * c:F * c + F], catT[:, P * c:P * c + P], lin_w[:, :], start=True, stop=True)
            ins.then_inc(back, 1)

        @block.vector
        def _(dve):
            dve.memset(v[:, :, F:AUG], 1.0)
            dve.memset(col[:, NC:NC + 1], 0.0)
            dve.tensor_copy(cat[:, :, 0:F], keep["x"][:, :, :])
            dve.tensor_copy(v[:, :, 0:F], keep["x"][:, :, :]).then_inc(sm.ready, 1)
            dve.wait_ge(turned, 1)
            dve.tensor_copy(fT, flat[0:F, 0:NP]).then_inc(copied, 1)
            dve.wait_ge(mm, 1)
            dve.tensor_copy(col[:, 0:NC], pa[:, 7, 0:NC])
            dve.tensor_copy(src_all[:, :], flat[:, 0:NP]).then_inc(copied, 1)
            dve.wait_ge(low_made, 1)
            sm.vector_counters(dve)

            def peak(c, i, between=lambda b: None):
                xs = sm.xs[i % 4]

                def prepare(b):
                    lo, m = BLOCKS[b]
                    if b == 0:
                        dve.wait_ge(relued, c + 1)
                    dve.scalar_tensor_tensor(xs[:, lo:lo + m], xs[:, lo:lo + m], 1.0 - SLOPE, src_low[:, lo:lo + m],
                                             ALU.mult, ALU.add).then_inc(scored, 1)

                sm.vector_peak(dve, c, i, lambda b, lo, m: xs[:, lo:lo + m], scored, prepare, between)

            peak(0, 0)
            peak(1, 1)

            def body(c, i):
                copy_after = {1: [1], 3: [3], 5: [5]}
                if sm.has(c + 2):
                    peak(c + 2, i + 2, lambda b: sm.vector_odd(dve, c, copy_after.get(b, [])))
                else:
                    sm.vector_odd(dve, c)
                sm.vector_out(dve, c, i)

            sm.loop(dve, body)
            s = Steps(dve, dv)
            sm.vector_mean(dve, s, cat[:, :, F:P])
            dve.wait_ge(dv, s.n)
            dve.sem_inc(joined, 1)
            dve.wait_ge(back, 1)
            dve.tensor_copy(catT[:, :], flat[:, 0:NP]).then_inc(copied, 1)
            dve.wait_ge(back, 2)
            s.do(dve.tensor_tensor(res[:, :, :], flat[:, 0:NC * F].rearrange("p (c f) -> p c f", f=F),
                                   lin_b[:, :].rearrange("p (o f) -> p o f", o=1).to_broadcast([P, NC, F]), ALU.add))
            s.do(dve.scalar_tensor_tensor(res[:, :, :], res[:, :, :], 0.0, keep["x"][:, :, :], ALU.max, ALU.add))
            norm_vector(dve, s, w, 1, res[:, :, :], keep["x"][:, :, :])
            dve.wait_ge(dv, s.n)
            dve.sem_inc(normed, 1)

        @block.scalar
        def _(act):
            act.wait_ge(mm, 1)
            act.wait_ge(copied, 2)
            act.activation(src_low[:, :], flat[:, 0:N], ACT.Copy, scale=SLOPE).then_inc(low_made, 1)

            def relu(c, i, halves=(0, 1)):
                for h in halves:
                    lo, hi = HALVES[h]
                    ins = act.activation(sm.xs[i % 4][:, lo:hi], src_all[:, lo:hi], ACT.Relu,
                                         bias=col[:, ds(c, 1)] if type(c) is not int else col[:, c:c + 1])
                if 1 in halves:
                    ins.then_inc(relued, 1)

            for c in range(3):
                relu(c, c)
            sm.scalar_exp(act, 0, 0)

            def body(c, i):
                for k in range(4):
                    sm.scalar_even(act, c, [2 * k])
                    if k < 2:
                        if sm.has(c + 1):
                            sm.scalar_exp(act, c + 1, i + 1, [k])
                    elif sm.has(c + 3):
                        relu(c + 3, i + 3, [k - 2])

            sm.loop(act, body)
            norm_scalar(act, w, 1)


def program(nc, io, out):
    def scratch(name, shape, dt=F32):
        return nc.dram_tensor(name, shape, dt, kind="Internal").ap()

    dram = {
        "table_src": scratch("table_src", (NP, M)), "table_dst": scratch("table_dst", (NP, M)),
        "counts": scratch("counts", (COUNTS + 4 * P, 1)), "runs": scratch("runs", (EP, 2 * M)),
        "logs": scratch("logs", (NP, N)),
        "sheaf_src": scratch("sheaf_src", (NP, WS)),
        "spread": scratch("spread", (EP + NP, M)),
        "sums": scratch("sums", (EP, F)),
    }
    with ExitStack() as ctx:
        def sb(name, shape, dt=F32):
            return ctx.enter_context(nc.sbuf_tensor(name, shape, dt))

        keep = {n: sb(n, [P, NC]) for n in ("nid", "first", "last", "degree", "out_deg")}
        keep.update({n: sb(n, [P, T], I32) for n in ("src", "dst")})
        keep["last_idx"], keep["first_idx"] = sb("last_idx", [P, NC], I32), sb("first_idx", [P, NC], I32)
        keep["head_idx"] = sb("head_idx", [P, 1], I32)
        keep["ident"] = sb("ident", [P, P])
        keep["x"] = sb("x", [P, NC, F])
        with ExitStack() as ctx:
            keep["key"], keep["dump"], keep["earlier"] = sb("key", [P, T]), sb("dump", [P, 4]), sb("earlier", [P, 7 * P])
            setup_phase(nc, io, dram, keep)
            message_phase(nc, io, dram, keep)
        node_phase(nc, io, dram, keep)
        with ExitStack() as ctx:
            keep["h"] = sb("h", [P, NC, F])
            for l in range(4):
                conv_phase(nc, io, dram, keep, l)
        with ExitStack() as ctx:
            keep["src_tab"], keep["dst_tab"] = sb("src_tab", [P, NC, WS]), sb("dst_tab", [P, NC, M])
            keep["dis"] = sb("dis", [P, NC])
            keep["loops"] = sb("loops", [P, NC, F])
            sheaf_tables_phase(nc, io, dram, keep)
            sheaf_phase(nc, io, dram, keep)
            sheaf_node_phase(nc, io, dram, keep)
        attention_phase(nc, io, dram, keep, out)


SHAPE = (N, F)


def kernel(**inputs):
    import concourse.bacc as _bacc
    from concourse.bass_utils import run_bass_kernel_spmd as _run

    nc = _bacc.Bacc("TRN2", target_bir_lowering=False, num_devices=1)
    a = {k: np.ascontiguousarray(v) for k, v in inputs.items()}
    x, src, dst, attr = (a[k] for k in ("x", "src", "dst", "edge_attr_32"))
    node = np.full(EP, PAD_NODE, dst.dtype)
    node[:E] = dst
    of = np.full(EP, PAD_NODE, src.dtype)
    of[:E] = src
    feats = np.zeros((EP, M), attr.dtype)
    feats[:E] = attr
    arrays = {k: v for k, v in a.items() if k[0] == "L"}
    arrays["x"] = x
    arrays["xT"] = x.T
    arrays["src_pm"] = of.reshape(T, P).T
    arrays["dst_pm"] = node.reshape(T, P).T
    arrays["dst_tiles"] = node.reshape(T, P)
    arrays["dst_last"] = node.reshape(T, P)[:, P - 1]
    arrays["dst_heads"] = np.tile(node[::QE], P // 4)
    seq = np.full((4, QE + 1), -1, dst.dtype)
    seq[:, 1:] = node.reshape(4, QE)
    arrays["dst_seq"] = seq
    arrays["edge_T"] = feats.reshape(4, QE, M).transpose(0, 2, 1).reshape(4 * M, QE)
    arrays["mlp1_T"] = a["L2_gnn_mlp1_w"].T
    order = [0, 1, 3, 2, 4, 5]
    arrays["mlp2_T"] = a["L2_gnn_mlp2_w"][order].T
    arrays["mlp2_b"] = a["L2_gnn_mlp2_b"][order]
    arrays["lin_T"] = a["L3_gnn_lin_w"].T
    arrays = {k: np.ascontiguousarray(v) for k, v in arrays.items()}
    io = {k: nc.dram_tensor(f"in_{k}", v.shape, mybir.dt.from_np(v.dtype), kind="ExternalInput").ap()
          for k, v in arrays.items()}
    out = nc.dram_tensor("out", SHAPE, F32, kind="ExternalOutput").ap()
    program(nc, io, out)
    r = _run(nc, [{f"in_{k}": v for k, v in arrays.items()}], core_ids=[0])
    return r.results[0]["out"]
```
